# Optimizing a Trainium2 kernel written in Bass

```python
import numpy as np
import jax
import jax.numpy as jnp

def _softmax(x, axis=-1):
    return jax.nn.softmax(x, axis=axis)

def _gelu(x):
    return jax.nn.gelu(x, approximate=True)

def _silu(x):
    return jax.nn.silu(x)

def _sigmoid(x):
    return jax.nn.sigmoid(x)

def _layernorm(x, axis=-1, eps=1e-05):
    m = jnp.mean(x, axis=axis, keepdims=True)
    v = jnp.var(x, axis=axis, keepdims=True)
    return (x - m) / jnp.sqrt(v + eps)

def _scatter_add(tgt, idx, src, axis=0):
    return tgt.at[idx].add(src)

def _segment_sum(src, seg, n):
    return jax.ops.segment_sum(src, seg, n)
kernel_name = 'mk_lm_tower_d1_tok_ids512_r4_0dac98'

def setup_inputs(seed: int=0):
    np.random.seed(seed)
    _w = jnp.asarray

    def _rec_inputs():
        import jax
        import jax.numpy as jnp
        _rk = jax.random.key(seed)
        x = jax.random.randint(jax.random.fold_in(_rk, 1), (16, 512), 0, 16, jnp.int32)
        return x
    x = _rec_inputs()

    def _L0_tok_setup():
        import jax, jax.numpy as jnp
        import numpy as np
        VOCAB = 16
        D_MODEL = 128
        D_EMB = int(D_MODEL * 0.7)
        D_STFT = D_MODEL - D_EMB
        N_FFT = 64
        HOP = 64
        N_FREQ = N_FFT // 2 + 1
        B, L = (4, 2048)

        def _stft_mag(signal):
            pad = N_FFT // 2
            padded = jnp.pad(signal, ((0, 0), (pad, pad)), mode='reflect')
            n_frames = signal.shape[1] // HOP + 1
            idx = jnp.arange(n_frames)[:, None] * HOP + jnp.arange(N_FFT)[None, :]
            window = 0.5 - 0.5 * jnp.cos(2.0 * jnp.pi * jnp.arange(N_FFT) / N_FFT)
            frames = padded[:, idx] * window.astype(signal.dtype)
            return jnp.abs(jnp.fft.rfft(frames, axis=-1))
        key = jax.random.key(seed)
        k1, k2, k3, k4 = jax.random.split(key, 4)
        input_ids = jax.random.randint(k1, (B, L), 0, VOCAB)
        emb_table = jax.random.normal(k2, (VOCAB, D_EMB), dtype=jnp.float32) * 0.02
        proj_w = jax.random.normal(k3, (VOCAB * N_FREQ, D_STFT), dtype=jnp.float32) * 0.02
        proj_b = jnp.zeros((D_STFT,), dtype=jnp.float32)
        return {'input_ids': input_ids, 'emb_table': emb_table, 'proj_w': proj_w, 'proj_b': proj_b}
    _L0_tok_all = _L0_tok_setup()
    _L0_tok_in = {k: v for k, v in _L0_tok_all.items() if k in ('emb_table', 'proj_w', 'proj_b')}
    del _L0_tok_all

    def _L0_attn_setup():
        import jax, jax.numpy as jnp
        import numpy as np
        HEADS = 8
        DIM_HEAD = 64
        EPS = 1e-05

        def layer_norm(x, gamma):
            mu = jnp.mean(x, axis=-1, keepdims=True)
            var = jnp.var(x, axis=-1, keepdims=True)
            return (x - mu) * jax.lax.rsqrt(var + EPS) * gamma
        key = jax.random.key(seed)
        k1, k2, k3 = jax.random.split(key, 3)
        b, n, dim = (4, 4096, 128)
        hidden = HEADS * DIM_HEAD
        x = jax.random.normal(k1, (b, n, dim), dtype=jnp.float32)
        norm_gamma = jnp.ones((dim,), dtype=jnp.float32)
        w_qkv = jax.random.normal(k2, (hidden * 3, dim), dtype=jnp.float32) * dim ** (-0.5)
        w_out = jax.random.normal(k3, (dim, hidden), dtype=jnp.float32) * hidden ** (-0.5)
        out_gamma = jnp.ones((dim,), dtype=jnp.float32)
        return {'x': x, 'norm_gamma': norm_gamma, 'w_qkv': w_qkv, 'w_out': w_out, 'out_gamma': out_gamma}
    _L0_attn_all = _L0_attn_setup()
    _L0_attn_in = {k: v for k, v in _L0_attn_all.items() if k in ('norm_gamma', 'w_qkv', 'w_out', 'out_gamma')}
    del _L0_attn_all

    def _L0_ffn_setup():
        import jax, jax.numpy as jnp
        import numpy as np
        NUM_EXPERTS = 32
        GROUP_SIZE = 4
        NUM_GROUPS = NUM_EXPERTS // GROUP_SIZE
        C_CAP = 1.0
        key = jax.random.key(seed)
        ks = jax.random.split(key, 5)
        B, S, H = (16, 512, 128)
        D_FF = int(H * 4 * (2.0 / 3.0))
        x = jax.random.normal(ks[0], (B, S, H), dtype=jnp.float32)
        W_router = jax.random.normal(ks[1], (H, NUM_EXPERTS), dtype=jnp.float32) * (1.0 / np.sqrt(H))
        b_router = jnp.zeros((NUM_EXPERTS,), dtype=jnp.float32)
        W_up = jax.random.normal(ks[2], (NUM_GROUPS, H, D_FF), dtype=jnp.float32) * (1.0 / np.sqrt(H))
        b_up = jnp.zeros((NUM_GROUPS, D_FF), dtype=jnp.float32)
        W_down = jax.random.normal(ks[3], (NUM_EXPERTS, D_FF, H), dtype=jnp.float32) * (1.0 / np.sqrt(D_FF))
        b_down = jnp.zeros((NUM_EXPERTS, H), dtype=jnp.float32)
        return {'x': x, 'W_router': W_router, 'b_router': b_router, 'W_up': W_up, 'b_up': b_up, 'W_down': W_down, 'b_down': b_down}
    _L0_ffn_all = _L0_ffn_setup()
    _L0_ffn_in = {k: v for k, v in _L0_ffn_all.items() if k in ('W_router', 'b_router', 'W_up', 'b_up', 'W_down', 'b_down')}
    del _L0_ffn_all
    return {'x': x, 'L0_tok_emb_table': _L0_tok_in['emb_table'], 'L0_tok_proj_w': _L0_tok_in['proj_w'], 'L0_tok_proj_b': _L0_tok_in['proj_b'], 'L0_attn_norm_gamma': _L0_attn_in['norm_gamma'], 'L0_attn_w_qkv': _L0_attn_in['w_qkv'], 'L0_attn_w_out': _L0_attn_in['w_out'], 'L0_attn_out_gamma': _L0_attn_in['out_gamma'], 'L0_ffn_W_router': _L0_ffn_in['W_router'], 'L0_ffn_b_router': _L0_ffn_in['b_router'], 'L0_ffn_W_up': _L0_ffn_in['W_up'], 'L0_ffn_b_up': _L0_ffn_in['b_up'], 'L0_ffn_W_down': _L0_ffn_in['W_down'], 'L0_ffn_b_down': _L0_ffn_in['b_down']}

def reference(x, L0_tok_emb_table, L0_tok_proj_w, L0_tok_proj_b, L0_attn_norm_gamma, L0_attn_w_qkv, L0_attn_w_out, L0_attn_out_gamma, L0_ffn_W_router, L0_ffn_b_router, L0_ffn_W_up, L0_ffn_b_up, L0_ffn_W_down, L0_ffn_b_down):
    import jax
    import jax.numpy as jnp

    def _L0_tok_ref(input_ids, emb_table, proj_w, proj_b):
        import jax, jax.numpy as jnp
        import numpy as np
        VOCAB = 16
        D_MODEL = 128
        D_EMB = int(D_MODEL * 0.7)
        D_STFT = D_MODEL - D_EMB
        N_FFT = 64
        HOP = 64
        N_FREQ = N_FFT // 2 + 1
        B, L = (4, 2048)

        def _stft_mag(signal):
            pad = N_FFT // 2
            padded = jnp.pad(signal, ((0, 0), (pad, pad)), mode='reflect')
            n_frames = signal.shape[1] // HOP + 1
            idx = jnp.arange(n_frames)[:, None] * HOP + jnp.arange(N_FFT)[None, :]
            window = 0.5 - 0.5 * jnp.cos(2.0 * jnp.pi * jnp.arange(N_FFT) / N_FFT)
            frames = padded[:, idx] * window.astype(signal.dtype)
            return jnp.abs(jnp.fft.rfft(frames, axis=-1))
        b, seq_len = input_ids.shape
        word_embeds = emb_table[input_ids]
        onehot = jax.nn.one_hot(input_ids, VOCAB, dtype=jnp.float32)
        signal = onehot.transpose(0, 2, 1).reshape(b * VOCAB, seq_len)
        spec = _stft_mag(signal)
        n_frames = spec.shape[1]
        stft_mag = spec.reshape(b, VOCAB, n_frames, N_FREQ).transpose(0, 1, 3, 2)
        stft_to_up = stft_mag.transpose(0, 2, 1, 3).reshape(b, N_FREQ * VOCAB, n_frames)
        up_idx = jnp.arange(seq_len) * n_frames // seq_len
        stft_up = stft_to_up[:, :, up_idx]
        feats = stft_up.transpose(0, 2, 1)
        stft_enc = jnp.einsum('bli,io->blo', feats, proj_w) + proj_b
        return jnp.concatenate([word_embeds, stft_enc], axis=-1)

    def _L0_attn_ref(x, norm_gamma, w_qkv, w_out, out_gamma):
        import jax, jax.numpy as jnp
        import numpy as np
        HEADS = 8
        DIM_HEAD = 64
        EPS = 1e-05

        def layer_norm(x, gamma):
            mu = jnp.mean(x, axis=-1, keepdims=True)
            var = jnp.var(x, axis=-1, keepdims=True)
            return (x - mu) * jax.lax.rsqrt(var + EPS) * gamma
        b, n, dim = x.shape
        h, d = (HEADS, DIM_HEAD)
        scale = d ** (-0.5)
        x = layer_norm(x, norm_gamma)
        qkv = jnp.einsum('bnc,fc->bnf', x, w_qkv)
        q, k, v = jnp.split(qkv, 3, axis=-1)
        to_bhnd = lambda t: t.reshape(b, n, h, d).transpose(0, 2, 1, 3)
        q, k, v = (to_bhnd(q), to_bhnd(k), to_bhnd(v))
        q = jax.nn.softmax(q, axis=-1) * scale
        k = jax.nn.softmax(k, axis=-2)
        context = jnp.einsum('bhnd,bhne->bhde', k, v)
        out = jnp.einsum('bhde,bhnd->bhne', context, q)
        out = out.transpose(0, 2, 1, 3).reshape(b, n, h * d)
        out = jnp.einsum('bnf,cf->bnc', out, w_out)
        return layer_norm(out, out_gamma)

    def _L0_ffn_ref(x, W_router, b_router, W_up, b_up, W_down, b_down):
        import jax, jax.numpy as jnp
        import numpy as np
        NUM_EXPERTS = 32
        GROUP_SIZE = 4
        NUM_GROUPS = NUM_EXPERTS // GROUP_SIZE
        C_CAP = 1.0
        B, S, H = x.shape
        bs = B * S
        E = NUM_EXPERTS
        k = min(int(bs * C_CAP) // E, bs)
        xf = x.reshape(bs, H)
        h = xf @ W_router + b_router
        Sm = jax.nn.softmax(h, axis=-1)
        G_ek, idx_ek = jax.lax.top_k(Sm.T, k)
        tokens = xf[idx_ek]
        D_FF = W_up.shape[-1]
        tok_g = tokens.reshape(NUM_GROUPS, GROUP_SIZE, k, H)
        up = jnp.einsum('gjkh,ghf->gjkf', tok_g, W_up) + b_up[:, None, None, :]
        act = jax.nn.silu(up).reshape(E, k, D_FF)
        Eout = jnp.einsum('ekf,efh->ekh', act, W_down) + b_down[:, None, :]
        weighted = G_ek[..., None] * Eout
        y = jnp.zeros((bs, H), dtype=x.dtype).at[idx_ek.reshape(-1)].add(weighted.reshape(-1, H))
        return y.reshape(B, S, H)
    h = _L0_tok_ref(x, L0_tok_emb_table, L0_tok_proj_w, L0_tok_proj_b)
    h = h + _L0_attn_ref(_layernorm(h, axis=-1), L0_attn_norm_gamma, L0_attn_w_qkv, L0_attn_w_out, L0_attn_out_gamma)
    h = h + _L0_ffn_ref(_layernorm(h, axis=-1), L0_ffn_W_router, L0_ffn_b_router, L0_ffn_W_up, L0_ffn_b_up, L0_ffn_W_down, L0_ffn_b_down)
    return h

_drawn_inputs = setup_inputs


def setup_inputs(seed=0):
    import zlib

    import numpy as np

    out = dict(_drawn_inputs(seed))
    spreads = {'L0_tok_proj_b': (0.0, 0.1),
     'L0_attn_norm_gamma': (1.0, 0.2),
     'L0_attn_out_gamma': (1.0, 0.2),
     'L0_ffn_b_router': (0.0, 0.8),
     'L0_ffn_b_up': (0.0, 0.8),
     'L0_ffn_b_down': (0.0, 0.8)}
    factors = {}
    for name, (base, spread) in spreads.items():
        noise = np.random.default_rng([zlib.crc32(name.encode()), seed]).standard_normal(out[name].shape)
        drawn = base * np.exp(spread * noise) if base else spread * noise
        out[name] = jnp.asarray(drawn.astype(out[name].dtype))
    for name, factor in factors.items():
        out[name] = (out[name] * factor).astype(out[name].dtype)
    return out
```

```python
from contextlib import ExitStack

import concourse.bass as bass
from concourse import mybir
import numpy as np

ALU = mybir.AluOpType
ACT = mybir.ActivationFunctionType
AX = mybir.AxisListType
F32 = mybir.dt.float32
BF16 = mybir.dt.bfloat16
I32 = mybir.dt.int32
U32 = mybir.dt.uint32

P = 128
B, L, V = 16, 512, 16
NFFT, HOP = 64, 64
NT = L // HOP + 1
NF = NFFT // 2 + 1
D, DE = 128, 89
DS = D - DE
H, DH = 8, 64
HD = H * DH
E, GS = 32, 4
NG = E // GS
FF = 341
FT = (FF + P - 1) // P
FL = FF - (FT - 1) * P
CAP = B * L // E
EPS = 1e-5
TM = NT - 1
NB = B + B // 8
NTT = B * L // P
CW = 3 * HD + D
QC, KC, VC, HC = 0, HD, 2 * HD, 3 * HD
BITS = 30
TW = D + E
LAST0 = -(-L * TM // NT)


def _split3(a):
    bf = mybir.dt.np(BF16)
    hi = a.astype(bf)
    r = a - hi.astype(np.float64)
    mid = r.astype(bf)
    lo = (r - mid.astype(np.float64)).astype(bf)
    return hi.astype(np.float64), mid.astype(np.float64), lo.astype(np.float64)


def constants():
    p = np.arange(P)
    n = np.arange(NFFT)
    f = np.arange(NF)
    win = 0.5 - 0.5 * np.cos(2 * np.pi * n / NFFT)
    ang = 2 * np.pi * np.outer(n, f) / NFFT
    dft = np.concatenate([win[:, None] * np.cos(ang), -win[:, None] * np.sin(ang)], 1)
    hi, mid, lo = _split3(dft)
    eye = np.eye(P)
    cf = {
        "ident": eye,
        "frame16": np.tile(16.0 * (np.arange(L) * NT // L), (B, 1)),
        "sameexp": (p[:, None] % E == p[None, :] % E) * 1.0,
        "eyeexp": (p[:, None] == np.arange(E)[None, :]) * 1.0,
        "pidx": p[:, None] * 1.0,
        "lastid": (P + p[:, None] % V) * 1.0,
        "lastb": (np.arange(B)[None, :] % 8 == p[:, None] // V) * 1.0,
        "parity": np.stack([p // V % 2 == 0, p // V % 2 == 1], 1) * 1.0,
        "parrow": np.tile(np.stack([p // V % 2 == 0, p // V % 2 == 1], 0).reshape(1, 2 * P), (P, 1)) * 1.0,
        "slot": np.stack([p, p + P], 1) * 1.0,
        "ids": np.tile(np.arange(V), (P, 1)) * 1.0,
        "tau16": np.tile(16.0 * np.arange(NTT), (P, 1)),
    }
    cb = {
        "dftab": np.concatenate([hi, mid], 0),
        "dftc": lo,
        "sela": np.tile(np.arange(V)[:, None] == p[None, :] % V, (3, 1)) * 1.0,
        "selb": np.tile(np.arange(TM)[:, None] == p[None, :] // V, (3, 1)) * 1.0,
        "identb": eye,
        "before": (p[:, None] < p[None, :]) * 1.0,
        "notbefore": -1.0 * (p[:, None] >= p[None, :]),
        "onesb": np.ones((P, P)),
        "diff": eye * 1.0 - (p[:, None] == p[None, :] - 1),
        "shift": (p[:, None] == p[None, :] - 1) * 1.0,
        "headsel": (np.arange(HD)[None, :] // DH == np.arange(H)[:, None]) * 1.0,
        "slots": np.tile(np.arange(CAP), (P, 1)) * 1.0,
        "carry": np.tile(np.arange(NTT) > 0, (P, E)) * 1.0,
        "rowb": np.stack([np.tile(np.arange(B) == i, (P, 1)) if i < B else
                          np.arange(B)[None, :] == 8 * (i - B) + p[:, None] // V for i in range(NB)], 1) * 1.0,
    }
    return cf, cb


def _layout(tables):
    at, where = 0, {}
    for name, a in tables.items():
        w = int(np.prod(a.shape[1:]))
        where[name] = (a.shape[0], at, w)
        at += w
    return where, at


def _pack(tables, dtype):
    where, width = _layout(tables)
    out = np.zeros((P, width), dtype)
    for name, a in tables.items():
        r, at, w = where[name]
        out[:r, at:at + w] = a.reshape(r, w).astype(dtype)
    return out



def program(nc, A, out):
    cfw, cfn = _layout(constants()[0])
    cbw, cbn = _layout(constants()[1])
    with ExitStack() as ctx:
        def sb(name, shape, dt=F32):
            return ctx.enter_context(nc.sbuf_tensor(name, shape, dt))

        def sem(name):
            return ctx.enter_context(nc.semaphore(name))

        cf = sb("cf", [P, cfn])
        cb = sb("cb", [P, cbn], BF16)

        def cfv(name):
            r, at, w = cfw[name]
            return cf[0:r, at:at + w]

        def cbv(name):
            r, at, w = cbw[name]
            return cb[0:r, at:at + w]

        ident, identb = cfv("ident"), cbv("identb")
        sela, selb = cbv("sela"), cbv("selb")
        xfrm = sb("xfrm", [P, B * NT], I32)
        xtok = sb("xtok", [P, NTT], I32)
        xkey = sb("xkey", [B, L], BF16)
        gcol = sb("gcol", [P, 1])
        ogam = sb("ogam", [P, D])
        wrt = sb("wrt", [P, E])
        brt = sb("brt", [P, E])
        wup = sb("wup", [P, NG, FF])
        bup = sb("bup", [P, FT, NG])
        wo = sb("wo", [P, 4, D])
        oh = sb("oh", [P, B, L], BF16)
        ohl = sb("ohl", [P, B, P], BF16)
        h0 = sb("h0", [P, NB, D])
        ra = sb("ra", [3 * V, CW], BF16)

        arA = sb("arA", [P, NB * CW // 2])
        tabx = arA[:, 0:CW]
        tabxq = arA[0:2 * V, CW:2 * CW]
        tabp = arA[:, 2 * CW:2 * CW + 3 * CW // 2].bitcast(BF16).rearrange("p (s c) -> p s c", s=3)
        tabq = arA[0:2 * V, 4 * CW:4 * CW + 3 * CW // 2].bitcast(BF16).rearrange("p (s c) -> p s c", s=3)
        rb = arA[0:3 * TM, :].bitcast(BF16).rearrange("p (i c) -> p i c", i=NB)
        WD = E * FT * D
        wdn = arA[:, 0:WD].rearrange("p (e k h) -> p e k h", e=E, k=FT)
        h1 = arA[:, WD:WD + NB * D].rearrange("p (i c) -> p i c", i=NB)

        BW = B * HD + 2 * 2 * HD
        arB = sb("arB", [P, BW])

        def at(arena, start, words, rows=P, dt=F32):
            v = arena[0:rows, start:start + words]
            return v if dt == F32 else v.bitcast(dt)

        ohn = at(arB, 0, 1152, P, BF16).rearrange("p (v k) -> p v k", v=V)
        ohn2 = at(arB, 0, 1152, P, BF16)
        sq = at(arB, 1152, 4608, NF).rearrange("p (r c) -> p r c", r=2)
        mag = at(arB, 5760, 2304, NF)
        wqkv = at(arB, 8064, 3 * HD)
        projw = at(arB, 9600, V * DS, NF)
        qt = at(arB, 0, B * HD).rearrange("p (i j r) -> p i j r", i=B, j=4)
        qtl = at(arB, B * HD, 4 * HD).rearrange("p (g o j r) -> p g o j r", g=2, o=2, j=4)
        xn = at(arB, 0, NB * D).rearrange("p (i c) -> p i c", i=NB)
        xnT = at(arB, 2304, NB * P)
        SW = E * NTT // 2
        eqT = at(arB, 0, SW, P, BF16)
        gtT = at(arB, SW, SW, P, BF16)
        eqS = at(arB, 2 * SW, SW, P, BF16)
        pin = at(arB, 3 * SW, SW, P, BF16)
        PDW = E * (NTT + 2) // 2
        pd = at(arB, 4 * SW, PDW, P, BF16).rearrange("p (e t) -> p e t", e=E)
        step = at(arB, 4 * SW + PDW, E * CAP // 2, P, BF16).rearrange("p (e s) -> p e s", e=E)

        arC = sb("arC", [P, 8192])
        sbc = at(arC, 0, NB * P).rearrange("p (i r) -> p i r", i=NB)
        prod = at(arC, 2304, 512, P, BF16).rearrange("p (s j r) -> p s j r", s=2, j=4)
        eq_ = at(arC, 3072, 3 * HD).rearrange("p (s c) -> p s c", s=3)
        qn = at(arC, 4608, 2 * HD).rearrange("p (s c) -> p s c", s=2)
        ek = at(arC, 0, 2 * HD).rearrange("p (s c) -> p s c", s=2)
        ekl = at(arC, 1024, 2 * HD).rearrange("p (s c) -> p s c", s=2)
        vv = at(arC, 2048, 2 * HD).rearrange("p (s c) -> p s c", s=2)
        vl = at(arC, 3072, 4 * HD).rearrange("p (g o c) -> p g o c", g=2, o=2)
        ct = at(arC, 5120, 2 * HD).rearrange("p (s j c) -> p s j c", s=2, j=4)
        mb = at(arC, 6144, 2 * HD).rearrange("p (s j c) -> p s j c", s=2, j=4)
        pbis = at(arC, 0, 640)
        wbis = at(arC, 640, 640)
        junk = at(arC, 1280, 640)
        h1p = at(arC, 1920, 3 * NB * D // 2, P, BF16).rearrange("p (s i c) -> p s i c", s=3, i=NB)
        h1r = at(arB, 4608, NB * D).rearrange("p (i c) -> p i c", i=NB)
        hout = at(arC, 5632, 5 * 512).rearrange("p (s w c) -> p s w c", s=5, w=4)
        xg = at(arC, 0, 4 * 2 * TW).rearrange("p (s h c) -> p s h c", s=4, h=2)
        xgT = at(arC, 1280, 2 * CAP).rearrange("p (s c) -> p s c", s=2)
        actT = at(arC, 1792, 2 * FT * CAP).rearrange("p (s k c) -> p s k c", s=2, k=FT)
        eo = at(arC, 3328, 4 * 2 * D).rearrange("p (s h c) -> p s h c", s=4, h=2)
        lm = at(arC, 4352, 256).rearrange("p (b h c) -> p b h c", b=2, h=2)
        lp = at(arC, 4608, 256).rearrange("p (b h c) -> p b h c", b=2, h=2)

        _small = {}

        def tiny(name, words, rows=P, dt=F32):
            a = sb(name, [rows, words], dt)
            return a[:, :]

        projb = at(arC, 6816, DS)
        xseq = at(arC, 5632, L, B, I32)
        fp = at(arC, 6144, D)
        fpc = at(arC, 6272, D)
        fq = at(arC, 6400, D, 2 * V)
        fqc = at(arC, 6528, D, 2 * V)
        fm = tiny("fm", 4)
        ft = at(arC, 6656, P + 2 * V)
        stats = tiny("stats", NB * 6).rearrange("p (i c) -> p i c", i=NB)
        mv = tiny("mv", NB * 2).rearrange("p (i c) -> p i c", i=NB)
        cnt = tiny("cnt", 20)
        lnv = tiny("lnv", NB)
        invs = tiny("invs", NB)
        s1 = tiny("s1", NB)
        sT = tiny("sT", P, NB)
        absent = tiny("absent", NB, P, BF16)
        maskT = tiny("maskT", P, NB, BF16)
        mx = tiny("mx", 4 * B).rearrange("p (j b) -> p j b", j=4)
        mxl = tiny("mxl", 4 * B).rearrange("p (j b) -> p j b", j=4)
        negm = tiny("negm", 4 * 3 * B, P, BF16).rearrange("p (j s b) -> p j s b", j=4, s=3)
        nm = tiny("nm", HD, 3 * B, BF16)
        ivr = tiny("ivr", 2 * NB).rearrange("p (s i) -> p s i", s=2)
        ivp = tiny("ivp", 3 * NB, P, BF16).rearrange("p (s i) -> p s i", s=3)
        wsh = at(arC, 6912, NB * 3 * B // 2, P, BF16).rearrange("p (i s b) -> p i s b", i=NB, s=3)
        lsh = tiny("lsh", NB * P, 3 * B, BF16).rearrange("p (i r) -> p i r", i=NB)
        mq = tiny("mq", 3 * H, P, BF16).rearrange("p (s h) -> p s h", s=3)
        mqT = tiny("mqT", 2 * P, H, BF16).rearrange("p (s r) -> p s r", s=2)
        zq = tiny("zq", 2 * H).rearrange("p (s h) -> p s h", s=2)
        rq = tiny("rq", 2 * H).rearrange("p (s h) -> p s h", s=2)
        sc = tiny("sc", NB)
        scl = tiny("scl", 4).rearrange("p (g o) -> p g o", g=2)
        cntl = tiny("cntl", 4).rearrange("p (g o) -> p g o", g=2)
        rz = tiny("rz", 4 * B).rearrange("p (b j) -> p b j", b=B)
        rstd = tiny("rstd", NB)
        nbias = tiny("nbias", NB)
        pr = tiny("pr", 20 * E).rearrange("p (i e) -> p i e", i=20)
        px = at(arC, 5632, 20 * E).rearrange("p (i e) -> p i e", i=20)
        pmx = tiny("pmx", NB)
        psm = tiny("psm", NB)
        cand = tiny("cand", 1, P, I32)
        delta = tiny("delta", 1, P, I32)
        bits = tiny("bits", BITS, P, I32)
        part = tiny("part", 1)
        need = tiny("need", 1)
        dtn = tiny("dtn", 2 * E, E)
        onesf = tiny("onesf", P, E)
        tn = tiny("tn", 2 * E)
        ge = at(arC, 1280, NB * E, P, BF16).rearrange("p (i c) -> p i c", i=NB)
        cq = tiny("cq", E, P, BF16)
        bx = tiny("bx", E)
        vtok = tiny("vtok", NTT)
        g0 = tiny("g0", NTT + 2, P, BF16)
        gd = tiny("gd", NTT + 2, P, BF16)
        sr = tiny("sr", 4)
        sv = tiny("sv", 4)
        vi = tiny("vi", 4, P, I32)
        offi = tiny("offi", 4, P, I32)
        idi = tiny("idi", 4, P, I32)
        seg = tiny("seg", 4, P, I32)
        rowi = tiny("rowi", 2 * E, P, U32)
        toki = tiny("toki", 2 * E, P, U32)

        ps = ctx.enter_context(nc.psum_tensor("ps", [P, 8, 512], F32))
        dtab = nc.dram_tensor("factors", (P + 2 * V, 3, CW), BF16, kind="Internal").ap()
        table = nc.dram_tensor("rows", (B * NT * V, TW), F32, kind="Internal").ap()

        in_x, in_c, in_p, in_w, in_r = (sem(n) for n in ("in_x", "in_c", "in_p", "in_w", "in_r"))
        s_ohn, s_stft, s_sq, s_msq, s_mag, s_enc, s_fc, s_tr, s_ft, s_proj = (
            sem(n) for n in ("s_ohn", "s_stft", "s_sq", "s_msq", "s_mag", "s_enc", "s_fc", "s_tr", "s_ft", "s_proj"))
        s_hi, s_r, s_mid, s_lo, s_dtab, s_rb = (sem(n) for n in ("s_hi", "s_r", "s_mid", "s_lo", "s_dtab", "s_rb"))
        s_xkey, s_kb, s_oh = (sem(n) for n in ("s_xkey", "s_kb", "s_oh"))
        s_h0m, s_h0, s_var, s_invs, s_s1, s_sTm, s_sT, s_bcm, s_bc = (
            sem(n) for n in ("s_h0m", "s_h0", "s_var", "s_invs", "s_s1", "s_sTm", "s_sT", "s_bcm", "s_bc"))
        s_kt, s_ktu, s_negm, s_shm, s_sh = (sem(n) for n in ("s_kt", "s_ktu", "s_negm", "s_shm", "s_sh"))
        q_x, q_mx, q_mt, q_mc, q_sh, q_e, q_r, q_n, q_t, q_c, q_cl = (
            sem(n) for n in ("q_x", "q_mx", "q_mt", "q_mc", "q_sh", "q_e", "q_r", "q_n", "q_t", "q_c", "q_cl"))
        k_k, k_v, k_e, k_vc, k_cx, k_ca, k_cd, k_rz, k_m, k_mc, k_o, k_oc, k_zero = (
            sem(n) for n in ("k_k", "k_v", "k_e", "k_vc", "k_cx", "k_ca", "k_cd", "k_rz", "k_m", "k_mc", "k_o", "k_oc",
                             "k_zero"))
        l_v, l_s, l_n, l_h, l_v2, l_s2, l_n2, l_x = (
            sem(n) for n in ("l_v", "l_s", "l_n", "l_h", "l_v2", "l_s2", "l_n2", "l_x"))
        r_t, r_c, r_l, r_sub, r_exp, r_p, r_bt, r_b, r_tab, r_wd = (
            sem(n) for n in ("r_t", "r_c", "r_l", "r_sub", "r_exp", "r_p", "r_bt", "r_b", "r_tab", "r_wd"))
        b_part, b_tot, b_init = (sem(n) for n in ("b_part", "b_tot", "b_init"))
        x_p, x_p2, x_m, x_c = sem("x_p"), sem("x_p2"), sem("x_m"), sem("x_c")
        x_d = [sem(f"x_d{i}") for i in range(5)]
        t_d, t_m, t_ge, t_x, t_eq, t_gt, t_s, t_rk, t_sel, t_pin, t_bx, t_bc, t_df, t_pd, t_st, t_g = (
            sem(n) for n in ("t_d", "t_m", "t_ge", "t_x", "t_eq", "t_gt", "t_s", "t_rk", "t_sel", "t_pin", "t_bx",
                             "t_bc", "t_df", "t_pd", "t_st", "t_g"))
        m_sl, m_ls, m_t, m_tc, m_up, m_si, m_dn, m_eo, m_one = (
            sem(n) for n in ("m_sl", "m_ls", "m_t", "m_tc", "m_up", "m_si", "m_dn", "m_eo", "m_one"))
        g_x = [sem(f"g_x{i}") for i in range(4)]
        g_s = [sem(f"g_s{i}") for i in range(2)]
        s_dve, s_act, s_pool = sem("s_dve"), sem("s_act"), sem("s_pool")

        CH = [(c * 512, min(512, 2304 - c * 512)) for c in range(5)]
        TILES4 = [(4 * k, min(4, NB - 4 * k)) for k in range(5)]
        block = ctx.enter_context(nc.Block())

        @block.sync
        def _(sp):
            sp.dma_start(xfrm[:, :], A["x_frames"]).then_inc(in_x, 16)
            sp.dma_start(cb[:, :], A["const_bf16"]).then_inc(in_x, 16)
            sp.dma_start(cf[:, :], A["const_f32"]).then_inc(in_c, 16)
            sp.dma_start(xseq, A["x_seq"]).then_inc(in_c, 16)
            sp.dma_start(projw, A["proj_w"]).then_inc(in_p, 16)
            sp.dma_start(projb, A["proj_b"].partition_broadcast(P)).then_inc(in_p, 16)
            sp.wait_ge(k_zero, 1)
            sp.dma_start(fq[V:2 * V, 0:DE], A["emb"]).then_inc(in_p, 16)
            sp.dma_start(wqkv, A["w_qkv_t"]).then_inc(in_w, 16)
            sp.dma_start(gcol[:, :], A["norm_gamma"]).then_inc(in_w, 16)
            sp.dma_start(xtok[:, :], A["x_tokens"]).then_inc(in_r, 16)
            sp.dma_start(wo[:, :, :], A["w_out_t"].rearrange("(j p) c -> p j c", p=P)).then_inc(in_r, 16)
            sp.dma_start(ogam[:, :], A["out_gamma"].partition_broadcast(P)).then_inc(in_r, 16)
            sp.dma_start(wrt[:, :], A["w_router"]).then_inc(in_r, 16)
            sp.dma_start(brt[:, :], A["b_router"].partition_broadcast(P)).then_inc(in_r, 16)
            sp.dma_start(wup[:, :, :], A["w_up"].rearrange("g h f -> h g f")).then_inc(in_r, 16)
            for k in range(FT):
                n = min(P, FF - k * P)
                sp.dma_start(bup[0:n, k, :], A["b_up_t"][k * P:k * P + n, :]).then_inc(in_r, 16)
            sp.wait_ge(s_lo, 8)
            sp.dma_start(dtab[0:P], tabp).then_inc(s_dtab, 16)
            sp.dma_start(dtab[P:P + 2 * V], tabq).then_inc(s_dtab, 16)
            sp.wait_ge(s_dtab, 32)
            for part_ in range(3):
                sp.dma_start(rb[part_ * TM:(part_ + 1) * TM, 0:B, :],
                             dtab[0:P, part_, :].rearrange("(b t) c -> t b c", t=TM)).then_inc(s_rb, 16)
                sp.dma_start(rb[part_ * TM:(part_ + 1) * TM, B:NB, :],
                             dtab[P:P + B, part_, :].rearrange("(g t) c -> t g c", t=TM)).then_inc(s_rb, 16)
                sp.dma_start(ra[part_ * V:(part_ + 1) * V, :],
                             dtab[P + V:P + 2 * V, part_, :]).then_inc(s_rb, 16)
            sp.wait_ge(k_v, NB)
            for k in range(FT):
                n = min(P, FF - k * P)
                sp.dma_start(wdn[0:n, :, k, :], A["w_down"][:, k * P:k * P + n, :].rearrange("e f h -> f e h"))\
                  .then_inc(r_wd, 16)
            sp.dma_start(wdn[FL:FL + 1, :, FT - 1, :], A["b_down"].rearrange("(a e) h -> a e h", a=1))\
              .then_inc(r_wd, 16)
            sp.wait_ge(r_p, 1)
            rows = table.rearrange("(b r) c -> b r c", b=B)
            for col, src in ((slice(0, D), xn), (slice(D, TW), pr)):
                sp.dma_start(rows[:, 0:P, col].rearrange("b r c -> r b c"), src[:, 0:B, :]).then_inc(r_tab, 16)
                for g in range(2):
                    sp.dma_start(rows[8 * g:8 * g + 8, P:P + V, col], src[:, B + g, :]).then_inc(r_tab, 16)
            for b in range(B):
                sp.wait_ge(x_c, b + 1)
                sp.dma_start(out[b * L:(b + 1) * L, :].rearrange("(w q) c -> q w c", q=P), hout[:, b % 5])\
                  .then_inc(x_d[b % 5], 16)

        @block.gpsimd
        def _(pool):
            nc.gpsimd.memset(fq, 0.0).then_inc(k_zero, 1)
            nc.gpsimd.memset(fp, 0.0).then_inc(k_zero, 1)
            nc.gpsimd.memset(ohl[:, :, 0:LAST0 - 3 * P], 0.0).then_inc(k_zero, 1)
            nc.gpsimd.memset(cnt[:, NB:20], 0.0).then_inc(b_init, 1)
            nc.gpsimd.memset(pr[:, NB:20, :], 0.0).then_inc(b_init, 1)
            for k in range(BITS):
                nc.gpsimd.memset(bits[:, k:k + 1], 1 << k).then_inc(b_init, 1)
            nc.gpsimd.memset(cand, 1 << (BITS - 1)).then_inc(b_init, 1)
            nc.gpsimd.memset(onesf, 1.0).then_inc(b_init, 1)
            for i in range(NB):
                pool.wait_ge(q_e, i + 1)
                pool.wait_ge(q_r, i + 1)
                if i >= 2:
                    pool.wait_ge(q_t, i - 1)
                nc.gpsimd.tensor_tensor(qn[:, i % 2, :].rearrange("p (h d) -> p h d", h=H),
                                        eq_[:, i % 3, :].rearrange("p (h d) -> p h d", h=H),
                                        rq[:, i % 2, :].unsqueeze(2).broadcast_to([P, H, DH]),
                                        ALU.mult).then_inc(q_n, 1)
            pool.wait_ge(q_t, NB)
            nc.gpsimd.memset(ct, 0.0).then_inc(k_zero, 1)
            pool.wait_ge(r_tab, 6 * 16)
            for n in range(-2, E):
                e = n + 2
                if e < E:
                    pool.wait_ge(m_ls, e // 2 + 1)
                    if e >= 4:
                        pool.wait_ge(m_t, e - 3)
                        pool.wait_ge(m_eo, e - 3)
                    for h in range(2):
                        pool.indirect_dma_start(
                            xg[:, e % 4, h, :], None, table,
                            bass.IndirectOffsetOnAxis(ap=rowi[:, 2 * e + h:2 * e + h + 1], axis=0))\
                            .then_inc(g_x[e % 4], 16)
                if n >= 0:
                    if n == 0:
                        for b in range(5):
                            pool.wait_ge(x_d[b], 16 * len(range(b, B, 5)))
                    pool.wait_ge(m_eo, n + 1)
                    if n >= 1:
                        pool.wait_ge(g_s[(n - 1) % 2], 32 * ((n - 1) // 2 + 1))
                    for h in range(2):
                        pool.indirect_dma_start(
                            out, bass.IndirectOffsetOnAxis(ap=toki[:, 2 * n + h:2 * n + h + 1], axis=0),
                            eo[:, n % 4, h, :], None, compute_op=ALU.add).then_inc(g_s[n % 2], 16)
            for k in range(2):
                pool.wait_ge(g_s[k], 32 * (E // 2))

        @block.tensor
        def _(pe):
            mm, tp = nc.tensor.matmul, nc.tensor.transpose
            bank16 = lambda k: ps[:, k, :].bitcast(BF16)
            pe.wait_ge(in_x, 32)
            pe.wait_ge(s_ohn, 1)
            dftab, dftc = cbv("dftab"), cbv("dftc")
            for c, (at_, n) in enumerate(CH):
                if c >= 4:
                    pe.wait_ge(s_sq, 2 * (c - 3))
                for r in range(2):
                    o = ps[0:NF, 2 * (c % 4) + r, 0:n]
                    mm(o, dftab[:, r * NF:(r + 1) * NF], ohn2[:, at_:at_ + n], start=True, stop=False)
                    mm(o, dftc[:, r * NF:(r + 1) * NF], ohn2[0:NFFT, at_:at_ + n], start=False, stop=True)\
                        .then_inc(s_stft, 1)
            pe.wait_ge(s_mag, 1)
            pe.wait_ge(in_p, 48)
            for bank, lo_, n in ((4, 0, P), (5, P, V)):
                for v in range(V):
                    last = mm(ps[0:n, bank, 0:DS], mag[:, v * B * NT + lo_:v * B * NT + lo_ + n],
                              projw[:, v * DS:(v + 1) * DS], start=v == 0, stop=v == V - 1)
                last.then_inc(s_enc, 1)
            pe.wait_ge(s_fc, 2)
            pe.wait_ge(in_c, 32)
            tp(ps[:, 6, 0:P], fpc, ident)
            tp(ps[:, 6, P:P + 2 * V], fqc, ident[0:2 * V, 0:2 * V]).then_inc(s_tr, 1)
            pe.wait_ge(s_ft, 1)
            for q in range(2):
                for c in range(3):
                    mm(ps[0:P if q == 0 else 2 * V, 3 * q + c, :], ft[:, 0:P] if q == 0 else ft[:, P:P + 2 * V],
                       wqkv[:, c * HD:(c + 1) * HD], start=True, stop=True).then_inc(s_proj, 1)
            pe.wait_ge(s_xkey, 1)
            for b in range(B):
                if b >= 2:
                    pe.wait_ge(s_oh, b - 1)
                mm(ps[:, 6 + b % 2, :], identb[0:B, b:b + 1].broadcast_to([B, P]), xkey[:, :], start=True,
                   stop=True).then_inc(s_kb, 1)

            def expand(o, i, lo_, hi_, stop=True):
                mm(o, sela, ra[:, lo_:hi_], start=True, stop=False)
                return mm(o, selb, rb[:, i, lo_:hi_], start=False, stop=stop)

            pe.wait_ge(s_rb, 9 * 16)
            for k, (i0, n) in enumerate(TILES4):
                for i in range(n):
                    last = expand(ps[:, k, i * P:(i + 1) * P], i0 + i, HC, HC + D)
                last.then_inc(s_h0m, 1)
            pe.wait_ge(s_s1, 2)
            pe.wait_ge(s_oh, B)
            tp(ps[0:NB, 5, 0:P], s1, ident)
            tp(bank16(6)[0:NB, 0:P], absent, identb).then_inc(s_sTm, 1)
            pe.wait_ge(s_sT, 2)
            pe.wait_ge(s_h0, 5)
            for k, (i0, n) in enumerate(TILES4):
                for i in range(n):
                    last = mm(ps[:, k, i * P:(i + 1) * P], ident[0:NB, i0 + i:i0 + i + 1].broadcast_to([NB, P]),
                              sT[:, :], start=True, stop=True)
                last.then_inc(s_bcm, 1)
            for i in range(NB):
                if i >= 3:
                    pe.wait_ge(s_ktu, i - 2)
                for j in range(4):
                    o = ps[:, 5 + i % 3, j * P:(j + 1) * P]
                    c = KC + j * P
                    mm(o, ra[:, c:c + P], sela, start=True, stop=False)
                    mm(o, rb[:, i, c:c + P], selb, start=False, stop=False)
                    last = mm(o, identb[0:NB, i:i + 1].broadcast_to([NB, P]), maskT[:, :], start=False, stop=True)
                last.then_inc(s_kt, 1)
            pe.wait_ge(s_negm, 2)
            pe.wait_ge(s_bc, 5)
            for j in range(4):
                last = tp(bank16(0)[0:3 * B, j * P:(j + 1) * P], negm[:, j].rearrange("p s b -> p (s b)"), identb)
            last.then_inc(s_shm, 1)
            for i in range(NB):
                last = tp(bank16(1 + i // 8)[0:3 * B, (i % 8) * P:(i % 8 + 1) * P],
                          wsh[:, i].rearrange("p s b -> p (s b)"), identb)
            last.then_inc(s_shm, 1)

            pe.wait_ge(s_sh, 2)
            pe.wait_ge(s_ktu, NB)
            for n in range(NB + 4):
                if n < NB:
                    if n >= 4:
                        pe.wait_ge(q_e, n - 3)
                    expand(ps[:, 4 + n % 4, :], n, QC, QC + HD).then_inc(q_x, 1)
                i = n - 1
                if 0 <= i < NB:
                    pe.wait_ge(q_mx, i + 1)
                    if i >= 2:
                        pe.wait_ge(q_mc, i - 1)
                    tp(bank16(i % 2)[0:H, 0:P], mq[:, i % 3, :], identb).then_inc(q_mt, 1)
                i = n - 2
                if 0 <= i < NB:
                    pe.wait_ge(q_mc, i + 1)
                    mm(ps[:, 4 + i % 4, :], mqT[:, i % 2, :], cbv("headsel"), start=False, stop=True,
                       skip_group_check=True).then_inc(q_sh, 1)
                i = n - 4
                if 0 <= i < NB:
                    pe.wait_ge(q_n, i + 1)
                    if 2 <= i:
                        pe.wait_ge(q_c, i - 1)
                    for j in range(4):
                        last = tp(ps[:, 2 + i % 2, j * P:(j + 1) * P], qn[:, i % 2, j * P:(j + 1) * P], ident)
                    last.then_inc(q_t, 1)

            ORDER = [B, B + 1] + list(range(B))

            def kv(n):
                i = ORDER[n]
                if n >= 2:
                    pe.wait_ge(k_e, n - 1)
                expand(ps[:, n % 2, :], i, KC, KC + HD, stop=False)
                mm(ps[:, n % 2, :], lsh[:, i, :], nm[:, :], start=False, stop=True).then_inc(k_k, 1)
                if n >= 1:
                    pe.wait_ge(k_vc, n)
                expand(ps[:, 2, :], i, VC, VC + HD).then_inc(k_v, 1)

            def context(b):
                g, o, m = b // 8, b % 2, (b % 8) // 2
                q32 = slice(32 * m, 32 * m + 32)
                pe.wait_ge(k_e, b + 3)
                pe.wait_ge(k_vc, b + 3)
                if b >= 1:
                    pe.wait_ge(k_ca, b)
                    pe.wait_ge(k_cd, b)
                for j in range(4):
                    c = slice(j * P, (j + 1) * P)
                    mm(ps[:, 3, c], vv[:, b % 2, c], ek[:, b % 2, c], start=True, stop=False)
                    mm(ps[:, 3, c], vl[q32, g, o, c], ekl[q32, g, c], start=False, stop=True)
                for j in range(4):
                    c = slice(j * P, (j + 1) * P)
                    z = ps[:, 4, 4 * b + j:4 * b + j + 1]
                    mm(z, ek[:, b % 2, c], cnt[:, b:b + 1], start=True, stop=False)
                    last = mm(z, ekl[q32, g, c], cntl[q32, g, o:o + 1], start=False, stop=True)
                last.then_inc(k_cx, 1)

            def ctx_out(b):
                pe.wait_ge(k_ca, b + 1)
                pe.wait_ge(k_cd, b + 1)
                if b >= 1:
                    pe.wait_ge(k_mc, b)
                for j in range(4):
                    last = mm(ps[:, 5, j * P:(j + 1) * P], ct[:, b % 2, j, :], wo[:, j, :], start=True, stop=True)
                last.then_inc(k_m, 1)

            def rows_out(b):
                g, o, m = b // 8, b % 2, (b % 8) // 2
                q32 = slice(32 * m, 32 * m + 32)
                pe.wait_ge(k_mc, b + 1)
                if b >= 1:
                    pe.wait_ge(k_oc, b)
                for j in range(4):
                    mm(ps[:, 6, 0:P], qt[:, b, j, :], mb[:, b % 2, j, :],
                       start=j == 0, stop=j == 3)
                for j in range(4):
                    last = mm(ps[q32, 7, g * P:(g + 1) * P], qtl[:, g, o, j, q32], mb[:, b % 2, j, :],
                              start=o == 0 and j == 0, stop=o == 1 and j == 3)
                last.then_inc(k_o, 1)

            pe.wait_ge(q_e, NB)
            pe.wait_ge(q_c, B)
            pe.wait_ge(q_cl, 2)
            pe.wait_ge(in_r, 9 * 16)
            kv(0)
            kv(1)
            for n in range(B + 3):
                if n < B:
                    kv(n + 2)
                if 0 <= n - 1 < B:
                    context(n - 1)
                if 0 <= n - 2 < B:
                    ctx_out(n - 2)
                if 0 <= n - 3 < B:
                    rows_out(n - 3)

            pe.wait_ge(l_x, NB)
            for k, (i0, n) in enumerate(TILES4):
                for i in range(n):
                    last = tp(ps[:, k, i * P:(i + 1) * P], xn[:, i0 + i, :], ident)
                last.then_inc(r_t, 1)
            pe.wait_ge(r_c, 5)
            for i in range(NB):
                last = mm(ps[:, 5 + i // 16, (i % 16) * E:(i % 16 + 1) * E], xnT[:, i * P:(i + 1) * P], wrt[:, :],
                          start=True, stop=True)
            last.then_inc(r_l, 1)
            pe.wait_ge(r_p, 1)
            for k in range(5):
                last = tp(ps[:, k // 4, (k % 4) * P:(k % 4 + 1) * P],
                          pr[:, 4 * k:4 * k + 4, :].rearrange("p i e -> p (i e)"), ident)
            last.then_inc(r_bt, 1)
            pe.wait_ge(r_p, 2)
            for k in range(5):
                last = tp(ps[:, 2 + k // 4, (k % 4) * P:(k % 4 + 1) * P],
                          px[:, 4 * k:4 * k + 4, :].rearrange("p i e -> p (i e)"), ident)
            last.then_inc(r_bt, 1)

            def token_rows(b):
                if b == 0:
                    pe.wait_ge(x_p, 2)
                    pe.wait_ge(x_p2, 1)
                if b >= 2:
                    pe.wait_ge(x_c, b - 1)
                for w in range(4):
                    o = ps[:, 6 + b % 2, w * P:(w + 1) * P]
                    for q in range(3):
                        last = mm(o, oh[:, b, w * P:(w + 1) * P], h1p[:, q, b, :], start=q == 0,
                                  stop=q == 2 and w < 3)
                    if w == 3:
                        for q in range(3):
                            last = mm(o, ohl[:, b, :], h1p[:, q, B + b // 8, :], start=False, stop=q == 2)
                last.then_inc(x_m, 1)

            for k in range(BITS + 1):
                pe.wait_ge(b_part, k + 1)
                mm(ps[:, 5, 0:1], cfv("sameexp"), part, start=True, stop=True).then_inc(b_tot, 1)
                if k >= 2 and k % 1 == 0 and k - 2 < B:
                    token_rows(k - 2)
            pe.wait_ge(t_d, 1)
            mm(ps[:, 5, 64:64 + 2 * E], onesf, dtn, start=True, stop=True).then_inc(t_m, 1)
            pe.wait_ge(t_ge, 2)
            pe.wait_ge(x_c, B)
            for t in range(NTT):
                b, w = t // 4, t % 4
                o = ps[:, t // 8, (t % 8) * 2 * E:(t % 8 + 1) * 2 * E]
                last = mm(o, oh[:, b, w * P:(w + 1) * P], ge[:, b, :], start=True, stop=w < 3)
                if w == 3:
                    last = mm(o, ohl[:, b, :], ge[:, B + b // 8, :], start=False, stop=True)
                if t % 8 == 7:
                    last.then_inc(t_x, 1)
            pe.wait_ge(t_s, 1)
            pe.wait_ge(t_gt, 4)
            for k in range(4):
                mm(ps[:, k, :], cbv("notbefore"), eqT[:, k * 512:(k + 1) * 512], start=True, stop=False)
                mm(ps[:, k, :], cbv("onesb"), eqS[:, k * 512:(k + 1) * 512], start=False, stop=True).then_inc(t_rk, 1)
            pe.wait_ge(t_g, 1)
            mm(ps[:, 4, 2 * E:2 * E + NTT + 2], cbv("diff"), g0, start=True, stop=True)
            pe.wait_ge(t_pin, 2)
            mm(ps[:, 4, 0:E], cbv("before"), cq, start=True, stop=True)
            mm(ps[:, 4, E:2 * E], cbv("shift"), cq, start=True, stop=True).then_inc(t_bx, 1)
            for k in range(4):
                mm(ps[:, k, :], cbv("diff"), pin[:, k * 512:(k + 1) * 512], start=True, stop=True).then_inc(t_df, 1)

            def slots(gr):
                if gr >= 1:
                    pe.wait_ge(m_ls, gr)
                pe.wait_ge(t_st, 2 * gr + 2)
                for e in (2 * gr, 2 * gr + 1):
                    for h in range(2):
                        lhs = step[:, e, h * P:(h + 1) * P]
                        c = h * (2 * NTT + 3)
                        mm(ps[:, 6 + e % 2, c:c + NTT + 1], lhs, pd[:, e, 0:NTT + 1], start=True, stop=True)
                        last = mm(ps[:, 6 + e % 2, c + NTT + 1:c + 2 * NTT + 3], lhs, gd, start=True, stop=True)
                last.then_inc(m_sl, 1)

            def gathered(e):
                pe.wait_ge(g_x[e % 4], 32 * (e // 4 + 1))
                if e >= 2:
                    pe.wait_ge(m_tc, e - 1)
                for h in range(2):
                    last = tp(ps[:, 5 * (e % 2), h * P:(h + 1) * P], xg[:, e % 4, h, 0:D], ident)
                last.then_inc(m_t, 1)

            def up(e):
                pe.wait_ge(m_tc, e + 1)
                for k in range(FT):
                    n = min(P, FF - k * P)
                    if e >= 1:
                        pe.wait_ge(m_si, FT * (e - 1) + k + 1)
                    mm(ps[0:n, 1 + k, 0:CAP], wup[:, e // GS, k * P:k * P + n],
                       xgT[:, e % 2, :], start=True, stop=True).then_inc(m_up, 1)

            def down(e):
                pe.wait_ge(m_si, FT * (e + 1))
                if e >= 1:
                    pe.wait_ge(m_eo, e)
                for h in range(2):
                    for k in range(FT):
                        n = P if k < FT - 1 else FL + 1
                        last = mm(ps[:, 4, h * P:(h + 1) * P],
                                  actT[0:n, e % 2, k, h * P:(h + 1) * P], wdn[0:n, e, k, :],
                                  start=k == 0, stop=k == FT - 1)
                last.then_inc(m_dn, 1)

            pe.wait_ge(t_bc, 3)
            pe.wait_ge(t_pd, 4)
            pe.wait_ge(r_wd, 4 * 16)
            pe.wait_ge(m_one, 1)
            slots(0)
            slots(1)
            gathered(0)
            up(0)
            for e in range(E):
                if e % 2 == 0 and e // 2 + 2 < E // 2:
                    slots(e // 2 + 2)
                if e + 1 < E:
                    gathered(e + 1)
                    up(e + 1)
                down(e)

        @block.scalar
        def _(act):
            A_ = nc.scalar.activation
            nact = [0]

            def done(ins):
                nact[0] += 1
                ins.then_inc(s_act, 1)
                act.wait_ge(s_act, nact[0])

            for c, (at_, n) in enumerate(CH):
                for r in range(2):
                    act.wait_ge(s_stft, 2 * c + r + 1)
                    A_(sq[:, r, at_:at_ + n], ps[0:NF, 2 * (c % 4) + r, 0:n], ACT.Square).then_inc(s_sq, 1)
            act.wait_ge(s_msq, 5)
            A_(mag, sq[:, 0, :], ACT.Sqrt).then_inc(s_mag, 1)
            act.wait_ge(s_tr, 1)
            act.wait_ge(in_w, 32)
            A_(ft, ps[:, 6, 0:P + 2 * V], ACT.Copy, scale=gcol[:, 0:1]).then_inc(s_ft, 1)
            chunks = [(0, c) for c in range(4)] + [(1, c) for c in range(4)]

            def src(q, c):
                rows = P if q == 0 else 2 * V
                return ps[0:rows, 3 * q + c, :] if c < 3 else (fp if q == 0 else fq)

            def dst(tab, c):
                return tab[:, c * HD:c * HD + (HD if c < 3 else D)]

            for n, (q, c) in enumerate(chunks):
                if c < 3:
                    act.wait_ge(s_proj, 3 * q + c + 1)
                A_(dst((tabp if q == 0 else tabq)[:, 0, :], c), src(q, c), ACT.Copy).then_inc(s_hi, 1)
            for n, (q, c) in enumerate(chunks):
                act.wait_ge(s_r, n + 1)
                A_(dst((tabp if q == 0 else tabq)[:, 1, :], c), dst(tabx if q == 0 else tabxq, c), ACT.Copy)\
                    .then_inc(s_mid, 1)
            for k, (i0, n) in enumerate(TILES4):
                act.wait_ge(s_h0m, k + 1)
                A_(h0[:, i0:i0 + n, :].rearrange("p i c -> p (i c)"), ps[:, k, 0:n * P], ACT.Copy).then_inc(s_h0, 1)
            act.wait_ge(s_var, 1)
            A_(invs, lnv, ACT.Sqrt).then_inc(s_invs, 1)
            act.wait_ge(s_sTm, 1)
            A_(sT, ps[0:NB, 5, 0:P], ACT.Copy).then_inc(s_sT, 1)
            A_(maskT, ps[:, 6, :].bitcast(BF16)[0:NB, 0:P], ACT.Copy).then_inc(s_sT, 1)
            for k, (i0, n) in enumerate(TILES4):
                act.wait_ge(s_bcm, k + 1)
                A_(sbc[:, i0:i0 + n, :].rearrange("p i c -> p (i c)"), ps[:, k, 0:n * P], ACT.Copy).then_inc(s_bc, 1)
            act.wait_ge(s_shm, 1)
            A_(nm, ps[:, 0, :].bitcast(BF16)[0:3 * B, 0:HD], ACT.Copy).then_inc(s_sh, 1)
            act.wait_ge(s_shm, 2)
            for k, n in enumerate((8, 8, 2)):
                ins = A_(lsh[:, 8 * k:8 * k + n, :].rearrange("p i r -> p (i r)"),
                         ps[:, 1 + k, :].bitcast(BF16)[0:3 * B, 0:n * P], ACT.Copy)
            ins.then_inc(s_sh, 1)
            for n in range(1, NB + 4):
                i = n - 1
                if 0 <= i < NB:
                    act.wait_ge(q_mt, i + 1)
                    if i >= 2:
                        act.wait_ge(q_sh, i - 1)
                    A_(mqT[:, i % 2, :], ps[:, i % 2, :].bitcast(BF16)[0:H, 0:P], ACT.Copy).then_inc(q_mc, 1)
                i = n - 2
                if 0 <= i < NB:
                    act.wait_ge(q_sh, i + 1)
                    if i >= 3:
                        act.wait_ge(q_n, i - 2)
                    A_(eq_[:, i % 3, :], ps[:, 4 + i % 4, :], ACT.Exp, scale=s1[:, i:i + 1]).then_inc(q_e, 1)
                i = n - 4
                if 0 <= i < B:
                    act.wait_ge(q_t, i + 1)
                    A_(qt[:, i, :, :].rearrange("p j r -> p (j r)"), ps[:, 2 + i % 2, :], ACT.Copy).then_inc(q_c, 1)
            for n in range(-2, B + 3):
                if n < B:
                    i, m = (B + n + 2, n + 2) if n < 0 else (n, n + 2)
                    act.wait_ge(k_k, m + 1)
                    if n >= 2:
                        act.wait_ge(k_cx, n - 1)
                    if n == -2:
                        act.wait_ge(q_n, NB)
                        act.wait_ge(q_t, NB)
                        act.wait_ge(q_c, B)
                        act.wait_ge(q_cl, 2)
                    A_(ekl[:, n + 2, :] if n < 0 else ek[:, n % 2, :], ps[:, m % 2, :], ACT.Exp,
                       scale=s1[:, i:i + 1]).then_inc(k_e, 1)
                    act.wait_ge(k_v, m + 1)
                    if n < 0:
                        act.wait_ge(k_rz, 1)
                        for o in range(2):
                            ins = A_(vl[:, n + 2, o, :], ps[:, 2, :], ACT.Copy, scale=scl[:, n + 2, o:o + 1])
                    else:
                        ins = A_(vv[:, n % 2, :], ps[:, 2, :], ACT.Copy, scale=sc[:, i:i + 1])
                    ins.then_inc(k_vc, 1)
                b = n - 1
                if 0 <= b < B:
                    act.wait_ge(k_cx, b + 1)
                    if b == 0:
                        act.wait_ge(k_zero, 4)
                    if b >= 2:
                        act.wait_ge(k_m, b - 1)
                    A_(ct[0:DH, b % 2, :, 0:DH],
                       ps[0:DH, 3, :].rearrange("p (j c) -> p j c", j=4)[:, :, 0:DH], ACT.Copy).then_inc(k_ca, 1)
                b = n - 3
                if 0 <= b < B:
                    act.wait_ge(k_o, b + 1)
                    A_(qt[:, b, 0, :], ps[:, 6, 0:P], ACT.Copy).then_inc(k_oc, 1)
            for g in range(2):
                A_(qtl[:, g, 0, 0, :], ps[:, 7, g * P:(g + 1) * P], ACT.Copy).then_inc(k_oc, 1)
            act.wait_ge(l_v, 1)
            A_(rstd, lnv, ACT.Sqrt).then_inc(l_s, 1)
            act.wait_ge(l_v2, 1)
            A_(rstd, lnv, ACT.Sqrt).then_inc(l_s2, 1)
            act.wait_ge(l_n2, 1)
            for i in range(NB):
                A_(xn[:, i, :], h1[:, i, :], ACT.Identity, bias=nbias[:, i:i + 1], scale=rstd[:, i:i + 1])\
                    .then_inc(l_x, 1)
            for k, (i0, n) in enumerate(TILES4):
                act.wait_ge(r_t, k + 1)
                A_(xnT[:, i0 * P:(i0 + n) * P], ps[:, k, 0:n * P], ACT.Copy).then_inc(r_c, 1)
            act.wait_ge(r_sub, 1)
            A_(pr[:, 0:NB, :], px[:, 0:NB, :], ACT.Exp).then_inc(r_exp, 1)
            act.wait_ge(r_bt, 1)
            A_(pbis[:, 0:512], ps[:, 0, :], ACT.Copy)
            A_(pbis[:, 512:640], ps[:, 1, 0:P], ACT.Copy).then_inc(r_b, 1)
            act.wait_ge(r_bt, 2)
            A_(wbis[:, 0:512], ps[:, 2, :], ACT.Copy)
            A_(wbis[:, 512:640], ps[:, 3, 0:P], ACT.Copy).then_inc(r_b, 1)
            done(A_(h1p[:, 0], h1, ACT.Copy))
            act.wait_ge(x_p, 1)
            A_(h1p[:, 1], h1r, ACT.Copy).then_inc(x_p2, 1)
            for b in range(B):
                act.wait_ge(x_m, b + 1)
                if b >= 5:
                    act.wait_ge(x_d[b % 5], 16 * (b // 5))
                A_(hout[:, b % 5].rearrange("p w c -> p (w c)"), ps[:, 6 + b % 2, :], ACT.Copy).then_inc(x_c, 1)
            act.wait_ge(t_m, 1)
            act.wait_ge(r_tab, 6 * 16)
            for k in range(1, 8, 2):
                act.wait_ge(t_x, k + 1)
                for c, o in ((0, eqT), (E, gtT)):
                    ins = A_(o.rearrange("p (e t) -> p t e", e=E)[:, 8 * k:8 * k + 8, :],
                             ps[:, k, :].rearrange("p (t c) -> p t c", t=8)[:, :, c:c + E], ACT.Copy)
                ins.then_inc(t_gt, 1)
            for k in range(4):
                act.wait_ge(t_df, k + 1)
                A_(pd[:, 8 * k:8 * k + 8, 0:NTT], ps[:, k, :].rearrange("p (e t) -> p e t", e=8), ACT.Copy)\
                    .then_inc(t_pd, 1)
            for e in range(-1, E):
                if e + 1 < E:
                    n = e + 1
                    act.wait_ge(m_t, n + 1)
                    if n >= 2:
                        act.wait_ge(m_up, FT * (n - 1))
                    A_(xgT[:, n % 2, :], ps[:, 5 * (n % 2), 0:CAP], ACT.Copy).then_inc(m_tc, 1)
                    if n >= 2:
                        act.wait_ge(m_dn, n - 1)
                    if n == 0:
                        act.wait_ge(m_one, 1)
                    for k in range(FT):
                        r = min(P, FF - k * P)
                        act.wait_ge(m_up, FT * n + k + 1)
                        A_(actT[0:r, n % 2, k, :], ps[0:r, 1 + k, 0:CAP], ACT.Silu,
                           bias=bup[0:r, k, n // GS:n // GS + 1]).then_inc(m_si, 1)

        @block.vector
        def _(dve):
            vec = nc.vector
            ndve = [0]

            def done(ins):
                nonlocal_ = ndve
                nonlocal_[0] += 1
                ins.then_inc(s_dve, 1)
                dve.wait_ge(s_dve, nonlocal_[0])

            dve.wait_ge(in_x, 32)
            dve.wait_ge(in_c, 32)
            vec.tensor_tensor(ohn, xfrm[:, :].unsqueeze(1).broadcast_to([P, V, B * NT]),
                              cfv("ids").unsqueeze(2).broadcast_to([P, V, B * NT]), ALU.is_equal).then_inc(s_ohn, 1)
            vec.tensor_tensor(xkey[:, :], xseq, cfv("frame16"), ALU.add).then_inc(s_xkey, 1)
            for c, (at_, n) in enumerate(CH):
                dve.wait_ge(s_sq, 2 * c + 2)
                vec.scalar_tensor_tensor(out=sq[:, 0, at_:at_ + n], in0=sq[:, 0, at_:at_ + n], scalar=1e-34,
                                         in1=sq[:, 1, at_:at_ + n], op0=ALU.max, op1=ALU.add).then_inc(s_msq, 1)
            dve.wait_ge(s_enc, 2)
            dve.wait_ge(k_zero, 3)
            vec.tensor_tensor(fp[:, DE:D], ps[:, 4, 0:DS], projb, ALU.add)
            done(vec.tensor_tensor(fq[0:V, DE:D], ps[0:V, 5, 0:DS], projb[0:V], ALU.add))
            vec.tensor_reduce(fm[:, 0:1], fp, AX.X, ALU.add)
            done(vec.tensor_reduce(fm[0:2 * V, 1:2], fq, AX.X, ALU.add))
            done(vec.tensor_scalar(fm[:, 2:3], fm[:, 0:1], -1.0 / D, None, ALU.mult))
            done(vec.tensor_scalar(fm[0:2 * V, 3:4], fm[0:2 * V, 1:2], -1.0 / D, None, ALU.mult))
            vec.tensor_scalar(fpc, fp, fm[:, 2:3], None, ALU.add).then_inc(s_fc, 1)
            vec.tensor_scalar(fqc, fq, fm[0:2 * V, 3:4], None, ALU.add).then_inc(s_fc, 1)
            chunks = [(0, c) for c in range(4)] + [(1, c) for c in range(4)]

            def src(q, c):
                rows = P if q == 0 else 2 * V
                return ps[0:rows, 3 * q + c, :] if c < 3 else (fp if q == 0 else fq)

            def dst(tab, c):
                return tab[:, c * HD:c * HD + (HD if c < 3 else D)]

            for n, (q, c) in enumerate(chunks):
                dve.wait_ge(s_hi, n + 1)
                vec.tensor_tensor(dst(tabx if q == 0 else tabxq, c), src(q, c),
                                  dst((tabp if q == 0 else tabq)[:, 0, :], c), ALU.subtract).then_inc(s_r, 1)
            for n, (q, c) in enumerate(chunks):
                dve.wait_ge(s_mid, n + 1)
                vec.tensor_tensor(dst((tabp if q == 0 else tabq)[:, 2, :], c), dst(tabx if q == 0 else tabxq, c),
                                  dst((tabp if q == 0 else tabq)[:, 1, :], c), ALU.subtract).then_inc(s_lo, 1)
            for b in range(B):
                dve.wait_ge(s_kb, b + 1)
                vec.tensor_scalar(oh[:, b, :], ps[:, 6 + b % 2, :], cfv("pidx"), 0.0, ALU.is_equal, ALU.add,
                                  accum_out=cnt[:, b:b + 1])
                vec.tensor_scalar(ohl[:, b, LAST0 - 3 * P:P], ps[:, 6 + b % 2, LAST0:L], cfv("lastid"),
                                  cfv("lastb")[:, b:b + 1], ALU.is_equal, ALU.mult).then_inc(s_oh, 1)
            dve.wait_ge(s_oh, B)
            for g in range(2):
                ins = vec.tensor_reduce(cnt[:, B + g:B + g + 1], ohl[:, 8 * g:8 * g + 8, LAST0 - 3 * P:P], AX.XY,
                                        ALU.add)
            done(ins)
            vec.tensor_scalar(absent, cnt[:, 0:NB], 0.5, -1e30, ALU.is_lt, ALU.mult).then_inc(s_s1, 1)

            def variances(rows, eps_of):
                for i in range(NB):
                    ins = vec.bn_stats(stats[:, i, :], rows(i))
                done(ins)
                for i in range(NB):
                    ins = vec.bn_aggr(mv[:, i, :], stats[:, i, :])
                done(ins)
                return vec.tensor_scalar(lnv, mv[:, :, 1], eps_of[0], eps_of[1], ALU.mult, ALU.add)

            dve.wait_ge(s_h0, 5)
            variances(lambda i: h0[:, i, :], (1.0 + EPS, EPS * EPS)).then_inc(s_var, 1)
            dve.wait_ge(s_invs, 1)
            done(vec.reciprocal(s1, invs))
            vec.tensor_copy(ivp[:, 0, :], invs).then_inc(s_s1, 1)
            done(vec.tensor_tensor(sc, s1, cnt[:, 0:NB], ALU.mult))
            done(vec.tensor_tensor(ivr[:, 0, :], invs, ivp[:, 0, :], ALU.subtract))
            done(vec.tensor_copy(ivp[:, 1, :], ivr[:, 0, :]))
            done(vec.tensor_tensor(ivp[:, 2, :], ivr[:, 0, :], ivp[:, 1, :], ALU.subtract))
            for q in range(3):
                ins = vec.tensor_tensor(wsh[:, :, q, :], cbv("rowb").rearrange("p (i b) -> p i b", i=NB),
                                        ivp[:, q, :].unsqueeze(2).broadcast_to([P, NB, B]), ALU.mult)
            ins.then_inc(s_negm, 1)
            par = cfv("parity")
            for g in range(2):
                for o in range(2):
                    vec.tensor_tensor(scl[:, g, o:o + 1], sc[:, B + g:B + g + 1], par[:, o:o + 1], ALU.mult)
                    ins = vec.tensor_tensor(cntl[:, g, o:o + 1], cnt[:, B + g:B + g + 1], par[:, o:o + 1], ALU.mult)
            ins.then_inc(k_rz, 1)
            dve.wait_ge(s_bc, 5)
            for i in range(NB):
                dve.wait_ge(s_kt, i + 1)
                ins = vec.tensor_tensor(prod[:, i % 2], ps[:, 5 + i % 3, :].rearrange("p (j r) -> p j r", j=4),
                                        sbc[:, i, :].unsqueeze(1).broadcast_to([P, 4, P]), ALU.mult)
                ins.then_inc(s_ktu, 1)
                dve.wait_ge(s_ktu, i + 1)
                if i < B:
                    vec.tensor_reduce(mx[:, :, i:i + 1], prod[:, i % 2], AX.X, ALU.max)
                else:
                    ins = vec.tensor_reduce(mxl[:, :, 8 * (i - B):8 * (i - B) + 8],
                                            prod[:, i % 2].rearrange("p j (b v) -> p j b v", b=8), AX.X, ALU.max)
            done(ins)
            done(vec.tensor_tensor(mx, mx, mxl, ALU.max))
            for q in range(3):
                ins = vec.tensor_scalar(negm[:, :, q, :], mx, -1.0, None, ALU.mult)
            ins.then_inc(s_negm, 1)
            for n in range(NB + 5):
                if n < NB:
                    dve.wait_ge(q_x, n + 1)
                    if n >= 3:
                        dve.wait_ge(q_mt, n - 2)
                    vec.tensor_reduce(mq[:, n % 3, :], ps[:, 4 + n % 4, :].rearrange("p (h d) -> p h d", h=H), AX.X,
                                      ALU.max, negate=True).then_inc(q_mx, 1)
                i = n - 3
                if 0 <= i < NB:
                    dve.wait_ge(q_e, i + 1)
                    if i >= 2:
                        dve.wait_ge(q_n, i - 1)
                    done(vec.tensor_reduce(zq[:, i % 2, :], eq_[:, i % 3, :].rearrange("p (h d) -> p h d", h=H),
                                           AX.X, ALU.add))
                    vec.reciprocal(rq[:, i % 2, :], zq[:, i % 2, :]).then_inc(q_r, 1)
                i = n - 5
                if B <= i < NB:
                    dve.wait_ge(q_t, i + 1)
                    for o in range(2):
                        ins = vec.tensor_tensor(
                            qtl[:, i - B, o], ps[:, 2 + i % 2, :].rearrange("p (j r) -> p j r", j=4),
                            cfv("parrow")[:, o * P:(o + 1) * P].unsqueeze(1).broadcast_to([P, 4, P]), ALU.mult)
                    ins.then_inc(q_cl, 1)
            for n in range(1, B + 2):
                b = n - 1
                if 0 <= b < B:
                    dve.wait_ge(k_cx, b + 1)
                    if b == 0:
                        dve.wait_ge(k_zero, 4)
                    if b >= 2:
                        dve.wait_ge(k_m, b - 1)
                    vec.tensor_copy(ct[DH:P, b % 2, :, DH:P],
                                    ps[DH:P, 3, :].rearrange("p (j c) -> p j c", j=4)[:, :, DH:P])
                    vec.reciprocal(rz[:, b, :], ps[:, 4, 4 * b:4 * b + 4]).then_inc(k_cd, 1)
                    dve.wait_ge(k_cd, b + 1)
                    done(vec.tensor_scalar(rz[:, b, :], rz[:, b, :], DH ** -0.5, None, ALU.mult))
                b = n - 2
                if 0 <= b < B:
                    dve.wait_ge(k_m, b + 1)
                    if b >= 2:
                        dve.wait_ge(k_o, b - 1)
                    vec.tensor_tensor(mb[:, b % 2], ps[:, 5, :].rearrange("p (j c) -> p j c", j=4),
                                      rz[:, b, :].unsqueeze(2).broadcast_to([P, 4, P]), ALU.mult).then_inc(k_mc, 1)
            dve.wait_ge(k_oc, NB)
            ao = lambda i: qt[:, i, 0, :] if i < B else qtl[:, i - B, 0, 0, :]
            variances(ao, (1.0, EPS)).then_inc(l_v, 1)
            dve.wait_ge(l_s, 1)
            done(vec.reciprocal(rstd, rstd))
            done(vec.scalar_tensor_tensor(out=nbias, in0=mv[:, :, 0], scalar=-1.0, in1=rstd, op0=ALU.mult,
                                          op1=ALU.mult))
            for i in range(NB):
                ins = vec.tensor_scalar(h1[:, i, :], ao(i), rstd[:, i:i + 1], nbias[:, i:i + 1], ALU.mult, ALU.add)
            done(ins)
            done(vec.tensor_tensor(h1, h1, ogam[:, :].unsqueeze(1).broadcast_to([P, NB, D]), ALU.mult))
            done(vec.tensor_tensor(h1, h1, h0[:, :, :], ALU.add))
            variances(lambda i: h1[:, i, :], (1.0, EPS)).then_inc(l_v2, 1)
            dve.wait_ge(l_s2, 1)
            done(vec.reciprocal(rstd, rstd))
            vec.scalar_tensor_tensor(out=nbias, in0=mv[:, :, 0], scalar=-1.0, in1=rstd, op0=ALU.mult,
                                     op1=ALU.mult).then_inc(l_n2, 1)
            dve.wait_ge(r_l, 1)
            vec.tensor_tensor(px[:, 0:B, :], ps[:, 5, :].rearrange("p (i e) -> p i e", i=B),
                              brt[:, :].unsqueeze(1).broadcast_to([P, B, E]), ALU.add)
            done(vec.tensor_tensor(px[:, B:NB, :], ps[:, 6, 0:2 * E].rearrange("p (i e) -> p i e", i=2),
                                   brt[:, :].unsqueeze(1).broadcast_to([P, 2, E]), ALU.add))
            done(vec.tensor_reduce(pmx, px[:, 0:NB, :], AX.X, ALU.max))
            vec.tensor_tensor(px[:, 0:NB, :], px[:, 0:NB, :], pmx.unsqueeze(2).broadcast_to([P, NB, E]),
                              ALU.subtract).then_inc(r_sub, 1)
            dve.wait_ge(r_exp, 1)
            done(vec.tensor_reduce(psm, pr[:, 0:NB, :], AX.X, ALU.add))
            done(vec.reciprocal(psm, psm))
            dve.wait_ge(b_init, 34)
            vec.tensor_tensor(pr[:, 0:NB, :], pr[:, 0:NB, :], psm.unsqueeze(2).broadcast_to([P, NB, E]),
                              ALU.mult).then_inc(r_p, 1)
            vec.tensor_copy(px, cnt.unsqueeze(2).broadcast_to([P, 20, E])).then_inc(r_p, 1)
            dve.wait_ge(r_b, 2)
            cf_ = cand.bitcast(F32)

            def count(op):
                vec.scalar_tensor_tensor(out=junk, in0=pbis, scalar=cf_, in1=wbis, op0=op, op1=ALU.mult,
                                         accum_out=part).then_inc(b_part, 1)

            for k in range(BITS):
                bit = BITS - 1 - k
                count(ALU.is_ge)
                if k == 0:
                    dve.wait_ge(s_act, 1)
                    done(vec.tensor_tensor(h1r, h1, h1p[:, 0], ALU.subtract))
                    vec.tensor_copy(sv[:, 0:1], h1r[:, 0, 0:1]).then_inc(x_p, 1)
                if k == 1:
                    dve.wait_ge(x_p2, 1)
                    vec.tensor_tensor(h1p[:, 2], h1r, h1p[:, 1], ALU.subtract).then_inc(x_p, 1)
                dve.wait_ge(b_tot, k + 1)
                done(vec.tensor_scalar(delta, ps[:, 5, 0:1], CAP - 0.5, float(1 << bit), ALU.is_lt, ALU.mult))
                if bit > 0:
                    done(vec.scalar_tensor_tensor(out=cand, in0=cand, scalar=delta, in1=bits[:, bit - 1:bit],
                                                  op0=ALU.bitwise_xor, op1=ALU.bitwise_xor))
                else:
                    done(vec.tensor_tensor(cand, cand, delta, ALU.bitwise_xor))
            count(ALU.is_gt)
            dve.wait_ge(b_tot, BITS + 1)
            done(vec.tensor_scalar(need, ps[:, 5, 0:1], -1.0, float(CAP), ALU.mult, ALU.add))
            vec.tensor_scalar(dtn[:, 0:E], cfv("eyeexp")[0:E], cf_[0:E], None, ALU.mult)
            vec.tensor_scalar(dtn[:, E:2 * E], cfv("eyeexp")[0:E], need[0:E], None, ALU.mult).then_inc(t_d, 1)
            dve.wait_ge(t_m, 1)
            done(vec.tensor_copy(tn, ps[:, 5, 64:64 + 2 * E]))
            for q, op in ((0, ALU.is_equal), (1, ALU.is_gt)):
                vec.tensor_tensor(ge[:, :, q * E:(q + 1) * E], pr[:, 0:NB, :],
                                  tn[:, 0:E].unsqueeze(1).broadcast_to([P, NB, E]), op).then_inc(t_ge, 1)
            done(vec.tensor_tensor(vtok, xtok[:, :], cfv("tau16"), ALU.add))
            vec.tensor_tensor(g0[:, 0:NTT - 1], vtok[:, 1:NTT], vtok[:, 0:NTT - 1], ALU.subtract)
            vec.memset(g0[:, NTT - 1:NTT], 0.0)
            vec.tensor_copy(g0[:, NTT:NTT + 1], vtok[:, 0:1])
            vec.tensor_copy(g0[:, NTT + 1:NTT + 2], cfv("pidx")).then_inc(t_g, 1)
            vec.memset(actT[64:P, :, FT - 1, :], 1.0).then_inc(m_one, 1)
            dve.wait_ge(r_tab, 6 * 16)
            for k in range(0, 8, 2):
                dve.wait_ge(t_x, k + 1)
                for c, o in ((0, eqT), (E, gtT)):
                    ins = vec.tensor_copy(o.rearrange("p (e t) -> p t e", e=E)[:, 8 * k:8 * k + 8, :],
                                          ps[:, k, :].rearrange("p (t c) -> p t c", t=8)[:, :, c:c + E])
                ins.then_inc(t_eq, 1)
            dve.wait_ge(t_eq, 4)
            dve.wait_ge(t_gt, 4)
            vec.tensor_tensor_scan(eqS, cbv("carry"), eqT, 0.0, ALU.mult, ALU.add).then_inc(t_s, 1)
            dve.wait_ge(t_s, 1)
            for k in range(4):
                c = slice(k * 512, (k + 1) * 512)
                dve.wait_ge(t_rk, k + 1)
                done(vec.tensor_tensor(pin[:, c].rearrange("p (e t) -> p e t", e=8),
                                       ps[:, k, :].rearrange("p (e t) -> p e t", e=8),
                                       tn[:, E + 8 * k:E + 8 * k + 8].unsqueeze(2).broadcast_to([P, 8, NTT]),
                                       ALU.is_lt))
                done(vec.tensor_tensor(eqT[:, c], pin[:, c], eqT[:, c], ALU.mult))
                done(vec.tensor_tensor(gtT[:, c], eqT[:, c], gtT[:, c], ALU.add))
            done(vec.tensor_tensor_scan(pin, cbv("carry"), gtT, 0.0, ALU.mult, ALU.add))
            vec.tensor_copy(cq, pin.rearrange("p (e t) -> p e t", e=E)[:, :, NTT - 1]).then_inc(t_pin, 2)
            dve.wait_ge(t_bx, 1)
            vec.tensor_copy(bx, ps[:, 4, 0:E]).then_inc(t_bc, 1)
            vec.tensor_copy(pd[:, :, NTT], ps[:, 4, E:2 * E]).then_inc(t_bc, 1)
            vec.tensor_copy(gd, ps[:, 4, 2 * E:2 * E + NTT + 2]).then_inc(t_bc, 1)
            dve.wait_ge(t_bc, 3)
            for e in range(E):
                vec.tensor_scalar(step[:, e, :], cbv("slots"), bx[:, e:e + 1], None, ALU.is_ge).then_inc(t_st, 1)

            def listed(gr):
                v = ps[:, 6:8, 0:2 * (2 * NTT + 3)].rearrange("p b (h c) -> p b h c", h=2)
                as3 = lambda a: a.rearrange("p (b h) -> p b h", b=2)
                dve.wait_ge(m_sl, gr + 1)
                done(vec.tensor_tensor(as3(sr), cfv("slot").unsqueeze(1).broadcast_to([P, 2, 2]), v[:, :, :, NTT],
                                       ALU.subtract))
                done(vec.tensor_tensor(lm, v[:, :, :, 0:NTT],
                                       as3(sr).unsqueeze(3).broadcast_to([P, 2, 2, NTT]), ALU.is_le))
                done(vec.tensor_tensor(lp, lm, v[:, :, :, NTT + 1:2 * NTT + 1], ALU.mult))
                done(vec.tensor_reduce(sv, lp.rearrange("p b h c -> p (b h) c"), AX.X, ALU.add))
                done(vec.tensor_tensor(as3(vi), as3(sv), v[:, :, :, 2 * NTT + 1], ALU.add))
                vec.tensor_scalar(offi, vi, 4, None, ALU.arith_shift_right)
                done(vec.tensor_scalar(idi, vi, V - 1, None, ALU.bitwise_and))
                done(vec.tensor_scalar(sv, offi, float(P), None, ALU.mult))
                done(vec.tensor_tensor(as3(sr), as3(sv), v[:, :, :, 2 * NTT + 2], ALU.add))
                vec.tensor_copy(toki[:, 4 * gr:4 * gr + 4], sr)
                done(vec.tensor_scalar(seg, sr, NT / L, 0.5 / L - 0.5 + 0.5 / L, ALU.mult, ALU.add))
                vec.scalar_tensor_tensor(out=rowi[:, 4 * gr:4 * gr + 4], in0=seg, scalar=float(V), in1=idi,
                                         op0=ALU.mult, op1=ALU.add).then_inc(m_ls, 1)

            listed(0)
            listed(1)
            for e in range(E):
                if e % 2 == 0 and e // 2 + 2 < E // 2:
                    listed(e // 2 + 2)
                dve.wait_ge(m_dn, e + 1)
                if e >= 4:
                    dve.wait_ge(g_s[e % 2], 32 * (e // 2 - 1))
                for h in range(2):
                    c = h * P
                    ins = vec.tensor_scalar(eo[:, e % 4, h, :], ps[:, 4, c:c + P],
                                            xg[:, e % 4, h, D + e:D + e + 1], None, ALU.mult)
                ins.then_inc(m_eo, 1)


_OUT = "out_dram"


def kernel(**inputs):
    import concourse.bacc as bacc
    from concourse.bass_utils import run_bass_kernel_spmd

    c = np.ascontiguousarray
    x = np.asarray(inputs["x"])
    at = np.arange(NT * NFFT) - NFFT // 2
    at = np.where(at < 0, -at, at)
    at = np.where(at >= L, 2 * (L - 1) - at, at)
    frames = x[:, at].reshape(B, NT, NFFT)
    cols = np.concatenate([frames[:, :TM].reshape(B * TM, NFFT), frames[:, TM]], 0).T
    cf, cb = constants()
    w_qkv, w_out, b_up = (np.asarray(inputs[n]) for n in ("L0_attn_w_qkv", "L0_attn_w_out", "L0_ffn_b_up"))
    arrays = {
        "x_frames": c(np.concatenate([cols, cols], 0)),
        "x_seq": c(x),
        "x_tokens": c(x.reshape(NTT, P).T),
        "const_f32": _pack(cf, np.float32),
        "const_bf16": _pack(cb, mybir.dt.np(BF16)),
        "emb": c(inputs["L0_tok_emb_table"]),
        "proj_w": c(np.asarray(inputs["L0_tok_proj_w"]).reshape(NF, V * DS)),
        "proj_b": c(inputs["L0_tok_proj_b"]),
        "norm_gamma": c(np.asarray(inputs["L0_attn_norm_gamma"]).reshape(D, 1)),
        "w_qkv_t": c(w_qkv.T),
        "w_out_t": c(w_out.T),
        "out_gamma": c(inputs["L0_attn_out_gamma"]),
        "w_router": c(inputs["L0_ffn_W_router"]),
        "b_router": c(inputs["L0_ffn_b_router"]),
        "w_up": c(inputs["L0_ffn_W_up"]),
        "b_up_t": c(b_up.T),
        "w_down": c(inputs["L0_ffn_W_down"]),
        "b_down": c(inputs["L0_ffn_b_down"]),
    }
    nc = bacc.Bacc("TRN2", target_bir_lowering=False, num_devices=1)
    args = {n: nc.dram_tensor(f"in_{n}", a.shape, mybir.dt.from_np(a.dtype), kind="ExternalInput").ap()
            for n, a in arrays.items()}
    out = nc.dram_tensor(_OUT, (B * L, D), F32, kind="ExternalOutput").ap()
    program(nc, args, out)
    r = run_bass_kernel_spmd(nc, [{f"in_{n}": a for n, a in arrays.items()}], core_ids=[0])
    return r.results[0][_OUT].reshape(B, L, D)
```

```python
from contextlib import ExitStack

import concourse.bass as bass
from concourse import mybir
import numpy as np

ALU = mybir.AluOpType
ACT = mybir.ActivationFunctionType
AX = mybir.AxisListType
F32 = mybir.dt.float32
BF16 = mybir.dt.bfloat16
I32 = mybir.dt.int32
U32 = mybir.dt.uint32

P = 128
B, L, V = 16, 512, 16
NFFT, HOP = 64, 64
NT = L // HOP + 1
NF = NFFT // 2 + 1
D, DE = 128, 89
DS = D - DE
H, DH = 8, 64
HD = H * DH
E, GS = 32, 4
NG = E // GS
FF = 341
FT = (FF + P - 1) // P
FL = FF - (FT - 1) * P
CAP = B * L // E
EPS = 1e-5
TM = NT - 1
NB = B + B // 8
NTT = B * L // P
UW = H * D
KC, HC, QC, UC = 0, HD, HD + D, 2 * HD + D
CW = 2 * HD + D + UW
KR = 3 * V + 3 * TM
GROUPS = ((KC, HC + D), (QC, UC), (UC, CW))
CHUNKS = ((KC, HD), (HC, D), (QC, HD), (UC, HD), (UC + HD, HD))
BITS = 30
TW = D + E
LAST0 = -(-L * TM // NT)


def _split3(a):
    bf = mybir.dt.np(BF16)
    hi = a.astype(bf)
    r = a - hi.astype(np.float64)
    mid = r.astype(bf)
    lo = (r - mid.astype(np.float64)).astype(bf)
    return hi.astype(np.float64), mid.astype(np.float64), lo.astype(np.float64)


def constants():
    p = np.arange(P)
    n = np.arange(NFFT)
    f = np.arange(NF)
    win = 0.5 - 0.5 * np.cos(2 * np.pi * n / NFFT)
    ang = 2 * np.pi * np.outer(n, f) / NFFT
    dft = np.concatenate([win[:, None] * np.cos(ang), -win[:, None] * np.sin(ang)], 1)
    wide = np.zeros((NFFT, 2, P // 2))
    wide[:, :, :NF] = dft.reshape(NFFT, 2, NF)
    hi, mid, lo = _split3(wide.reshape(NFFT, P))
    eye = np.eye(P)
    cf = {
        "ident": eye,
        "frame16": np.tile(16.0 * (np.arange(L) * NT // L), (B, 1)),
        "sameexp": (p[:, None] % E == p[None, :] % E) * 1.0,
        "eyeexp": (p[:, None] == np.arange(E)[None, :]) * 1.0,
        "pidx": p[:, None] * 1.0,
        "lastid": (P + p[:, None] % V) * 1.0,
        "lastb": (np.arange(B)[None, :] % 8 == p[:, None] // V) * 1.0,
        "lastsel": (np.arange(8)[None, :] == p[:, None] // V) * 1.0,
        "parity": np.stack([p // V % 2 == 0, p // V % 2 == 1], 1) * 1.0,
        "parrow": np.tile(np.stack([p // V % 2 == 0, p // V % 2 == 1], 0).reshape(1, 2 * P), (P, 1)) * 1.0,
        "slot": np.stack([p, p + P], 1) * 1.0,
        "ids": np.tile(np.arange(V), (P, 1)) * 1.0,
        "tau16": np.tile(16.0 * np.arange(NTT), (P, 1)),
    }
    cb = {
        "dftab": np.concatenate([hi, mid], 0),
        "dftc": np.concatenate([lo, 0 * lo], 0),
        "sel": np.concatenate([np.tile(np.arange(V)[:, None] == p[None, :] % V, (3, 1)),
                               np.tile(np.arange(TM)[:, None] == p[None, :] // V, (3, 1))], 0) * 1.0,
        "identb": eye,
        "before": (p[:, None] < p[None, :]) * 1.0,
        "notbefore": -1.0 * (p[:, None] >= p[None, :]),
        "onesb": np.ones((P, P)),
        "diff": eye * 1.0 - (p[:, None] == p[None, :] - 1),
        "shift": (p[:, None] == p[None, :] - 1) * 1.0,
        "headsel": (np.arange(HD)[None, :] // DH == np.arange(KR)[:, None]) * 1.0,
        "slots": np.tile(np.arange(CAP), (P, 1)) * 1.0,
        "carry": np.tile(np.arange(NTT) > 0, (P, E)) * 1.0,
        "rowb": np.stack([np.tile(np.arange(B) == i, (P, 1)) if i < B else
                          np.arange(B)[None, :] == 8 * (i - B) + p[:, None] // V for i in range(NB)], 1) * 1.0,
    }
    return cf, cb


def _layout(tables):
    at, where = 0, {}
    for name, a in tables.items():
        w = int(np.prod(a.shape[1:]))
        where[name] = (a.shape[0], at, w)
        at += w
    return where, at


def _pack(tables, dtype):
    where, width = _layout(tables)
    out = np.zeros((P, width), dtype)
    for name, a in tables.items():
        r, at, w = where[name]
        out[:r, at:at + w] = a.reshape(r, w).astype(dtype)
    return out



def program(nc, A, out):
    cfw, cfn = _layout(constants()[0])
    cbw, cbn = _layout(constants()[1])
    with ExitStack() as ctx:
        def sb(name, shape, dt=F32):
            return ctx.enter_context(nc.sbuf_tensor(name, shape, dt))

        def sem(name):
            return ctx.enter_context(nc.semaphore(name))

        cf = sb("cf", [P, cfn])
        cb = sb("cb", [P, cbn], BF16)

        def cfv(name):
            r, at, w = cfw[name]
            return cf[0:r, at:at + w]

        def cbv(name):
            r, at, w = cbw[name]
            return cb[0:r, at:at + w]

        ident, identb = cfv("ident"), cbv("identb")
        sel = cbv("sel")
        xfrm = sb("xfrm", [P, B * NT], I32)
        xtok = sb("xtok", [P, NTT], I32)

        gcol = sb("gcol", [P, 1])
        ogam = sb("ogam", [P, D])
        wrt = sb("wrt", [P, P])
        brt = sb("brt", [P, E])

        bup = sb("bup", [P, FT, NG])
        wo = sb("wo", [P, 4, D])
        oh = sb("oh", [P, B, L], BF16)
        ohl = sb("ohl", [P, B, P], BF16)


        arA = sb("arA", [P, NB * CW // 2])
        tabx = arA[:, 0:CW]
        tabxq = arA[0:2 * V, CW:2 * CW]
        tabp = arA[:, 2 * CW:2 * CW + 3 * CW // 2].bitcast(BF16).rearrange("p (s c) -> p s c", s=3)
        tabq = arA[0:2 * V, 4 * CW:4 * CW + 3 * CW // 2].bitcast(BF16).rearrange("p (s c) -> p s c", s=3)
        rb = arA[0:KR, :].bitcast(BF16).rearrange("p (i c) -> p i c", i=NB)
        WD = E * FT * D
        wdn = arA[:, 0:WD].rearrange("p (e k h) -> p e k h", e=E, k=FT)
        h1 = arA[:, WD:WD + NB * D].rearrange("p (i c) -> p i c", i=NB)
        wup = arA[:, WD + NB * D:WD + NB * D + NG * FF].rearrange("p (g f) -> p g f", g=NG)

        BW = B * HD + 2 * 2 * HD
        arB = sb("arB", [P, BW])

        def at(arena, start, words, rows=P, dt=F32):
            v = arena[0:rows, start:start + words]
            return v if dt == F32 else v.bitcast(dt)

        ohn = at(arB, 0, 1152, P, BF16).rearrange("p (v k) -> p v k", v=V)
        sq = at(arB, 1152, 2304).rearrange("p (r c) -> p r c", r=2)
        mag = at(arB, 3456, 1152).rearrange("p (v k) -> p v k", v=V // 2)
        wall = at(arB, 4608, 2 * HD + UW)
        wv = at(arB, 6656, 4 * D).rearrange("p (j c) -> p j c", j=4)
        projw = at(arB, 7168, V // 2 * D).rearrange("p (v c) -> p v c", v=V // 2)
        xkey = at(arB, 8192, L // 2, P, BF16)
        qt = at(arB, 0, B * HD).rearrange("p (i j r) -> p i j r", i=B, j=4)
        qtl = at(arB, B * HD, 4 * HD).rearrange("p (g o j r) -> p g o j r", g=2, o=2, j=4)
        xn = at(arB, 0, NB * D).rearrange("p (i c) -> p i c", i=NB)
        xnT = at(arB, 2304, NB * P)
        SW = E * NTT // 2
        eqT = at(arB, 0, SW, P, BF16)
        gtT = at(arB, SW, SW, P, BF16)
        eqS = at(arB, 2 * SW, SW, P, BF16)
        pin = at(arB, 3 * SW, SW, P, BF16)
        PDW = E * (NTT + 2) // 2
        pd = at(arB, 4 * SW, PDW, P, BF16).rearrange("p (e t) -> p e t", e=E)
        step = at(arB, 4 * SW + PDW, E * CAP // 2, P, BF16).rearrange("p (e s) -> p e s", e=E)

        arC = sb("arC", [P, 4096 + 4 * H * (D + 1)])
        sbc = at(arC, 0, NB * P).rearrange("p (i r) -> p i r", i=NB)
        prod = at(arC, 2304, 512, P, BF16).rearrange("p (s j r) -> p s j r", s=2, j=4)
        eq_ = at(arC, 3072, 3 * HD).rearrange("p (s c) -> p s c", s=3)
        qn = at(arC, 4608, 2 * HD).rearrange("p (s c) -> p s c", s=2)
        ek = at(arC, 0, 2 * HD).rearrange("p (s c) -> p s c", s=2)
        ekl = at(arC, 1024, 2 * HD).rearrange("p (s c) -> p s c", s=2)
        ekm = at(arC, 2048, 2 * HD).rearrange("p (s c) -> p s c", s=2)
        mb = at(arC, 3072, 2 * HD).rearrange("p (s j c) -> p s j c", s=2, j=4)
        uu = at(arC, 4096, 4 * H * (D + 1)).rearrange("p (s h c) -> p s h c", s=4, h=H)
        pbis = at(arC, 0, 640)
        wbis = at(arC, 640, 640)
        junk = at(arC, 1280, 640)
        h1p = at(arC, 1920, 3 * NB * D // 2, P, BF16).rearrange("p (s i c) -> p s i c", s=3, i=NB)
        h1r = at(arB, 4608, NB * D).rearrange("p (i c) -> p i c", i=NB)
        hout = at(arC, 5632, 5 * 512).rearrange("p (s w c) -> p s w c", s=5, w=4)
        xg = at(arC, 0, 4 * 2 * TW).rearrange("p (s h c) -> p s h c", s=4, h=2)
        xgT = at(arC, 1280, 2 * CAP).rearrange("p (s c) -> p s c", s=2)
        actT = at(arC, 1792, 2 * FT * CAP).rearrange("p (s k c) -> p s k c", s=2, k=FT)
        eo = at(arC, 3328, 4 * 2 * D).rearrange("p (s h c) -> p s h c", s=4, h=2)
        lm = at(arC, 4352, 256).rearrange("p (b h c) -> p b h c", b=2, h=2)
        lp = at(arC, 4608, 256).rearrange("p (b h c) -> p b h c", b=2, h=2)

        _small = {}

        def tiny(name, words, rows=P, dt=F32):
            a = sb(name, [rows, words], dt)
            return a[:, :]

        projb = at(arC, 7400, D)
        xseq = at(arC, 5632, L, B, I32)
        fp = at(arC, 6144, D)
        fpc = at(arC, 6272, D)
        fq = at(arC, 6400, D, 2 * V)
        fqc = at(arC, 6528, D, 2 * V)
        fm = tiny("fm", 4)
        ft = at(arC, 6656, P + 2 * V)
        stats = tiny("stats", NB * 6).rearrange("p (i c) -> p i c", i=NB)
        mv = tiny("mv", NB * 2).rearrange("p (i c) -> p i c", i=NB)
        cnt = tiny("cnt", 20)
        lnv = tiny("lnv", NB)
        invs = tiny("invs", NB)
        s1 = tiny("s1", KR)
        sT = tiny("sT", P, KR)
        absent = tiny("absent", KR, P, BF16)
        maskT = tiny("maskT", P, KR, BF16)
        mx = tiny("mx", 4 * B).rearrange("p (j b) -> p j b", j=4)
        mxl = tiny("mxl", 4 * B).rearrange("p (j b) -> p j b", j=4)
        negm = tiny("negm", 4 * KR, P, BF16).rearrange("p (j k) -> p j k", j=4)
        nm = tiny("nm", HD, KR, BF16)
        ivr = tiny("ivr", 2 * NB).rearrange("p (s i) -> p s i", s=2)
        ivp = tiny("ivp", 3 * NB, P, BF16).rearrange("p (s i) -> p s i", s=3)
        wsh = at(arC, 7528, NB * KR // 2, P, BF16).rearrange("p (i k) -> p i k", i=NB)
        lsh = tiny("lsh", NB * P, KR, BF16).rearrange("p (i r) -> p i r", i=NB)
        mq = tiny("mq", 3 * KR, P, BF16).rearrange("p (s k) -> p s k", s=3)
        mqT = tiny("mqT", 2 * P, KR, BF16).rearrange("p (s r) -> p s r", s=2)
        zq = tiny("zq", 2 * H).rearrange("p (s h) -> p s h", s=2)
        rq = tiny("rq", 2 * H).rearrange("p (s h) -> p s h", s=2)
        sc = tiny("sc", NB)

        rz = tiny("rz", 4 * B).rearrange("p (b j) -> p b j", b=B)
        rstd = tiny("rstd", NB)
        nbias = tiny("nbias", NB)
        pr = tiny("pr", 20 * E).rearrange("p (i e) -> p i e", i=20)
        px = at(arC, 5632, 20 * E).rearrange("p (i e) -> p i e", i=20)
        pmx = tiny("pmx", NB)
        psm = tiny("psm", NB)
        cand = tiny("cand", 1, P, I32)
        delta = tiny("delta", 1, P, I32)
        bits = tiny("bits", BITS, P, I32)
        part = tiny("part", 1)
        need = tiny("need", 1)
        dtn = tiny("dtn", 2 * E, E)
        onesf = tiny("onesf", P, E)
        tn = tiny("tn", 2 * E)
        ge = at(arC, 1280, NB * E, P, BF16).rearrange("p (i c) -> p i c", i=NB)
        cq = tiny("cq", E, P, BF16)
        bx = tiny("bx", E)
        vtok = tiny("vtok", NTT)
        g0 = tiny("g0", NTT + 2, P, BF16)
        gd = tiny("gd", NTT + 2, P, BF16)
        sr = tiny("sr", 4)
        sv = tiny("sv", 4)
        vi = tiny("vi", 4, P, I32)
        offi = tiny("offi", 4, P, I32)
        idi = tiny("idi", 4, P, I32)
        seg = tiny("seg", 4, P, I32)
        rowi = tiny("rowi", 2 * E, P, U32)
        toki = tiny("toki", 2 * E, P, U32)

        ps = ctx.enter_context(nc.psum_tensor("ps", [P, 8, 512], F32))
        dtab = nc.dram_tensor("factors", (P + 2 * V, 3, CW), BF16, kind="Internal").ap()
        table = nc.dram_tensor("rows", (B * NT * V, TW), F32, kind="Internal").ap()

        in_x, in_c, in_p, in_w, in_r = (sem(n) for n in ("in_x", "in_c", "in_p", "in_w", "in_r"))
        s_ohn, s_stft, s_sq, s_msq, s_mag, s_enc, s_fc, s_tr, s_ft, s_proj = (
            sem(n) for n in ("s_ohn", "s_stft", "s_sq", "s_msq", "s_mag", "s_enc", "s_fc", "s_tr", "s_ft", "s_proj"))
        s_hi, s_r, s_mid, s_lo = (sem(n) for n in ("s_hi", "s_r", "s_mid", "s_lo"))
        s_dtab, s_rb = [sem(f"s_dtab{g}") for g in range(3)], [sem(f"s_rb{g}") for g in range(3)]
        s_wvo, s_wvoc, s_pad, h_m = (sem(n) for n in ("s_wvo", "s_wvoc", "s_pad", "h_m"))
        s_xkey, s_kb, s_oh = (sem(n) for n in ("s_xkey", "s_kb", "s_oh"))
        s_h0m, s_h0, s_var, s_invs, s_s1, s_sTm, s_sT, s_bcm, s_bc = (
            sem(n) for n in ("s_h0m", "s_h0", "s_var", "s_invs", "s_s1", "s_sTm", "s_sT", "s_bcm", "s_bc"))
        s_kt, s_ktu, s_negm, s_shm, s_sh = (sem(n) for n in ("s_kt", "s_ktu", "s_negm", "s_shm", "s_sh"))
        q_x, q_mx, q_mt, q_mc, q_sh, q_e, q_r, q_n, q_t, q_c, q_cl = (
            sem(n) for n in ("q_x", "q_mx", "q_mt", "q_mc", "q_sh", "q_e", "q_r", "q_n", "q_t", "q_c", "q_cl"))
        k_k, k_u, k_e, k_uc, k_cc, k_em, k_m, k_mc, k_o, k_oc, k_zero = (
            sem(n) for n in ("k_k", "k_u", "k_e", "k_uc", "k_cc", "k_em", "k_m", "k_mc", "k_o", "k_oc", "k_zero"))
        l_v, l_s, l_n, l_h, l_v2, l_s2, l_n2, l_x = (
            sem(n) for n in ("l_v", "l_s", "l_n", "l_h", "l_v2", "l_s2", "l_n2", "l_x"))
        r_t, r_c, r_l, r_sub, r_exp, r_p, r_bt, r_b, r_tab, r_wd = (
            sem(n) for n in ("r_t", "r_c", "r_l", "r_sub", "r_exp", "r_p", "r_bt", "r_b", "r_tab", "r_wd"))
        b_part, b_tot, b_init = (sem(n) for n in ("b_part", "b_tot", "b_init"))
        x_p, x_p2, x_m, x_c = sem("x_p"), sem("x_p2"), sem("x_m"), sem("x_c")
        x_d = [sem(f"x_d{i}") for i in range(5)]
        t_d, t_m, t_ge, t_x, t_eq, t_gt, t_s, t_rk, t_sel, t_pin, t_bx, t_bc, t_df, t_pd, t_st, t_g = (
            sem(n) for n in ("t_d", "t_m", "t_ge", "t_x", "t_eq", "t_gt", "t_s", "t_rk", "t_sel", "t_pin", "t_bx",
                             "t_bc", "t_df", "t_pd", "t_st", "t_g"))
        m_sl, m_ls, m_t, m_tc, m_up, m_si, m_dn, m_eo, m_one = (
            sem(n) for n in ("m_sl", "m_ls", "m_t", "m_tc", "m_up", "m_si", "m_dn", "m_eo", "m_one"))
        g_x = [sem(f"g_x{i}") for i in range(4)]
        g_s = [sem(f"g_s{i}") for i in range(2)]
        s_dve, s_act, s_pool = sem("s_dve"), sem("s_act"), sem("s_pool")

        VP = ((0, 3), (3, 3), (6, 2))
        PROJ = {0: 0, 2: 1, 3: 2, 4: 3}

        def tab(q):
            return tabp if q == 0 else tabq

        def rest(q):
            return tabx if q == 0 else tabxq

        def full(q, c):
            if c == 1:
                return fp if q == 0 else fq
            return ps[0:P if q == 0 else 2 * V, 4 * q + PROJ[c], :]
        TILES4 = [(4 * k, min(4, NB - 4 * k)) for k in range(5)]
        block = ctx.enter_context(nc.Block())

        @block.sync
        def _(sp):
            sp.dma_start(xfrm[:, :], A["x_frames"]).then_inc(in_x, 16)
            sp.dma_start(cf[:, :], A["const_f32"]).then_inc(in_x, 16)
            sp.dma_start(cb[:, :], A["const_bf16"]).then_inc(in_c, 16)
            sp.dma_start(wv, A["w_v"].rearrange("(j p) c -> p j c", p=P)).then_inc(in_w, 16)
            sp.dma_start(wo[:, :, :], A["w_out_t"].rearrange("(j p) c -> p j c", p=P)).then_inc(in_w, 16)
            sp.dma_start(xseq, A["x_seq"]).then_inc(in_c, 16)
            sp.dma_start(projw, A["proj_w"]).then_inc(in_p, 16)
            sp.dma_start(projb, A["proj_b"].partition_broadcast(P)).then_inc(in_p, 16)
            sp.dma_start(fq[V:2 * V, :], A["emb"]).then_inc(in_p, 16)
            sp.dma_start(wall[:, 0:2 * HD], A["w_kq_t"]).then_inc(in_p, 16)
            sp.dma_start(gcol[:, :], A["norm_gamma"]).then_inc(in_p, 16)
            sp.dma_start(xtok[:, :], A["x_tokens"]).then_inc(in_r, 16)
            sp.dma_start(ogam[:, :], A["out_gamma"].partition_broadcast(P)).then_inc(in_r, 16)
            sp.wait_ge(k_zero, 2)
            sp.dma_start(wrt[:, 0:E], A["w_router"]).then_inc(in_r, 16)
            sp.dma_start(brt[:, :], A["b_router"].partition_broadcast(P)).then_inc(in_r, 16)
            for k in range(FT):
                n = min(P, FF - k * P)
                sp.dma_start(bup[0:n, k, :], A["b_up_t"][k * P:k * P + n, :]).then_inc(in_r, 16)
            for g, (lo_, hi_) in enumerate(GROUPS):
                c = slice(lo_, hi_)
                sp.wait_ge(s_lo, (4, 6, 10)[g])
                sp.dma_start(dtab[0:P, :, c], tabp[:, :, c]).then_inc(s_dtab[g], 16)
                sp.dma_start(dtab[P:P + 2 * V, :, c], tabq[:, :, c]).then_inc(s_dtab[g], 16)
            sp.wait_ge(s_dtab[0], 32)
            sp.wait_ge(s_dtab[1], 32)
            sp.wait_ge(s_dtab[2], 32)
            for g, (lo_, hi_) in enumerate(GROUPS):
                c = slice(lo_, hi_)
                for q in range(3):
                    r0 = 3 * V + q * TM
                    sp.dma_start(rb[q * V:(q + 1) * V, :, c],
                                 dtab[P + V:P + 2 * V, q, c].unsqueeze(1).broadcast_to([V, NB, hi_ - lo_]))\
                      .then_inc(s_rb[g], 16)
                    sp.dma_start(rb[r0:r0 + TM, 0:B, c],
                                 dtab[0:P, q, c].rearrange("(b t) c -> t b c", t=TM)).then_inc(s_rb[g], 16)
                    sp.dma_start(rb[r0:r0 + TM, B:NB, c],
                                 dtab[P:P + B, q, c].rearrange("(g t) c -> t g c", t=TM)).then_inc(s_rb[g], 16)
            sp.wait_ge(h_m, 5)
            sp.dma_start(wup, A["w_up"].rearrange("g h f -> h g f")).then_inc(r_wd, 16)
            for k in range(FT):
                n = min(P, FF - k * P)
                sp.dma_start(wdn[0:n, :, k, :], A["w_down"][:, k * P:k * P + n, :].rearrange("e f h -> f e h"))\
                  .then_inc(r_wd, 16)
            sp.dma_start(wdn[FL:FL + 1, :, FT - 1, :], A["b_down"].rearrange("(a e) h -> a e h", a=1))\
              .then_inc(r_wd, 16)
            sp.wait_ge(r_p, 1)
            rows = table.rearrange("(b r) c -> b r c", b=B)
            for col, src in ((slice(0, D), xn), (slice(D, TW), pr)):
                sp.dma_start(rows[:, 0:P, col].rearrange("b r c -> r b c"), src[:, 0:B, :]).then_inc(r_tab, 16)
                for g in range(2):
                    sp.dma_start(rows[8 * g:8 * g + 8, P:P + V, col], src[:, B + g, :]).then_inc(r_tab, 16)
            for b in range(B):
                sp.wait_ge(x_c, b + 1)
                sp.dma_start(out[b * L:(b + 1) * L, :].rearrange("(w q) c -> q w c", q=P), hout[:, b % 5])\
                  .then_inc(x_d[b % 5], 16)

        @block.gpsimd
        def _(pool):
            nc.gpsimd.memset(xkey, 0.0).then_inc(k_zero, 1)
            nc.gpsimd.memset(wrt[:, E:P], 0.0).then_inc(k_zero, 1)
            for a in (s1, absent, mq, negm, wsh):
                nc.gpsimd.memset(a, 0.0).then_inc(s_pad, 1)
            nc.gpsimd.memset(ohl[:, :, 0:LAST0 - 3 * P], 0.0).then_inc(s_pad, 1)
            nc.gpsimd.memset(cnt[:, NB:20], 0.0).then_inc(b_init, 1)
            nc.gpsimd.memset(pr[:, NB:20, :], 0.0).then_inc(b_init, 1)
            for k in range(BITS):
                nc.gpsimd.memset(bits[:, k:k + 1], 1 << k).then_inc(b_init, 1)
            nc.gpsimd.memset(cand, 1 << (BITS - 1)).then_inc(b_init, 1)
            nc.gpsimd.memset(onesf, 1.0).then_inc(b_init, 1)
            for i in range(NB):
                pool.wait_ge(q_e, i + 1)
                pool.wait_ge(q_r, i + 1)
                if i >= 2:
                    pool.wait_ge(q_t, i - 1)
                nc.gpsimd.tensor_tensor(qn[:, i % 2, :].rearrange("p (h d) -> p h d", h=H),
                                        eq_[:, i % 3, :].rearrange("p (h d) -> p h d", h=H),
                                        rq[:, i % 2, :].unsqueeze(2).broadcast_to([P, H, DH]),
                                        ALU.mult).then_inc(q_n, 1)
            pool.wait_ge(q_t, NB)
            for n in range(-2, B):
                m, i = n + 2, B + n + 2 if n < 0 else n
                u = (2 + m if n < 0 else n % 2)
                if n >= 2:
                    pool.wait_ge(k_m, n - 1)
                nc.gpsimd.tensor_copy(uu[:, u, :, D], cnt[:, i:i + 1].broadcast_to([P, H])).then_inc(k_cc, 1)
                if n >= 0:
                    pool.wait_ge(k_e, n // 8 + 1)
                    nc.gpsimd.tensor_scalar(ekm[:, n % 2, :], ekl[:, n // 8, :], cfv("lastsel")[:, n % 8:n % 8 + 1],
                                            None, ALU.mult).then_inc(k_em, 1)
            pool.wait_ge(r_tab, 6 * 16)
            for n in range(-3, E):
                e = n + 3
                if e < E:
                    pool.wait_ge(m_ls, e // 2 + 1)
                    if e >= 4:
                        pool.wait_ge(m_t, e - 3)
                        pool.wait_ge(m_eo, e - 3)
                    for h in range(2):
                        pool.indirect_dma_start(
                            xg[:, e % 4, h, :], None, table,
                            bass.IndirectOffsetOnAxis(ap=rowi[:, 2 * e + h:2 * e + h + 1], axis=0))\
                            .then_inc(g_x[e % 4], 16)
                if n >= 0:
                    if n == 0:
                        for b in range(5):
                            pool.wait_ge(x_d[b], 16 * len(range(b, B, 5)))
                    pool.wait_ge(m_eo, n + 1)
                    if n >= 1:
                        pool.wait_ge(g_s[(n - 1) % 2], 32 * ((n - 1) // 2 + 1))
                    for h in range(2):
                        pool.indirect_dma_start(
                            out, bass.IndirectOffsetOnAxis(ap=toki[:, 2 * n + h:2 * n + h + 1], axis=0),
                            eo[:, n % 4, h, :], None, compute_op=ALU.add).then_inc(g_s[n % 2], 16)
            for k in range(2):
                pool.wait_ge(g_s[k], 32 * (E // 2))

        @block.tensor
        def _(pe):
            mm, tp = nc.tensor.matmul, nc.tensor.transpose
            bank16 = lambda k: ps[:, k, :].bitcast(BF16)
            pe.wait_ge(in_c, 32)
            pe.wait_ge(s_ohn, 1)
            dftab, dftc = cbv("dftab"), cbv("dftc")
            ohp = ohn.rearrange("p (v o) k -> p o v k", o=2)
            for c, (v0, nv) in enumerate(VP):
                for r in range(2):
                    w = slice(r * DH, (r + 1) * DH)
                    for o in range(2):
                        d = ps[o * DH:(o + 1) * DH, 2 * c + r, 0:nv * B * NT].rearrange("p (v k) -> p v k", v=nv)
                        mm(d, dftab[:, w], ohp[:, o, v0:v0 + nv, :], start=True, stop=False)
                        last = mm(d, dftc[:, w], ohp[:, o, v0:v0 + nv, :], start=False, stop=True)
                    last.then_inc(s_stft, 1)
            pe.wait_ge(in_w, 32)
            for h in range(H):
                r = slice((h % 2) * DH, (h % 2 + 1) * DH)
                last = mm(ps[:, 6 + h % 2, (h // 2) * D:(h // 2 + 1) * D], wv[r, h // 2, :], wo[r, h // 2, :],
                          start=True, stop=True)
            last.then_inc(s_wvo, 1)
            pe.wait_ge(s_mag, 1)
            pe.wait_ge(in_p, 5 * 16)
            for bank, lo_, n in ((4, 0, P), (5, P, V)):
                for v in range(V // 2):
                    last = mm(ps[0:n, bank, 0:D], mag[:, v, lo_:lo_ + n], projw[:, v, :],
                              start=v == 0, stop=v == V // 2 - 1)
                last.then_inc(s_enc, 1)
            pe.wait_ge(s_fc, 2)
            tp(ps[:, 6, 0:P], fpc, ident)
            tp(ps[:, 6, P:P + 2 * V], fqc, ident[0:2 * V, 0:2 * V]).then_inc(s_tr, 1)
            pe.wait_ge(s_ft, 1)
            for c in range(4):
                for q in range(2):
                    mm(ps[0:P if q == 0 else 2 * V, 4 * q + c, :], ft[:, 0:P] if q == 0 else ft[:, P:P + 2 * V],
                       wall[:, c * HD:(c + 1) * HD], start=True, stop=True).then_inc(s_proj, 1)
            pe.wait_ge(s_xkey, 1)
            pe.wait_ge(s_r, 10)
            for b in range(B):
                if b >= 2:
                    pe.wait_ge(s_oh, b - 1)
                mm(ps[:, 6 + b % 2, :], identb[:, b:b + 1].broadcast_to([P, P]), xkey, start=True,
                   stop=True).then_inc(s_kb, 1)

            def expand(o, i, lo_, hi_, stop=True):
                return mm(o, sel, rb[:, i, lo_:hi_], start=True, stop=stop)

            def h0_rows():
                for k, (i0, n) in enumerate(TILES4):
                    for i in range(n):
                        last = expand(ps[:, k, i * P:(i + 1) * P], i0 + i, HC, HC + D)
                    last.then_inc(h_m, 1)

            pe.wait_ge(s_rb[0], 9 * 16)
            for k, (i0, n) in enumerate(TILES4):
                for i in range(n):
                    last = expand(ps[:, k, i * P:(i + 1) * P], i0 + i, HC, HC + D)
                last.then_inc(s_h0m, 1)
            pe.wait_ge(s_s1, 2)
            pe.wait_ge(s_oh, B)
            tp(ps[0:KR, 5, 0:P], s1, ident)
            tp(bank16(6)[0:KR, 0:P], absent, identb).then_inc(s_sTm, 1)
            pe.wait_ge(s_sT, 2)
            for k, (i0, n) in enumerate(TILES4):
                for i in range(n):
                    last = mm(ps[:, k, i * P:(i + 1) * P], ident[0:KR, i0 + i:i0 + i + 1].broadcast_to([KR, P]),
                              sT[:, :], start=True, stop=True)
                last.then_inc(s_bcm, 1)
            for i in range(NB):
                if i >= 3:
                    pe.wait_ge(s_ktu, i - 2)
                for j in range(4):
                    o = ps[:, 5 + i % 3, j * P:(j + 1) * P]
                    mm(o, identb[0:KR, i:i + 1].broadcast_to([KR, P]), maskT, start=True, stop=False)
                    last = mm(o, rb[:, i, KC + j * P:KC + (j + 1) * P], sel, start=False, stop=True)


                last.then_inc(s_kt, 1)
            pe.wait_ge(s_negm, 2)
            pe.wait_ge(s_bc, 5)
            for j in range(4):
                last = tp(bank16(0)[0:KR, j * P:(j + 1) * P], negm[:, j], identb)
            last.then_inc(s_shm, 1)
            for i in range(NB):
                last = tp(bank16(1 + i // 8)[0:KR, (i % 8) * P:(i % 8 + 1) * P], wsh[:, i], identb)
            last.then_inc(s_shm, 1)

            pe.wait_ge(s_sh, 2)
            pe.wait_ge(s_ktu, NB)
            pe.wait_ge(s_rb[1], 9 * 16)
            for n in range(NB + 4):
                if n < NB:
                    if n >= 4:
                        pe.wait_ge(q_e, n - 3)
                    expand(ps[:, 4 + n % 4, :], n, QC, QC + HD).then_inc(q_x, 1)
                i = n - 1
                if 0 <= i < NB:
                    pe.wait_ge(q_mx, i + 1)
                    if i >= 2:
                        pe.wait_ge(q_mc, i - 1)
                    tp(bank16(i % 2)[0:KR, 0:P], mq[:, i % 3, :], identb).then_inc(q_mt, 1)
                i = n - 2
                if 0 <= i < NB:
                    pe.wait_ge(q_mc, i + 1)
                    mm(ps[:, 4 + i % 4, :], mqT[:, i % 2, :], cbv("headsel"), start=False, stop=True,
                       skip_group_check=True).then_inc(q_sh, 1)
                i = n - 4
                if 0 <= i < NB:
                    pe.wait_ge(q_n, i + 1)
                    if 2 <= i:
                        pe.wait_ge(q_c, i - 1)
                    for j in range(4):
                        last = tp(ps[:, 2 + i % 2, j * P:(j + 1) * P], qn[:, i % 2, j * P:(j + 1) * P], ident)
                    last.then_inc(q_t, 1)

            ORDER = [B, B + 1] + list(range(B))

            def kv(n):
                i = ORDER[n]
                if n >= 2:
                    pe.wait_ge(k_e, n - 1)
                bank = 6 * (n % 2)
                expand(ps[:, bank, :], i, KC, KC + HD, stop=False)
                mm(ps[:, bank, :], lsh[:, i, :], nm[:, :], start=False, stop=True).then_inc(k_k, 1)
                if n >= 1:
                    pe.wait_ge(k_uc, n)
                for c in range(2):
                    last = expand(ps[:, 1 + c, :], i, UC + c * HD, UC + (c + 1) * HD)
                last.then_inc(k_u, 1)

            def context(b):
                pe.wait_ge(k_e, b + 3)
                pe.wait_ge(k_uc, b + 3)
                pe.wait_ge(k_cc, b + 3)
                pe.wait_ge(k_em, b + 1)
                if b >= 1:
                    pe.wait_ge(k_mc, b)
                for h in range(H):
                    o, j = h % 2, h // 2
                    d = ps[o * DH:(o + 1) * DH, 3 + j // 2, (j % 2) * (D + 1):(j % 2 + 1) * (D + 1)]
                    c = slice(h * DH, (h + 1) * DH)
                    mm(d, ek[:, b % 2, c], uu[:, b % 2, h, :], start=True, stop=False)
                    last = mm(d, ekm[:, b % 2, c], uu[:, 2 + b // 8, h, :], start=False, stop=True)
                last.then_inc(k_m, 1)

            def rows_out(b):
                g, o, m = b // 8, b % 2, (b % 8) // 2
                q32 = slice(32 * m, 32 * m + 32)
                pe.wait_ge(k_mc, b + 1)
                if b >= 1:
                    pe.wait_ge(k_oc, b)
                for j in range(4):
                    mm(ps[:, 5, 0:P], qt[:, b, j, :], mb[:, b % 2, j, :],
                       start=j == 0, stop=j == 3)
                for j in range(4):
                    last = mm(ps[q32, 7, g * P:(g + 1) * P], qtl[:, g, o, j, q32], mb[:, b % 2, j, :],
                              start=o == 0 and j == 0, stop=o == 1 and j == 3)
                last.then_inc(k_o, 1)

            pe.wait_ge(q_e, NB)
            pe.wait_ge(q_c, B)
            pe.wait_ge(q_cl, 2)
            pe.wait_ge(s_rb[2], 9 * 16)
            kv(0)
            kv(1)
            for n in range(B + 2):
                if n < B:
                    kv(n + 2)
                if 0 <= n - 1 < B:
                    context(n - 1)
                if 0 <= n - 2 < B:
                    rows_out(n - 2)
            pe.wait_ge(k_uc, NB)
            pe.wait_ge(k_mc, B)
            h0_rows()

            pe.wait_ge(in_r, 7 * 16)
            pe.wait_ge(l_x, NB)
            for k, (i0, n) in enumerate(TILES4):
                for i in range(n):
                    last = tp(ps[:, k, i * P:(i + 1) * P], xn[:, i0 + i, :], ident)
                last.then_inc(r_t, 1)
            pe.wait_ge(r_c, 5)
            for i in range(NB):
                mm(ps[:, i // 4, (i % 4) * P:(i % 4 + 1) * P], xnT[:, i * P:(i + 1) * P], wrt[:, :],
                   start=True, stop=True).then_inc(r_l, 1)
            pe.wait_ge(r_p, 1)
            for k in range(5):
                last = tp(ps[:, k // 4, (k % 4) * P:(k % 4 + 1) * P],
                          pr[:, 4 * k:4 * k + 4, :].rearrange("p i e -> p (i e)"), ident)
            last.then_inc(r_bt, 1)
            pe.wait_ge(r_p, 2)
            for k in range(5):
                last = tp(ps[:, 2 + k // 4, (k % 4) * P:(k % 4 + 1) * P],
                          px[:, 4 * k:4 * k + 4, :].rearrange("p i e -> p (i e)"), ident)
            last.then_inc(r_bt, 1)

            def token_rows(b):
                if b == 0:
                    pe.wait_ge(x_p, 2)
                    pe.wait_ge(x_p2, 1)
                if b >= 2:
                    pe.wait_ge(x_c, b - 1)
                for w in range(4):
                    o = ps[:, 6 + b % 2, w * P:(w + 1) * P]
                    for q in range(3):
                        last = mm(o, oh[:, b, w * P:(w + 1) * P], h1p[:, q, b, :], start=q == 0,
                                  stop=q == 2 and w < 3)
                    if w == 3:
                        for q in range(3):
                            last = mm(o, ohl[:, b, :], h1p[:, q, B + b // 8, :], start=False, stop=q == 2)
                last.then_inc(x_m, 1)

            for k in range(BITS + 1):
                pe.wait_ge(b_part, k + 1)
                mm(ps[:, 5, 0:P], cfv("sameexp"), part.broadcast_to([P, P]), start=True, stop=True).then_inc(b_tot, 1)
                if k >= 2 and k % 1 == 0 and k - 2 < B:
                    token_rows(k - 2)
            pe.wait_ge(t_d, 1)
            mm(ps[:, 5, 64:64 + 2 * E], onesf, dtn, start=True, stop=True).then_inc(t_m, 1)
            pe.wait_ge(t_ge, 2)
            pe.wait_ge(x_c, B)
            for t in range(NTT):
                b, w = t // 4, t % 4
                o = ps[:, t // 8, (t % 8) * 2 * E:(t % 8 + 1) * 2 * E]
                last = mm(o, oh[:, b, w * P:(w + 1) * P], ge[:, b, :], start=True, stop=w < 3)
                if w == 3:
                    last = mm(o, ohl[:, b, :], ge[:, B + b // 8, :], start=False, stop=True)
                if t % 8 == 7:
                    last.then_inc(t_x, 1)
            pe.wait_ge(t_s, 1)
            pe.wait_ge(t_gt, 4)
            for k in range(4):
                mm(ps[:, k, :], cbv("notbefore"), eqT[:, k * 512:(k + 1) * 512], start=True, stop=False)
                mm(ps[:, k, :], cbv("onesb"), eqS[:, k * 512:(k + 1) * 512], start=False, stop=True).then_inc(t_rk, 1)
            pe.wait_ge(t_g, 1)
            mm(ps[:, 4, 2 * E:2 * E + NTT + 2], cbv("diff"), g0, start=True, stop=True)
            pe.wait_ge(t_pin, 2)
            mm(ps[:, 4, 0:E], cbv("before"), cq, start=True, stop=True)
            mm(ps[:, 4, E:2 * E], cbv("shift"), cq, start=True, stop=True).then_inc(t_bx, 1)
            for k in range(4):
                mm(ps[:, k, :], cbv("diff"), pin[:, k * 512:(k + 1) * 512], start=True, stop=True).then_inc(t_df, 1)

            def slots(gr):
                if gr >= 1:
                    pe.wait_ge(m_ls, gr)
                pe.wait_ge(t_st, 2 * gr + 2)
                for e in (2 * gr, 2 * gr + 1):
                    for h in range(2):
                        lhs = step[:, e, h * P:(h + 1) * P]
                        c = h * (2 * NTT + 3)
                        mm(ps[:, 6 + e % 2, c:c + NTT + 1], lhs, pd[:, e, 0:NTT + 1], start=True, stop=True)
                        last = mm(ps[:, 6 + e % 2, c + NTT + 1:c + 2 * NTT + 3], lhs, gd, start=True, stop=True)
                last.then_inc(m_sl, 1)

            def gathered(e):
                pe.wait_ge(g_x[e % 4], 32 * (e // 4 + 1))
                if e >= 2:
                    pe.wait_ge(m_tc, e - 1)
                for h in range(2):
                    last = tp(ps[:, 5 * (e % 2), h * P:(h + 1) * P], xg[:, e % 4, h, 0:D], ident)
                last.then_inc(m_t, 1)

            def up(e):
                pe.wait_ge(m_tc, e + 1)
                for k in range(FT):
                    n = min(P, FF - k * P)
                    if e >= 1:
                        pe.wait_ge(m_si, FT * (e - 1) + k + 1)
                    mm(ps[0:n, 1 + k, 0:CAP], wup[:, e // GS, k * P:k * P + n],
                       xgT[:, e % 2, :], start=True, stop=True).then_inc(m_up, 1)

            def down(e):
                pe.wait_ge(m_si, FT * (e + 1))
                if e >= 1:
                    pe.wait_ge(m_eo, e)
                for h in range(2):
                    for k in range(FT):
                        n = P if k < FT - 1 else FL + 1
                        last = mm(ps[:, 4, h * P:(h + 1) * P],
                                  actT[0:n, e % 2, k, h * P:(h + 1) * P], wdn[0:n, e, k, :],
                                  start=k == 0, stop=k == FT - 1)
                last.then_inc(m_dn, 1)

            pe.wait_ge(t_bc, 3)
            pe.wait_ge(t_pd, 4)
            pe.wait_ge(r_wd, 5 * 16)
            pe.wait_ge(m_one, 1)
            slots(0)
            slots(1)
            gathered(0)
            gathered(1)
            up(0)
            for e in range(E):
                gr = 2 if e == 0 else e // 2 + 3
                if (e == 0 or e % 2 == 1) and gr < E // 2:
                    slots(gr)
                if e + 1 < E:
                    up(e + 1)
                down(e)
                if e + 2 < E:
                    gathered(e + 2)

        @block.scalar
        def _(act):
            A_ = nc.scalar.activation
            nact = [0]

            def done(ins):
                nact[0] += 1
                ins.then_inc(s_act, 1)
                act.wait_ge(s_act, nact[0])

            n3 = B * NT
            for c, (v0, nv) in enumerate(VP):
                for r in range(2):
                    act.wait_ge(s_stft, 2 * c + r + 1)
                    A_(sq[:, r, v0 * n3:(v0 + nv) * n3], ps[:, 2 * c + r, 0:nv * n3], ACT.Square).then_inc(s_sq, 1)
            act.wait_ge(s_wvo, 1)
            for c in range(2):
                A_(wall[:, 2 * HD:].rearrange("p (j o c) -> p o j c", j=4, o=2)[:, c],
                   ps[:, 6 + c, :].rearrange("p (j c) -> p j c", j=4), ACT.Copy).then_inc(s_wvoc, 1)

            act.wait_ge(s_msq, 3)
            A_(mag.rearrange("p v k -> p (v k)"), sq[:, 0, :], ACT.Sqrt).then_inc(s_mag, 1)
            act.wait_ge(s_tr, 1)
            act.wait_ge(in_p, 5 * 16)
            A_(ft, ps[:, 6, 0:P + 2 * V], ACT.Copy, scale=gcol[:, 0:1]).then_inc(s_ft, 1)
            for n in range(12):
                if n < 10:
                    c, q = divmod(n, 2)
                    at_, w = CHUNKS[c]
                    if c != 1:
                        act.wait_ge(s_proj, 2 * PROJ[c] + q + 1)
                    A_(tab(q)[:, 0, at_:at_ + w], full(q, c), ACT.Copy).then_inc(s_hi, 1)
                if n >= 2:
                    c, q = divmod(n - 2, 2)
                    at_, w = CHUNKS[c]
                    act.wait_ge(s_r, n - 1)
                    A_(tab(q)[:, 1, at_:at_ + w], rest(q)[:, at_:at_ + w], ACT.Copy).then_inc(s_mid, 1)
            act.wait_ge(s_var, 1)
            A_(invs, lnv, ACT.Sqrt).then_inc(s_invs, 1)
            act.wait_ge(s_sTm, 1)
            A_(sT, ps[0:KR, 5, 0:P], ACT.Copy).then_inc(s_sT, 1)
            A_(maskT, ps[:, 6, :].bitcast(BF16)[0:KR, 0:P], ACT.Copy).then_inc(s_sT, 1)
            for k, (i0, n) in enumerate(TILES4):
                act.wait_ge(s_bcm, k + 1)
                A_(sbc[:, i0:i0 + n, :].rearrange("p i c -> p (i c)"), ps[:, k, 0:n * P], ACT.Copy).then_inc(s_bc, 1)
            act.wait_ge(s_shm, 1)
            A_(nm, ps[:, 0, :].bitcast(BF16)[0:KR, 0:HD], ACT.Copy).then_inc(s_sh, 1)
            act.wait_ge(s_shm, 2)
            for k, n in enumerate((8, 8, 2)):
                ins = A_(lsh[:, 8 * k:8 * k + n, :].rearrange("p i r -> p (i r)"),
                         ps[:, 1 + k, :].bitcast(BF16)[0:KR, 0:n * P], ACT.Copy)
            ins.then_inc(s_sh, 1)
            for n in range(1, NB + 4):
                i = n - 1
                if 0 <= i < NB:
                    act.wait_ge(q_mt, i + 1)
                    if i >= 2:
                        act.wait_ge(q_sh, i - 1)
                    A_(mqT[:, i % 2, :], ps[:, i % 2, :].bitcast(BF16)[0:KR, 0:P], ACT.Copy).then_inc(q_mc, 1)
                i = n - 2
                if 0 <= i < NB:
                    act.wait_ge(q_sh, i + 1)
                    if i >= 3:
                        act.wait_ge(q_n, i - 2)
                    A_(eq_[:, i % 3, :], ps[:, 4 + i % 4, :], ACT.Exp, scale=s1[:, i:i + 1]).then_inc(q_e, 1)
                i = n - 4
                if 0 <= i < B:
                    act.wait_ge(q_t, i + 1)
                    A_(qt[:, i, :, :].rearrange("p j r -> p (j r)"), ps[:, 2 + i % 2, :], ACT.Copy).then_inc(q_c, 1)
            for n in range(-2, B + 2):
                if n < B:
                    i, m = (B + n + 2, n + 2) if n < 0 else (n, n + 2)
                    act.wait_ge(k_k, m + 1)
                    if n >= 2:
                        act.wait_ge(k_m, n - 1)
                    if n == -2:
                        act.wait_ge(q_n, NB)
                        act.wait_ge(q_t, NB)
                        act.wait_ge(q_c, B)
                        act.wait_ge(q_cl, 2)
                    A_(ekl[:, n + 2, :] if n < 0 else ek[:, n % 2, :], ps[:, 6 * (m % 2), :], ACT.Exp,
                       scale=s1[:, i:i + 1]).then_inc(k_e, 1)
                    act.wait_ge(k_u, m + 1)
                    A_(uu[:, m if n < 0 else n % 2][:, :, 0:D] if False else uu[:, 2 + m if n < 0 else n % 2, :, 0:D],
                       ps[:, 1:3, :].rearrange("p b (h c) -> p (b h) c", c=D), ACT.Copy,
                       scale=sc[:, i:i + 1]).then_inc(k_uc, 1)
                b = n - 2
                if 0 <= b < B:
                    act.wait_ge(k_o, b + 1)
                    A_(qt[:, b, 0, :], ps[:, 5, 0:P], ACT.Copy).then_inc(k_oc, 1)
            for g in range(2):
                A_(qtl[:, g, 0, 0, :], ps[:, 7, g * P:(g + 1) * P], ACT.Copy).then_inc(k_oc, 1)
            act.wait_ge(l_v, 1)
            A_(rstd, lnv, ACT.Sqrt).then_inc(l_s, 1)
            act.wait_ge(l_v2, 1)
            A_(rstd, lnv, ACT.Sqrt).then_inc(l_s2, 1)
            act.wait_ge(l_n2, 1)
            for i in range(NB):
                A_(xn[:, i, :], h1[:, i, :], ACT.Identity, bias=nbias[:, i:i + 1], scale=rstd[:, i:i + 1])\
                    .then_inc(l_x, 1)
            for k, (i0, n) in enumerate(TILES4):
                act.wait_ge(r_t, k + 1)
                A_(xnT[:, i0 * P:(i0 + n) * P], ps[:, k, 0:n * P], ACT.Copy).then_inc(r_c, 1)
            act.wait_ge(r_sub, 1)
            A_(pr[:, 0:NB, :], px[:, 0:NB, :], ACT.Exp).then_inc(r_exp, 1)
            act.wait_ge(r_bt, 1)
            A_(pbis[:, 0:512], ps[:, 0, :], ACT.Copy)
            A_(pbis[:, 512:640], ps[:, 1, 0:P], ACT.Copy).then_inc(r_b, 1)
            act.wait_ge(r_bt, 2)
            A_(wbis[:, 0:512], ps[:, 2, :], ACT.Copy)
            A_(wbis[:, 512:640], ps[:, 3, 0:P], ACT.Copy).then_inc(r_b, 1)
            done(A_(h1p[:, 0], h1, ACT.Copy))
            act.wait_ge(x_p, 1)
            A_(h1p[:, 1], h1r, ACT.Copy).then_inc(x_p2, 1)
            for b in range(B):
                act.wait_ge(x_m, b + 1)
                if b >= 5:
                    act.wait_ge(x_d[b % 5], 16 * (b // 5))
                A_(hout[:, b % 5].rearrange("p w c -> p (w c)"), ps[:, 6 + b % 2, :], ACT.Copy).then_inc(x_c, 1)
            act.wait_ge(t_m, 1)
            act.wait_ge(r_tab, 6 * 16)
            for k in range(1, 8, 2):
                act.wait_ge(t_x, k + 1)
                for c, o in ((0, eqT), (E, gtT)):
                    ins = A_(o.rearrange("p (e t) -> p t e", e=E)[:, 8 * k:8 * k + 8, :],
                             ps[:, k, :].rearrange("p (t c) -> p t c", t=8)[:, :, c:c + E], ACT.Copy)
                ins.then_inc(t_gt, 1)
            for k in range(4):
                act.wait_ge(t_df, k + 1)
                A_(pd[:, 8 * k:8 * k + 8, 0:NTT], ps[:, k, :].rearrange("p (e t) -> p e t", e=8), ACT.Copy)\
                    .then_inc(t_pd, 1)
            for e in range(-1, E):
                if e + 1 < E:
                    n = e + 1
                    act.wait_ge(m_t, n + 1)
                    if n >= 2:
                        act.wait_ge(m_up, FT * (n - 1))
                    A_(xgT[:, n % 2, :], ps[:, 5 * (n % 2), 0:CAP], ACT.Copy).then_inc(m_tc, 1)
                    if n >= 2:
                        act.wait_ge(m_dn, n - 1)
                    if n == 0:
                        act.wait_ge(m_one, 1)
                    for k in range(FT):
                        r = min(P, FF - k * P)
                        act.wait_ge(m_up, FT * n + k + 1)
                        A_(actT[0:r, n % 2, k, :], ps[0:r, 1 + k, 0:CAP], ACT.Silu,
                           bias=bup[0:r, k, n // GS:n // GS + 1]).then_inc(m_si, 1)

        @block.vector
        def _(dve):
            vec = nc.vector
            ndve = [0]

            def done(ins):
                nonlocal_ = ndve
                nonlocal_[0] += 1
                ins.then_inc(s_dve, 1)
                dve.wait_ge(s_dve, nonlocal_[0])

            dve.wait_ge(in_x, 32)
            vec.tensor_tensor(ohn, xfrm[:, :].unsqueeze(1).broadcast_to([P, V, B * NT]),
                              cfv("ids").unsqueeze(2).broadcast_to([P, V, B * NT]), ALU.is_equal).then_inc(s_ohn, 1)
            dve.wait_ge(in_c, 32)
            dve.wait_ge(k_zero, 2)
            vec.tensor_tensor(xkey[0:B], xseq, cfv("frame16"), ALU.add).then_inc(s_xkey, 1)
            for c, (v0, nv) in enumerate(VP):
                dve.wait_ge(s_sq, 2 * c + 2)
                at_, n = v0 * B * NT, nv * B * NT
                vec.scalar_tensor_tensor(out=sq[:, 0, at_:at_ + n], in0=sq[:, 0, at_:at_ + n], scalar=1e-34,
                                         in1=sq[:, 1, at_:at_ + n], op0=ALU.max, op1=ALU.add).then_inc(s_msq, 1)
            dve.wait_ge(s_enc, 2)
            dve.wait_ge(in_p, 5 * 16)
            vec.tensor_tensor(fp, ps[:, 4, 0:D], projb, ALU.add)
            done(vec.tensor_tensor(fq[0:V], ps[0:V, 5, 0:D], projb[0:V], ALU.add))
            vec.tensor_reduce(fm[:, 0:1], fp, AX.X, ALU.add)
            done(vec.tensor_reduce(fm[0:2 * V, 1:2], fq, AX.X, ALU.add))
            done(vec.tensor_scalar(fm[:, 2:3], fm[:, 0:1], -1.0 / D, None, ALU.mult))
            done(vec.tensor_scalar(fm[0:2 * V, 3:4], fm[0:2 * V, 1:2], -1.0 / D, None, ALU.mult))
            vec.tensor_scalar(fpc, fp, fm[:, 2:3], None, ALU.add).then_inc(s_fc, 1)
            vec.tensor_scalar(fqc, fq, fm[0:2 * V, 3:4], None, ALU.add).then_inc(s_fc, 1)
            for n in range(12):
                if n < 10:
                    c, q = divmod(n, 2)
                    at_, w = CHUNKS[c]
                    dve.wait_ge(s_hi, n + 1)
                    vec.tensor_tensor(rest(q)[:, at_:at_ + w], full(q, c), tab(q)[:, 0, at_:at_ + w],
                                      ALU.subtract).then_inc(s_r, 1)
                if n >= 2:
                    c, q = divmod(n - 2, 2)
                    at_, w = CHUNKS[c]
                    dve.wait_ge(s_mid, n - 1)
                    vec.tensor_tensor(tab(q)[:, 2, at_:at_ + w], rest(q)[:, at_:at_ + w], tab(q)[:, 1, at_:at_ + w],
                                      ALU.subtract).then_inc(s_lo, 1)
            dve.wait_ge(s_pad, 6)
            for b in range(B):
                dve.wait_ge(s_kb, b + 1)
                vec.tensor_scalar(oh[:, b, :], ps[:, 6 + b % 2, :], cfv("pidx"), 0.0, ALU.is_equal, ALU.add,
                                  accum_out=cnt[:, b:b + 1])
                vec.tensor_scalar(ohl[:, b, LAST0 - 3 * P:P], ps[:, 6 + b % 2, LAST0:L], cfv("lastid"),
                                  cfv("lastb")[:, b:b + 1], ALU.is_equal, ALU.mult).then_inc(s_oh, 1)
            dve.wait_ge(s_oh, B)
            for g in range(2):
                ins = vec.tensor_reduce(cnt[:, B + g:B + g + 1], ohl[:, 8 * g:8 * g + 8, LAST0 - 3 * P:P], AX.XY,
                                        ALU.add)
            done(ins)
            vec.tensor_scalar(absent[:, 0:NB], cnt[:, 0:NB], 0.5, -1e30, ALU.is_lt, ALU.mult).then_inc(s_s1, 1)

            def variances(rows, eps_of):
                for i in range(NB):
                    ins = vec.bn_stats(stats[:, i, :], rows(i))
                done(ins)
                for i in range(NB):
                    ins = vec.bn_aggr(mv[:, i, :], stats[:, i, :])
                done(ins)
                return vec.tensor_scalar(lnv, mv[:, :, 1], eps_of[0], eps_of[1], ALU.mult, ALU.add)

            dve.wait_ge(s_h0m, 5)
            h0ps = lambda i: ps[:, i // 4, (i % 4) * P:(i % 4 + 1) * P]
            variances(h0ps, (1.0 + EPS, EPS * EPS)).then_inc(s_var, 1)
            dve.wait_ge(s_invs, 1)
            done(vec.reciprocal(s1[:, 0:NB], invs))
            vec.tensor_copy(ivp[:, 0, :], invs).then_inc(s_s1, 1)
            done(vec.tensor_tensor(sc, s1[:, 0:NB], cnt[:, 0:NB], ALU.mult))
            done(vec.tensor_tensor(ivr[:, 0, :], invs, ivp[:, 0, :], ALU.subtract))
            done(vec.tensor_copy(ivp[:, 1, :], ivr[:, 0, :]))
            done(vec.tensor_tensor(ivp[:, 2, :], ivr[:, 0, :], ivp[:, 1, :], ALU.subtract))
            for q in range(3):
                ins = vec.tensor_tensor(wsh[:, :, q * B:(q + 1) * B], cbv("rowb").rearrange("p (i b) -> p i b", i=NB),
                                        ivp[:, q, :].unsqueeze(2).broadcast_to([P, NB, B]), ALU.mult)
            ins.then_inc(s_negm, 1)

            dve.wait_ge(s_bc, 5)
            for i in range(NB):
                dve.wait_ge(s_kt, i + 1)
                ins = vec.tensor_tensor(prod[:, i % 2], ps[:, 5 + i % 3, :].rearrange("p (j r) -> p j r", j=4),
                                        sbc[:, i, :].unsqueeze(1).broadcast_to([P, 4, P]), ALU.mult)
                ins.then_inc(s_ktu, 1)
                dve.wait_ge(s_ktu, i + 1)
                if i < B:
                    vec.tensor_reduce(mx[:, :, i:i + 1], prod[:, i % 2], AX.X, ALU.max)
                else:
                    ins = vec.tensor_reduce(mxl[:, :, 8 * (i - B):8 * (i - B) + 8],
                                            prod[:, i % 2].rearrange("p j (b v) -> p j b v", b=8), AX.X, ALU.max)
            done(ins)
            done(vec.tensor_tensor(mx, mx, mxl, ALU.max))
            for q in range(3):
                ins = vec.tensor_scalar(negm[:, :, q * B:(q + 1) * B], mx, -1.0, None, ALU.mult)
            ins.then_inc(s_negm, 1)
            for n in range(NB + 5):
                if n < NB:
                    dve.wait_ge(q_x, n + 1)
                    if n >= 3:
                        dve.wait_ge(q_mt, n - 2)
                    vec.tensor_reduce(mq[:, n % 3, 0:H], ps[:, 4 + n % 4, :].rearrange("p (h d) -> p h d", h=H), AX.X,
                                      ALU.max, negate=True).then_inc(q_mx, 1)
                i = n - 3
                if 0 <= i < NB:
                    dve.wait_ge(q_e, i + 1)
                    if i >= 2:
                        dve.wait_ge(q_n, i - 1)
                    done(vec.tensor_reduce(zq[:, i % 2, :], eq_[:, i % 3, :].rearrange("p (h d) -> p h d", h=H),
                                           AX.X, ALU.add))
                    vec.reciprocal(rq[:, i % 2, :], zq[:, i % 2, :]).then_inc(q_r, 1)
                i = n - 5
                if B <= i < NB:
                    dve.wait_ge(q_t, i + 1)
                    for o in range(2):
                        ins = vec.tensor_tensor(
                            qtl[:, i - B, o], ps[:, 2 + i % 2, :].rearrange("p (j r) -> p j r", j=4),
                            cfv("parrow")[:, o * P:(o + 1) * P].unsqueeze(1).broadcast_to([P, 4, P]), ALU.mult)
                    ins.then_inc(q_cl, 1)
            for b in range(B):
                dve.wait_ge(k_m, b + 1)
                if b >= 2:
                    dve.wait_ge(k_o, b - 1)
                z = ps[:, 3:5, 0:2 * (D + 1)].rearrange("p k (j c) -> p k j c", j=2)
                jj = lambda a: a.rearrange("p (k j) -> p k j", k=2)
                done(vec.reciprocal(jj(rz[:, b, :]), z[:, :, :, D]))
                done(vec.tensor_scalar(rz[:, b, :], rz[:, b, :], DH ** -0.5, None, ALU.mult))
                vec.tensor_tensor(mb[:, b % 2].rearrange("p (k j) c -> p k j c", k=2), z[:, :, :, 0:D],
                                  jj(rz[:, b, :]).unsqueeze(3).broadcast_to([P, 2, 2, D]), ALU.mult).then_inc(k_mc, 1)
            dve.wait_ge(k_oc, NB)
            dve.wait_ge(h_m, 5)
            ao = lambda i: qt[:, i, 0, :] if i < B else qtl[:, i - B, 0, 0, :]
            variances(ao, (1.0, EPS)).then_inc(l_v, 1)
            dve.wait_ge(l_s, 1)
            done(vec.reciprocal(rstd, rstd))
            done(vec.scalar_tensor_tensor(out=nbias, in0=mv[:, :, 0], scalar=-1.0, in1=rstd, op0=ALU.mult,
                                          op1=ALU.mult))
            for i in range(NB):
                ins = vec.tensor_scalar(h1[:, i, :], ao(i), rstd[:, i:i + 1], nbias[:, i:i + 1], ALU.mult, ALU.add)
            done(ins)
            done(vec.tensor_tensor(h1, h1, ogam[:, :].unsqueeze(1).broadcast_to([P, NB, D]), ALU.mult))
            for k, (i0, n) in enumerate(TILES4):
                ins = vec.tensor_tensor(h1[:, i0:i0 + n, :], h1[:, i0:i0 + n, :],
                                        ps[:, k, 0:n * P].rearrange("p (i c) -> p i c", i=n), ALU.add)
            done(ins)
            variances(lambda i: h1[:, i, :], (1.0, EPS)).then_inc(l_v2, 1)
            dve.wait_ge(l_s2, 1)
            done(vec.reciprocal(rstd, rstd))
            vec.scalar_tensor_tensor(out=nbias, in0=mv[:, :, 0], scalar=-1.0, in1=rstd, op0=ALU.mult,
                                     op1=ALU.mult).then_inc(l_n2, 1)
            dve.wait_ge(r_l, NB)
            vec.tensor_tensor(px[:, 0:B, :].rearrange("p (k i) e -> p k i e", k=4),
                              ps[:, 0:4, :].rearrange("p k (i c) -> p k i c", i=4)[:, :, :, 0:E],
                              brt[:, :].unsqueeze(1).unsqueeze(1).broadcast_to([P, 4, 4, E]), ALU.add)
            done(vec.tensor_tensor(px[:, B:NB, :], ps[:, 4, 0:2 * P].rearrange("p (i c) -> p i c", i=2)[:, :, 0:E],
                                   brt[:, :].unsqueeze(1).broadcast_to([P, 2, E]), ALU.add))
            done(vec.tensor_reduce(pmx, px[:, 0:NB, :], AX.X, ALU.max))
            vec.tensor_tensor(px[:, 0:NB, :], px[:, 0:NB, :], pmx.unsqueeze(2).broadcast_to([P, NB, E]),
                              ALU.subtract).then_inc(r_sub, 1)
            dve.wait_ge(r_exp, 1)
            done(vec.tensor_reduce(psm, pr[:, 0:NB, :], AX.X, ALU.add))
            done(vec.reciprocal(psm, psm))
            dve.wait_ge(b_init, 34)
            vec.tensor_tensor(pr[:, 0:NB, :], pr[:, 0:NB, :], psm.unsqueeze(2).broadcast_to([P, NB, E]),
                              ALU.mult).then_inc(r_p, 1)
            vec.tensor_copy(px, cnt.unsqueeze(2).broadcast_to([P, 20, E])).then_inc(r_p, 1)
            dve.wait_ge(r_b, 2)
            cf_ = cand.bitcast(F32)

            def count(op):
                vec.scalar_tensor_tensor(out=junk, in0=pbis, scalar=cf_, in1=wbis, op0=op, op1=ALU.mult,
                                         accum_out=part).then_inc(b_part, 1)

            for k in range(BITS):
                bit = BITS - 1 - k
                count(ALU.is_ge)
                if k == 0:
                    dve.wait_ge(s_act, 1)
                    done(vec.tensor_tensor(h1r, h1, h1p[:, 0], ALU.subtract))
                    vec.tensor_copy(sv[:, 0:1], h1r[:, 0, 0:1]).then_inc(x_p, 1)
                if k == 1:
                    dve.wait_ge(x_p2, 1)
                    vec.tensor_tensor(h1p[:, 2], h1r, h1p[:, 1], ALU.subtract).then_inc(x_p, 1)
                dve.wait_ge(b_tot, k + 1)
                done(vec.tensor_scalar(delta, ps[:, 5, 0:1], CAP - 0.5, float(1 << bit), ALU.is_lt, ALU.mult))
                if bit > 0:
                    done(vec.scalar_tensor_tensor(out=cand, in0=cand, scalar=delta, in1=bits[:, bit - 1:bit],
                                                  op0=ALU.bitwise_xor, op1=ALU.bitwise_xor))
                else:
                    done(vec.tensor_tensor(cand, cand, delta, ALU.bitwise_xor))
            count(ALU.is_gt)
            dve.wait_ge(b_tot, BITS + 1)
            done(vec.tensor_scalar(need, ps[:, 5, 0:1], -1.0, float(CAP), ALU.mult, ALU.add))
            vec.tensor_scalar(dtn[:, 0:E], cfv("eyeexp")[0:E], cf_[0:E], None, ALU.mult)
            vec.tensor_scalar(dtn[:, E:2 * E], cfv("eyeexp")[0:E], need[0:E], None, ALU.mult).then_inc(t_d, 1)
            dve.wait_ge(t_m, 1)
            done(vec.tensor_copy(tn, ps[:, 5, 64:64 + 2 * E]))
            for q, op in ((0, ALU.is_equal), (1, ALU.is_gt)):
                vec.tensor_tensor(ge[:, :, q * E:(q + 1) * E], pr[:, 0:NB, :],
                                  tn[:, 0:E].unsqueeze(1).broadcast_to([P, NB, E]), op).then_inc(t_ge, 1)
            done(vec.tensor_tensor(vtok, xtok[:, :], cfv("tau16"), ALU.add))
            vec.tensor_tensor(g0[:, 0:NTT - 1], vtok[:, 1:NTT], vtok[:, 0:NTT - 1], ALU.subtract)
            vec.memset(g0[:, NTT - 1:NTT], 0.0)
            vec.tensor_copy(g0[:, NTT:NTT + 1], vtok[:, 0:1])
            vec.tensor_copy(g0[:, NTT + 1:NTT + 2], cfv("pidx")).then_inc(t_g, 1)
            vec.memset(actT[64:P, :, FT - 1, :], 1.0).then_inc(m_one, 1)
            dve.wait_ge(r_tab, 6 * 16)
            for k in range(0, 8, 2):
                dve.wait_ge(t_x, k + 1)
                for c, o in ((0, eqT), (E, gtT)):
                    ins = vec.tensor_copy(o.rearrange("p (e t) -> p t e", e=E)[:, 8 * k:8 * k + 8, :],
                                          ps[:, k, :].rearrange("p (t c) -> p t c", t=8)[:, :, c:c + E])
                ins.then_inc(t_eq, 1)
            dve.wait_ge(t_eq, 4)
            dve.wait_ge(t_gt, 4)
            vec.tensor_tensor_scan(eqS, cbv("carry"), eqT, 0.0, ALU.mult, ALU.add).then_inc(t_s, 1)
            dve.wait_ge(t_s, 1)
            for k in range(4):
                c = slice(k * 512, (k + 1) * 512)
                dve.wait_ge(t_rk, k + 1)
                done(vec.tensor_tensor(pin[:, c].rearrange("p (e t) -> p e t", e=8),
                                       ps[:, k, :].rearrange("p (e t) -> p e t", e=8),
                                       tn[:, E + 8 * k:E + 8 * k + 8].unsqueeze(2).broadcast_to([P, 8, NTT]),
                                       ALU.is_lt))
                done(vec.tensor_tensor(eqT[:, c], pin[:, c], eqT[:, c], ALU.mult))
                done(vec.tensor_tensor(gtT[:, c], eqT[:, c], gtT[:, c], ALU.add))
            done(vec.tensor_tensor_scan(pin, cbv("carry"), gtT, 0.0, ALU.mult, ALU.add))
            vec.tensor_copy(cq, pin.rearrange("p (e t) -> p e t", e=E)[:, :, NTT - 1]).then_inc(t_pin, 2)
            dve.wait_ge(t_bx, 1)
            vec.tensor_copy(bx, ps[:, 4, 0:E]).then_inc(t_bc, 1)
            vec.tensor_copy(pd[:, :, NTT], ps[:, 4, E:2 * E]).then_inc(t_bc, 1)
            vec.tensor_copy(gd, ps[:, 4, 2 * E:2 * E + NTT + 2]).then_inc(t_bc, 1)
            dve.wait_ge(t_bc, 3)
            for e in range(E):
                vec.tensor_scalar(step[:, e, :], cbv("slots"), bx[:, e:e + 1], None, ALU.is_ge).then_inc(t_st, 1)

            def listed(gr):
                v = ps[:, 6:8, 0:2 * (2 * NTT + 3)].rearrange("p b (h c) -> p b h c", h=2)
                as3 = lambda a: a.rearrange("p (b h) -> p b h", b=2)
                dve.wait_ge(m_sl, gr + 1)
                done(vec.tensor_tensor(as3(sr), cfv("slot").unsqueeze(1).broadcast_to([P, 2, 2]), v[:, :, :, NTT],
                                       ALU.subtract))
                done(vec.tensor_tensor(lm, v[:, :, :, 0:NTT],
                                       as3(sr).unsqueeze(3).broadcast_to([P, 2, 2, NTT]), ALU.is_le))
                done(vec.tensor_tensor(lp, lm, v[:, :, :, NTT + 1:2 * NTT + 1], ALU.mult))
                done(vec.tensor_reduce(sv, lp.rearrange("p b h c -> p (b h) c"), AX.X, ALU.add))
                done(vec.tensor_tensor(as3(vi), as3(sv), v[:, :, :, 2 * NTT + 1], ALU.add))
                vec.tensor_scalar(offi, vi, 4, None, ALU.arith_shift_right)
                done(vec.tensor_scalar(idi, vi, V - 1, None, ALU.bitwise_and))
                done(vec.tensor_scalar(sv, offi, float(P), None, ALU.mult))
                done(vec.tensor_tensor(as3(sr), as3(sv), v[:, :, :, 2 * NTT + 2], ALU.add))
                vec.tensor_copy(toki[:, 4 * gr:4 * gr + 4], sr)
                done(vec.tensor_scalar(seg, sr, NT / L, 0.5 / L - 0.5 + 0.5 / L, ALU.mult, ALU.add))
                vec.scalar_tensor_tensor(out=rowi[:, 4 * gr:4 * gr + 4], in0=seg, scalar=float(V), in1=idi,
                                         op0=ALU.mult, op1=ALU.add).then_inc(m_ls, 1)

            listed(0)
            listed(1)
            for e in range(E):
                dve.wait_ge(m_dn, e + 1)
                if e >= 4:
                    dve.wait_ge(g_s[e % 2], 32 * (e // 2 - 1))
                for h in range(2):
                    c = h * P
                    ins = vec.tensor_scalar(eo[:, e % 4, h, :], ps[:, 4, c:c + P],
                                            xg[:, e % 4, h, D + e:D + e + 1], None, ALU.mult)
                ins.then_inc(m_eo, 1)
                gr = 2 if e == 0 else e // 2 + 3
                if (e == 0 or e % 2 == 1) and gr < E // 2:
                    listed(gr)



_OUT = "out_dram"


def kernel(**inputs):
    import concourse.bacc as bacc
    from concourse.bass_utils import run_bass_kernel_spmd

    c = np.ascontiguousarray
    x = np.asarray(inputs["x"])
    at = np.arange(NT * NFFT) - NFFT // 2
    at = np.where(at < 0, -at, at)
    at = np.where(at >= L, 2 * (L - 1) - at, at)
    frames = x[:, at].reshape(B, NT, NFFT)
    cols = np.concatenate([frames[:, :TM].reshape(B * TM, NFFT), frames[:, TM]], 0).T
    cf, cb = constants()
    w_qkv, w_out, b_up = (np.asarray(inputs[n]) for n in ("L0_attn_w_qkv", "L0_attn_w_out", "L0_ffn_b_up"))
    zeros = np.zeros((P, P), np.float32)
    proj_w = np.zeros((2, P // 2, V // 2, D), np.float32)
    proj_w[:, :NF, :, DE:] = np.asarray(inputs["L0_tok_proj_w"]).reshape(NF, V // 2, 2, DS).transpose(2, 0, 1, 3)
    arrays = {
        "x_frames"
: c(np.concatenate([cols, cols], 0)),
        "x_seq": c(x),
        "x_tokens": c(x.reshape(NTT, P).T),
        "const_f32": _pack(cf, np.float32),
        "const_bf16": _pack(cb, mybir.dt.np(BF16)),
        "emb": c(np.concatenate([np.asarray(inputs["L0_tok_emb_table"]), zeros[:V, :DS]], 1)),
        "proj_w": proj_w.reshape(P, V // 2, D),
        "proj_b": c(np.concatenate([zeros[0, :DE], np.asarray(inputs["L0_tok_proj_b"])])),
        "norm_gamma": c(np.asarray(inputs["L0_attn_norm_gamma"]).reshape(D, 1)),
        "w_kq_t": c(np.concatenate([w_qkv[HD:2 * HD], w_qkv[:HD]], 0).T),
        "w_v": c(w_qkv[2 * HD:]),
        "w_out_t": c(w_out.T),
        "out_gamma": c(inputs["L0_attn_out_gamma"]),
        "w_router": c(inputs["L0_ffn_W_router"]),
        "b_router": c(inputs["L0_ffn_b_router"]),
        "w_up": c(inputs["L0_ffn_W_up"]),
        "b_up_t": c(b_up.T),
        "w_down": c(inputs["L0_ffn_W_down"]),
        "b_down": c(inputs["L0_ffn_b_down"]),
    }
    nc = bacc.Bacc("TRN2", target_bir_lowering=False, num_devices=1)
    args = {n: nc.dram_tensor(f"in_{n}", a.shape, mybir.dt.from_np(a.dtype), kind="ExternalInput").ap()
            for n, a in arrays.items()}
    out = nc.dram_tensor(_OUT, (B * L, D), F32, kind="ExternalOutput").ap()
    program(nc, args, out)
    r = run_bass_kernel_spmd(nc, [{f"in_{n}": a for n, a in arrays.items()}], core_ids=[0])
    return r.results[0][_OUT].reshape(B, L, D)
```

```python
from contextlib import ExitStack

import concourse.bass as bass
from concourse import mybir
import numpy as np

ALU = mybir.AluOpType
ACT = mybir.ActivationFunctionType
AX = mybir.AxisListType
F32 = mybir.dt.float32
BF16 = mybir.dt.bfloat16
I32 = mybir.dt.int32
U32 = mybir.dt.uint32

P = 128
B, L, V = 16, 512, 16
NFFT, HOP = 64, 64
NT = L // HOP + 1
NF = NFFT // 2 + 1
D, DE = 128, 89
DS = D - DE
H, DH = 8, 64
HD = H * DH
E, GS = 32, 4
NG = E // GS
FF = 341
FT = (FF + P - 1) // P
FL = FF - (FT - 1) * P
CAP = B * L // E
EPS = 1e-5
TM = NT - 1
NB = B + B // 8
NTT = B * L // P
UW = H * D
KC, HC, QC, UC = 0, HD, HD + D, 2 * HD + D
CW = 2 * HD + D + UW
KR = 3 * V + 3 * TM
GROUPS = ((HC, QC), (KC, HC), (QC, UC), (UC, CW))
BITS = 30
ROUNDS = BITS // 2
TW = D + E
LAST0 = -(-L * TM // NT)


def _split3(a):
    bf = mybir.dt.np(BF16)
    hi = a.astype(bf)
    r = a - hi.astype(np.float64)
    mid = r.astype(bf)
    lo = (r - mid.astype(np.float64)).astype(bf)
    return hi.astype(np.float64), mid.astype(np.float64), lo.astype(np.float64)


def constants():
    p = np.arange(P)
    n = np.arange(NFFT)
    f = np.arange(NF)
    win = 0.5 - 0.5 * np.cos(2 * np.pi * n / NFFT)
    ang = 2 * np.pi * np.outer(n, f) / NFFT
    dft = np.concatenate([win[:, None] * np.cos(ang), -win[:, None] * np.sin(ang)], 1)
    wide = np.zeros((NFFT, 2, P // 2))
    wide[:, :, :NF] = dft.reshape(NFFT, 2, NF)
    hi, mid, lo = _split3(wide.reshape(NFFT, P))
    eye = np.eye(P)
    cf = {
        "ident": eye,
        "frame16": np.tile(16.0 * (np.arange(L) * NT // L), (B, 1)),
        "sameexp": (p[:, None] % E == p[None, :] % E) * 1.0,
        "eyeexp": (p[:, None] == np.arange(E)[None, :]) * 1.0,
        "pidx": p[:, None] * 1.0,
        "lastid": (P + p[:, None] % V) * 1.0,
        "lastb": (np.arange(B)[None, :] % 8 == p[:, None] // V) * 1.0,
        "lastsel": (np.arange(8)[None, :] == p[:, None] // V) * 1.0,
        "parity": np.stack([p // V % 2 == 0, p // V % 2 == 1], 1) * 1.0,
        "slot": np.stack([p, p + P], 1) * 1.0,
        "ids": np.tile(np.arange(V), (P, 1)) * 1.0,
        "tau16": np.tile(16.0 * np.arange(NTT), (P, 1)),
    }
    cb = {
        "dftab": np.concatenate([hi, mid], 0),
        "dftc": np.concatenate([lo, 0 * lo], 0),
        "sel": np.concatenate([np.repeat(np.arange(V)[:, None] == p[None, :] % V, 3, 0),
                               np.repeat(np.arange(TM)[:, None] == p[None, :] // V, 3, 0),
                               np.ones((1, P))], 0) * 1.0,
        "identb": eye,
        "before": (p[:, None] < p[None, :]) * 1.0,
        "notbefore": -1.0 * (p[:, None] >= p[None, :]),
        "onesb": np.ones((P, P)),
        "diff": eye * 1.0 - (p[:, None] == p[None, :] - 1),
        "shift": (p[:, None] == p[None, :] - 1) * 1.0,
        "slots": np.tile(np.arange(CAP), (P, 1)) * 1.0,
        "carry": np.tile(np.arange(NTT) > 0, (P, E)) * 1.0,
        "rowb": np.stack([np.tile(np.arange(B) == i, (P, 1)) if i < B else
                          np.arange(B)[None, :] == 8 * (i - B) + p[:, None] // V for i in range(NB)], 1) * 1.0,
    }
    return cf, cb


def _layout(tables):
    at, where = 0, {}
    for name, a in tables.items():
        w = int(np.prod(a.shape[1:]))
        where[name] = (a.shape[0], at, w)
        at += w
    return where, at


def _pack(tables, dtype):
    where, width = _layout(tables)
    out = np.zeros((P, width), dtype)
    for name, a in tables.items():
        r, at, w = where[name]
        out[:r, at:at + w] = a.reshape(r, w).astype(dtype)
    return out


def program(nc, A, out):
    cfw, cfn = _layout(constants()[0])
    cbw, cbn = _layout(constants()[1])
    with ExitStack() as ctx:
        def sb(name, shape, dt=F32):
            return ctx.enter_context(nc.sbuf_tensor(name, shape, dt))

        def sem(name):
            return ctx.enter_context(nc.semaphore(name))

        cf = sb("cf", [P, cfn])
        cb = sb("cb", [P, cbn], BF16)

        def cfv(name):
            r, at, w = cfw[name]
            return cf[0:r, at:at + w]

        def cbv(name):
            r, at, w = cbw[name]
            return cb[0:r, at:at + w]

        ident, identb = cfv("ident"), cbv("identb")
        sel, sel1 = cbv("sel")[0:KR], cbv("sel")
        xfrm = sb("xfrm", [P, B * NT], I32)
        xtok = sb("xtok", [P, NTT], I32)
        gcol = sb("gcol", [P, 1])
        ogam = sb("ogam", [P, D])
        wrt = sb("wrt", [P, P])
        brt = sb("brt", [P, E])
        bup = sb("bup", [P, FT, NG])
        wo = sb("wo", [P, 4, D])
        oh = sb("oh", [P, B, L], BF16)
        ohl = sb("ohl", [P, B, P], BF16)

        arA = sb("arA", [P, NB * CW // 2])
        rb1 = arA[0:KR + 1, :].bitcast(BF16).rearrange("p (i c) -> p i c", i=NB)
        rb = rb1[0:KR]
        WD = E * FT * D
        wdn = arA[:, 0:WD].rearrange("p (e k h) -> p e k h", e=E, k=FT)
        h1 = arA[:, WD:WD + NB * D].rearrange("p (i c) -> p i c", i=NB)
        wup = arA[:, WD + NB * D:WD + NB * D + NG * FF].rearrange("p (g f) -> p g f", g=NG)

        BW = B * HD + 2 * 2 * HD
        arB = sb("arB", [P, BW])

        def at(arena, start, words, rows=P, dt=F32):
            v = arena[0:rows, start:start + words]
            return v if dt == F32 else v.bitcast(dt)

        ohn = at(arB, 0, 1152, P, BF16).rearrange("p (v k) -> p v k", v=V)
        sq = at(arB, 1152, 2304).rearrange("p (r c) -> p r c", r=2)
        mag = at(arB, 3456, 1152).rearrange("p (v k) -> p v k", v=V // 2)
        wall = at(arB, 4608, 2 * HD + UW)
        wv = at(arB, 6656, 4 * D).rearrange("p (j c) -> p j c", j=4)
        projw = at(arB, 7168, V // 2 * D).rearrange("p (v c) -> p v c", v=V // 2)
        xkey = at(arB, 8192, L // 2, B, BF16)
        xseq = at(arB, 8448, L, B, I32)
        pick = at(arB, 8960, (NB * (KR + 1) + 1) // 2, KR, BF16)[:, 0:NB * (KR + 1)].rearrange("k (i m) -> k i m", i=NB)
        tabp = at(arB, 0, 3 * CW // 2, P, BF16).rearrange("p (s c) -> p s c", s=3)
        tabq = at(arB, 3264, 3 * HD // 2, P, BF16).rearrange("p (s c) -> p s c", s=3)
        tabh = at(arB, 4032, 3 * D // 2, 2 * V, BF16).rearrange("p (s c) -> p s c", s=3)
        ao = at(arB, 2304, NB * D).rearrange("p (i c) -> p i c", i=NB)
        qt = at(arB, 4608, 4 * HD).rearrange("p (s j r) -> p s j r", s=4, j=4)
        qtl = at(arB, 6656, 2 * HD).rearrange("p (g j r) -> p g j r", g=2, j=4)
        eq_ = at(arB, 7680, 2 * HD).rearrange("p (s c) -> p s c", s=2)
        qn = at(arB, 8704, 2 * HD).rearrange("p (s c) -> p s c", s=2)
        xn = at(arB, 0, NB * D).rearrange("p (i c) -> p i c", i=NB)
        xnT = at(arB, 6912, NB * P)
        SW = E * NTT // 2
        eqT = at(arB, 0, SW, P, BF16)
        gtT = at(arB, SW, SW, P, BF16)
        eqS = at(arB, 2 * SW, SW, P, BF16)
        pin = at(arB, 3 * SW, SW, P, BF16)
        PDW = E * (NTT + 2) // 2
        pd = at(arB, 4 * SW, PDW, P, BF16).rearrange("p (e t) -> p e t", e=E)
        step = at(arB, 4 * SW + PDW, E * CAP // 2, P, BF16).rearrange("p (e s) -> p e s", e=E)

        arC = sb("arC", [P, 4096 + 4 * H * (D + 1)])
        keyb = at(arC, 0, B * L // 2, P, BF16).rearrange("p (b t) -> p b t", b=B)
        ring = at(arC, 4096, 4 * HD).rearrange("p (s c) -> p s c", s=4)
        sels = at(arC, 0, NB * P // 2, KR + 1, BF16).rearrange("p (i r) -> p i r", i=NB)
        ek = at(arC, 0, 2 * HD).rearrange("p (s c) -> p s c", s=2)
        ekl = at(arC, 1024, 2 * HD).rearrange("p (s c) -> p s c", s=2)
        ekm = at(arC, 2048, 2 * HD).rearrange("p (s c) -> p s c", s=2)
        mb = at(arC, 3072, 2 * HD).rearrange("p (s j c) -> p s j c", s=2, j=4)
        uu = at(arC, 4096, 4 * H * (D + 1)).rearrange("p (s h c) -> p s h c", s=4, h=H)
        BC = NB * P // 4
        pbis = at(arC, 0, BC)
        wbis = at(arC, 640, BC)
        junk = [at(*w, BC // 2, P, BF16) for w in ((arC, 1280), (arC, 1568), (arB, 9472))]
        h1p = at(arC, 1920, 3 * NB * D // 2, P, BF16).rearrange("p (s i c) -> p s i c", s=3, i=NB)
        h1r = at(arB, 4608, NB * D).rearrange("p (i c) -> p i c", i=NB)
        hout = at(arC, 5632, 5 * 512).rearrange("p (s w c) -> p s w c", s=5, w=4)
        xg = at(arC, 0, 4 * 2 * TW).rearrange("p (s h c) -> p s h c", s=4, h=2)
        xgT = at(arC, 1280, 2 * CAP).rearrange("p (s c) -> p s c", s=2)
        actT = at(arC, 1792, 2 * FT * CAP).rearrange("p (s k c) -> p s k c", s=2, k=FT)
        eo = at(arC, 3328, 4 * 2 * D).rearrange("p (s h c) -> p s h c", s=4, h=2)
        lm = at(arC, 4352, 256).rearrange("p (b h c) -> p b h c", b=2, h=2)
        lp = at(arC, 4608, 256).rearrange("p (b h c) -> p b h c", b=2, h=2)

        def tiny(name, words, rows=P, dt=F32):
            a = sb(name, [rows, words], dt)
            return a[:, :]

        projb = at(arC, 7400, D)
        fp = at(arC, 6144, D)
        fpc = at(arC, 6272, D)
        fq = at(arC, 6400, D, 2 * V)
        fqc = at(arC, 6528, D, 2 * V)
        fm = tiny("fm", 4)
        ft = at(arC, 6656, P + 2 * V)
        stats = tiny("stats", NB * 6).rearrange("p (i c) -> p i c", i=NB)
        mv = tiny("mv", NB * 2).rearrange("p (i c) -> p i c", i=NB)
        cnt = tiny("cnt", NB)
        lnv = tiny("lnv", NB)
        invs = tiny("invs", NB)
        s1 = tiny("s1", KR)
        absent = tiny("absent", KR, P, BF16)
        sT = tiny("sT", P, KR, BF16)
        mx = tiny("mx", 4 * B).rearrange("p (j b) -> p j b", j=4)
        mxl = tiny("mxl", 4 * B).rearrange("p (j b) -> p j b", j=4)
        negm = tiny("negm", 4 * KR, P, BF16).rearrange("p (j k) -> p j k", j=4)
        nm = tiny("nm", HD, KR, BF16)
        ivr = tiny("ivr", 2 * NB).rearrange("p (s i) -> p s i", s=2)
        ivp = tiny("ivp", 3 * NB, P, BF16).rearrange("p (s i) -> p s i", s=3)
        wsh = at(arC, 7528, NB * KR // 2, P, BF16).rearrange("p (i k) -> p i k", i=NB)
        lsh = tiny("lsh", NB * P, KR, BF16).rearrange("p (i r) -> p i r", i=NB)
        qm = tiny("qm", 2 * H).rearrange("p (s h) -> p s h", s=2)
        zq = tiny("zq", 2 * H).rearrange("p (s h) -> p s h", s=2)
        rq = tiny("rq", 2 * H).rearrange("p (s h) -> p s h", s=2)
        sc = tiny("sc", NB)
        rz = tiny("rz", 4 * B).rearrange("p (b j) -> p b j", b=B)
        rstd = tiny("rstd", NB)
        rstd2 = tiny("rstd2", NB)
        lnv2 = tiny("lnv2", NB)
        stats2 = tiny("stats2", NB * 6).rearrange("p (i c) -> p i c", i=NB)
        mv2 = tiny("mv2", NB * 2).rearrange("p (i c) -> p i c", i=NB)
        wm = tiny("wm", 2 * H)
        digit = tiny("digit", 1)
        dum, dum2, dum3 = tiny("dum", 1), tiny("dum2", 1), tiny("dum3", 1)
        nbias = tiny("nbias", NB)
        pr = tiny("pr", NB * E).rearrange("p (i e) -> p i e", i=NB)
        px = at(arC, 5632, NB * E).rearrange("p (i e) -> p i e", i=NB)
        pmx = tiny("pmx", NB)
        psm = tiny("psm", NB)
        cand = tiny("cand", 3, P, I32)
        base = tiny("base", 3, P, I32)
        delta = tiny("delta", 1, P, I32)
        steps3 = tiny("steps3", 3 * ROUNDS, P, I32).rearrange("p (r j) -> p r j", j=3)
        passed = tiny("passed", 3)
        part = tiny("part", 3)
        need = tiny("need", 1)
        dtn = tiny("dtn", 2 * E, E)
        onesf = tiny("onesf", P, E)
        tn = tiny("tn", 2 * E)
        ge = at(arC, 1280, NB * E, P, BF16).rearrange("p (i c) -> p i c", i=NB)
        cq = tiny("cq", E, P, BF16)
        bx = tiny("bx", E)
        vtok = tiny("vtok", NTT)
        g0 = tiny("g0", NTT + 2, P, BF16)
        gd = tiny("gd", NTT + 2, P, BF16)
        sr = tiny("sr", 4)
        sv = tiny("sv", 4)
        vi = tiny("vi", 4, P, I32)
        offi = tiny("offi", 4, P, I32)
        idi = tiny("idi", 4, P, I32)
        seg = tiny("seg", 4, P, I32)
        rowi = tiny("rowi", 2 * E, P, U32)
        toki = tiny("toki", 2 * E, P, U32)

        ps = ctx.enter_context(nc.psum_tensor("ps", [P, 8, 512], F32))
        dtab = nc.dram_tensor("factors", (P + 2 * V, 3, CW), BF16, kind="Internal").ap()
        drows = dtab.rearrange("r q c -> (r q) c")
        dkey = nc.dram_tensor("keys", (B, L), BF16, kind="Internal").ap()
        table = nc.dram_tensor("rows", (B * NT * V, TW), F32, kind="Internal").ap()

        loaded_frames, loaded_dft, loaded_ids, loaded_tables, loaded_proj = (
            sem(n) for n in ("loaded_frames", "loaded_dft", "loaded_ids", "loaded_tables", "loaded_proj"))
        loaded_w_vo, loaded_router = (
            sem(n) for n in ("loaded_w_vo", "loaded_router"))
        ids_onehot, spectra_ready, squares_ready, power_ready, mag_ready = (
            sem(n) for n in ("ids_onehot", "spectra_ready", "squares_ready", "power_ready", "mag_ready"))
        enc_ready, factors_centred, factors_turned, factors_t_ready, factor_products = (
            sem(n) for n in ("enc_ready", "factors_centred", "factors_turned", "factors_t_ready", "factor_products"))
        part1_ready, rest_ready, part2_ready, part3_ready = (
            sem(n) for n in ("part1_ready", "rest_ready", "part2_ready", "part3_ready"))
        tables_in_dram = [sem(f"tables_in_dram{g}") for g in range(4)]
        rb_ready = [sem(f"rb_ready{g}") for g in range(4)]
        w_vo_ready, w_vo_centred, padding_zero, h0_again = (
            sem(n) for n in ("w_vo_ready", "w_vo_centred", "padding_zero", "h0_again"))
        loaded_tokens = sem("loaded_tokens")
        keys_ready, keys_in_dram, onehots_ready = (
            sem(n) for n in ("keys_ready", "keys_in_dram", "onehots_ready"))
        last_onehots = sem("last_onehots")
        keys_spread = [sem(f"keys_spread{g}") for g in range(2)]
        h0_ready, h0_var, s_ready, inv_s_ready, scales_turned = (
            sem(n) for n in ("h0_ready", "h0_var", "s_ready", "inv_s_ready", "scales_turned"))
        scales_t_ready, scales_spread, scaled_sel_ready = (
            sem(n) for n in ("scales_t_ready", "scales_spread", "scaled_sel_ready"))
        kt_ready, kt_used, neg_max_ready, shift_turned, shift_ready = (
            sem(n) for n in ("kt_ready", "kt_used", "neg_max_ready", "shift_turned", "shift_ready"))
        q_ready, q_shifted, q_exp_ready, q_sum_ready, q_probs_ready = (
            sem(n) for n in ("q_ready", "q_shifted", "q_exp_ready", "q_sum_ready", "q_probs_ready"))
        qt_turned, qt_ready = (
            sem(n) for n in ("qt_turned", "qt_ready"))
        k_ready, u_ready, k_exp_ready, u_scaled, counts_placed = (
            sem(n) for n in ("k_ready", "u_ready", "k_exp_ready", "u_scaled", "counts_placed"))
        k_last_ready, context_ready, context_scaled, rows_ready, rows_taken = (
            sem(n) for n in ("k_last_ready", "context_ready", "context_scaled", "rows_ready", "rows_taken"))
        wrt_zero = sem("wrt_zero")
        att_var, att_std, h1_ready, h1_var, h1_std = (
            sem(n) for n in ("att_var", "att_std", "h1_ready", "h1_var", "h1_std"))
        ln2_factors, xn_ready = (
            sem(n) for n in ("ln2_factors", "xn_ready"))
        weights_spread = sem("weights_spread")
        xn_turned, xnt_ready, logits_ready, logits_shifted, logits_exp = (
            sem(n) for n in ("xn_turned", "xnt_ready", "logits_ready", "logits_shifted", "logits_exp"))
        probs_ready, pairs_turned, pairs_ready, table_written, experts_loaded = (
            sem(n) for n in ("probs_ready", "pairs_turned", "pairs_ready", "table_written", "experts_loaded"))
        partial_counts, total_counts, search_consts = (
            sem(n) for n in ("partial_counts", "total_counts", "search_consts"))
        h1_rest_ready, h1_part2_ready, token_rows_ready, token_rows_copied = (
            sem(n) for n in ("h1_rest_ready", "h1_part2_ready", "token_rows_ready", "token_rows_copied"))
        token_rows_written = [sem(f"token_rows_written{i}") for i in range(5)]
        thresholds_diag, thresholds_spread, row_marks, token_marks, eq_ready = (
            sem(n) for n in ("thresholds_diag", "thresholds_spread", "row_marks", "token_marks", "eq_ready"))
        gt_ready, eq_summed, rank_ready, places_ready, blocks_ready = (
            sem(n) for n in ("gt_ready", "eq_summed", "rank_ready", "places_ready", "blocks_ready"))
        blocks_copied, place_diffs, pd_ready, steps_ready, token_diffs = (
            sem(n) for n in ("blocks_copied", "place_diffs", "pd_ready", "steps_ready", "token_diffs"))
        slots_ready, slots_listed, rows_turned, xgt_ready, up_ready = (
            sem(n) for n in ("slots_ready", "slots_listed", "rows_turned", "xgt_ready", "up_ready"))
        hidden_ready, down_ready, eo_ready, ones_ready = (
            sem(n) for n in ("hidden_ready", "down_ready", "eo_ready", "ones_ready"))
        rows_gathered = [sem(f"rows_gathered{i}") for i in range(4)]
        rows_scattered = [sem(f"rows_scattered{i}") for i in range(2)]
        dve_step, h1_part1_ready = (
            sem(n) for n in ("dve_step", "h1_part1_ready"))

        VP = ((0, 3), (3, 3), (6, 2))
        ITEMS = ((fp, tabp[:, :, HC:HC + D], 0), (fq, tabh, 0), (ps[:, 0, :], tabp[:, :, KC:KC + HD], 1),
                 (ps[:, 4, :], tabq, 2), (ps[:, 1, :], tabp[:, :, QC:QC + HD], 3),
                 (ps[:, 2, :], tabp[:, :, UC:UC + HD], 4), (ps[:, 3, :], tabp[:, :, UC + HD:CW], 5))

        def rest(n):
            return ring[0:ITEMS[n][0].shape[0], n % 4, 0:ITEMS[n][0].shape[1]]

        TILES4 = [(4 * k, min(4, NB - 4 * k)) for k in range(5)]
        block = ctx.enter_context(nc.Block())

        @block.sync
        def _(sp):
            sp.dma_start(xfrm[:, :], A["x_frames"]).then_inc(loaded_frames, 16)
            sp.dma_start(cf[:, :], A["const_f32"]).then_inc(loaded_frames, 16)
            ndft = 2 * P
            sp.dma_start(cb[:, 0:ndft], A["const_bf16"][:, 0:ndft]).then_inc(loaded_dft, 16)
            sp.dma_start(xseq, A["x_seq"]).then_inc(loaded_ids, 16)
            sp.dma_start(wv, A["w_v"].rearrange("(j p) c -> p j c", p=P)).then_inc(loaded_w_vo, 16)
            sp.dma_start(wo[:, :, :], A["w_out_t"].rearrange("(j p) c -> p j c", p=P)).then_inc(loaded_w_vo, 16)
            sp.dma_start(projw, A["proj_w"]).then_inc(loaded_proj, 16)
            sp.dma_start(projb, A["proj_b"].partition_broadcast(P)).then_inc(loaded_proj, 16)
            sp.dma_start(fq[V:2 * V, :], A["emb"]).then_inc(loaded_proj, 16)
            sp.dma_start(wall[:, 0:2 * HD], A["w_kq_t"]).then_inc(loaded_proj, 16)
            sp.dma_start(gcol[:, :], A["norm_gamma"]).then_inc(loaded_proj, 16)
            sp.dma_start(cb[:, ndft:cbn], A["const_bf16"][:, ndft:cbn]).then_inc(loaded_tables, 16)
            sp.dma_start(pick, A["pick"].rearrange("k (i m) -> k i m", i=NB)).then_inc(loaded_tables, 16)
            sp.dma_start(rb1[KR:KR + 1, :, KC:KC + HD], A["ones"].unsqueeze(1).broadcast_to([1, NB, HD]))\
              .then_inc(loaded_tables, 16)
            sp.dma_start(xtok[:, :], A["x_tokens"]).then_inc(loaded_tokens, 16)
            sp.dma_start(ogam[:, :], A["out_gamma"].partition_broadcast(P)).then_inc(loaded_router, 16)
            sp.wait_ge(wrt_zero, 1)
            sp.dma_start(wrt[:, 0:E], A["w_router"]).then_inc(loaded_router, 16)
            sp.dma_start(brt[:, :], A["b_router"].partition_broadcast(P)).then_inc(loaded_router, 16)
            for k in range(FT):
                n = min(P, FF - k * P)
                sp.dma_start(bup[0:n, k, :], A["b_up_t"][k * P:k * P + n, :]).then_inc(loaded_router, 16)
            def write_tables(g):
                c = slice(*GROUPS[g])
                sp.dma_start(dtab[0:P, :, c], tabp[:, :, c]).then_inc(tables_in_dram[g], 16)
                for k in ((), (0,), (1,), (2, 3))[g]:
                    at_ = (KC, QC, UC, UC + HD)[k]
                    sp.dma_start(dtab[P:P + 2 * V, :, at_:at_ + HD], tabq[32 * k:32 * k + 2 * V])\
                        .then_inc(tables_in_dram[g], 16)
                if g == 0:
                    sp.dma_start(dtab[P:P + 2 * V, :, HC:HC + D], tabh).then_inc(tables_in_dram[g], 16)

            def read_tables(g):
                c, w = slice(*GROUPS[g]), GROUPS[g][1] - GROUPS[g][0]
                sp.wait_ge(tables_in_dram[g], (2, 2, 2, 3)[g] * 16)
                sp.dma_start(rb[0:3 * V, :, c], drows[3 * (P + V):3 * (P + 2 * V), c].unsqueeze(1)
                             .broadcast_to([3 * V, NB, w])).then_inc(rb_ready[g], 16)
                sp.dma_start(rb[3 * V:KR, 0:B, c],
                             drows[0:3 * P, c].rearrange("(b k) c -> k b c", b=B)).then_inc(rb_ready[g], 16)
                sp.dma_start(rb[3 * V:KR, B:NB, c],
                             drows[3 * P:3 * (P + V), c].rearrange("(g k) c -> k g c", g=2)).then_inc(rb_ready[g], 16)

            sp.wait_ge(part3_ready, 2)
            write_tables(0)
            read_tables(0)
            sp.wait_ge(part3_ready, 4)
            write_tables(1)
            sp.wait_ge(part3_ready, 5)
            write_tables(2)
            read_tables(1)
            sp.wait_ge(part3_ready, 7)
            write_tables(3)
            read_tables(2)
            read_tables(3)
            sp.wait_ge(h0_again, 5)
            sp.dma_start(wup, A["w_up"].rearrange("g h f -> h g f")).then_inc(experts_loaded, 16)
            for k in range(FT):
                n = min(P, FF - k * P)
                sp.dma_start(wdn[0:n, :, k, :], A["w_down"][:, k * P:k * P + n, :].rearrange("e f h -> f e h"))\
                  .then_inc(experts_loaded, 16)
            sp.dma_start(wdn[FL:FL + 1, :, FT - 1, :], A["b_down"].rearrange("(a e) h -> a e h", a=1))\
              .then_inc(experts_loaded, 16)
            sp.wait_ge(probs_ready, 1)
            rows = table.rearrange("(b r) c -> b r c", b=B)
            for col, src in ((slice(0, D), xn), (slice(D, TW), pr)):
                sp.dma_start(rows[:, 0:P, col].rearrange("b r c -> r b c"), src[:, 0:B, :]).then_inc(table_written, 16)
                for g in range(2):
                    sp.dma_start(rows[8 * g:8 * g + 8, P:P + V, col], src[:, B + g, :]).then_inc(table_written, 16)
            for b in range(B):
                sp.wait_ge(token_rows_copied, b + 1)
                sp.dma_start(out[b * L:(b + 1) * L, :].rearrange("(w q) c -> q w c", q=P), hout[:, b % 5])\
                  .then_inc(token_rows_written[b % 5], 16)

        @block.gpsimd
        def _(pool):
            nc.gpsimd.memset(wrt[:, E:P], 0.0).then_inc(wrt_zero, 1)
            for a in (s1, absent, negm, wsh):
                nc.gpsimd.memset(a, 0.0).then_inc(padding_zero, 1)
            nc.gpsimd.memset(ohl[:, :, 0:LAST0 - 3 * P], 0.0).then_inc(padding_zero, 1)
            pool.wait_ge(keys_ready, 1)
            nc.gpsimd.dma_start(dkey, xkey).then_inc(keys_in_dram, 16)
            pool.wait_ge(keys_in_dram, 16)
            for g in range(2):
                b8 = slice(8 * g, 8 * g + 8)
                nc.gpsimd.dma_start(keyb[:, b8], dkey[b8].rearrange("(a b) t -> a b t", a=1).broadcast_to([P, 8, L]))\
                    .then_inc(keys_spread[g], 16)
            for b in range(B):
                pool.wait_ge(keys_spread[b // 8], 16)
                nc.gpsimd.tensor_scalar(ohl[:, b, LAST0 - 3 * P:P], keyb[:, b, LAST0:L], cfv("lastid"),
                                        cfv("lastb")[:, b:b + 1], ALU.is_equal, ALU.mult).then_inc(last_onehots, 1)
            for r in range(ROUNDS):
                for j in range(3):
                    nc.gpsimd.memset(steps3[:, r, j:j + 1], (j + 1) << (2 * r)).then_inc(search_consts, 1)
            nc.gpsimd.memset(base, 0).then_inc(search_consts, 1)
            nc.gpsimd.memset(onesf, 1.0).then_inc(search_consts, 1)
            pool.wait_ge(shift_ready, 2)
            for n in range(NB + 1):
                if n < NB:
                    i, b = (B + n, n) if n < 2 else (n - 2, n - 2)
                    if n >= 4:
                        pool.wait_ge(context_ready, n - 3)
                    nc.gpsimd.tensor_copy(uu[:, 2 + n if n < 2 else n % 2, :, D],
                                          cnt[:, i:i + 1].broadcast_to([P, H])).then_inc(counts_placed, 1)
                    if n >= 2:
                        pool.wait_ge(k_exp_ready, b // 8 + 1)
                        nc.gpsimd.tensor_scalar(ekm[:, b % 2, :], ekl[:, b // 8, :],
                                                cfv("lastsel")[:, b % 8:b % 8 + 1], None, ALU.mult)\
                            .then_inc(k_last_ready, 1)
                i = n - 1
                if i >= 0:
                    pool.wait_ge(q_exp_ready, i + 1)
                    pool.wait_ge(q_sum_ready, i + 1)
                    if i >= 2:
                        pool.wait_ge(qt_turned, i - 1)
                    nc.gpsimd.tensor_tensor(qn[:, i % 2, :].rearrange("p (h d) -> p h d", h=H),
                                            eq_[:, i % 2, :].rearrange("p (h d) -> p h d", h=H),
                                            rq[:, i % 2, :].unsqueeze(2).broadcast_to([P, H, DH]),
                                            ALU.mult).then_inc(q_probs_ready, 1)
            pool.wait_ge(context_ready, B)
            nc.gpsimd.tensor_copy(px, cnt.unsqueeze(2).broadcast_to([P, NB, E])).then_inc(weights_spread, 1)
            pool.wait_ge(h1_part1_ready, 1)
            nc.gpsimd.tensor_tensor(h1r, h1, h1p[:, 0], ALU.subtract).then_inc(h1_rest_ready, 1)
            pool.wait_ge(h1_part2_ready, 1)
            nc.gpsimd.tensor_tensor(h1p[:, 2], h1r, h1p[:, 1], ALU.subtract).then_inc(h1_rest_ready, 1)
            pool.wait_ge(token_rows_copied, B)
            nc.gpsimd.memset(actT[64:P, :, FT - 1, :], 1.0).then_inc(ones_ready, 1)
            pool.wait_ge(table_written, 6 * 16)
            for n in range(-3, E):
                e = n + 3
                if e < E:
                    pool.wait_ge(slots_listed, e // 2 + 1)
                    if e >= 4:
                        pool.wait_ge(rows_turned, e - 3)
                        pool.wait_ge(eo_ready, e - 3)
                    for h in range(2):
                        pool.indirect_dma_start(
                            xg[:, e % 4, h, :], None, table,
                            bass.IndirectOffsetOnAxis(ap=rowi[:, 2 * e + h:2 * e + h + 1], axis=0))\
                            .then_inc(rows_gathered[e % 4], 16)
                if n >= 0:
                    if n == 0:
                        for b in range(5):
                            pool.wait_ge(token_rows_written[b], 16 * len(range(b, B, 5)))
                    pool.wait_ge(eo_ready, n + 1)
                    if n >= 1:
                        pool.wait_ge(rows_scattered[(n - 1) % 2], 32 * ((n - 1) // 2 + 1))
                    for h in range(2):
                        pool.indirect_dma_start(
                            out, bass.IndirectOffsetOnAxis(ap=toki[:, 2 * n + h:2 * n + h + 1], axis=0),
                            eo[:, n % 4, h, :], None, compute_op=ALU.add).then_inc(rows_scattered[n % 2], 16)
            for k in range(2):
                pool.wait_ge(rows_scattered[k], 32 * (E // 2))

        @block.tensor
        def _(pe):
            mm, tp = nc.tensor.matmul, nc.tensor.transpose
            bank16 = lambda k: ps[:, k, :].bitcast(BF16)
            pe.wait_ge(loaded_dft, 16)
            dftab, dftc = cbv("dftab"), cbv("dftc")
            ohp = ohn.rearrange("p (v o) k -> p o v k", o=2)
            for c, (v0, nv) in enumerate(VP):
                pe.wait_ge(ids_onehot, c + 1)
                for r in range(2):
                    w = slice(r * DH, (r + 1) * DH)
                    for o in range(2):
                        d = ps[o * DH:(o + 1) * DH, 2 * c + r, 0:nv * B * NT].rearrange("p (v k) -> p v k", v=nv)
                        mm(d, dftab[:, w], ohp[:, o, v0:v0 + nv, :], start=True, stop=False)
                        last = mm(d, dftc[:, w], ohp[:, o, v0:v0 + nv, :], start=False, stop=True)
                    last.then_inc(spectra_ready, 1)
            pe.wait_ge(loaded_w_vo, 32)
            for h in range(H):
                r = slice((h % 2) * DH, (h % 2 + 1) * DH)
                last = mm(ps[:, 6 + h % 2, (h // 2) * D:(h // 2 + 1) * D], wv[r, h // 2, :], wo[r, h // 2, :],
                          start=True, stop=True)
            last.then_inc(w_vo_ready, 1)
            pe.wait_ge(mag_ready, 1)
            pe.wait_ge(loaded_proj, 5 * 16)
            for bank, lo_, n in ((4, 0, P), (5, P, V)):
                for v in range(V // 2):
                    last = mm(ps[0:n, bank, 0:D], mag[:, v, lo_:lo_ + n], projw[:, v, :],
                              start=v == 0, stop=v == V // 2 - 1)
                last.then_inc(enc_ready, 1)
            pe.wait_ge(factors_centred, 2)
            tp(ps[:, 6, 0:P], fpc, ident)
            tp(ps[:, 6, P:P + 2 * V], fqc, ident[0:2 * V, 0:2 * V]).then_inc(factors_turned, 1)
            pe.wait_ge(factors_t_ready, 1)
            pe.wait_ge(w_vo_centred, 1)
            mm(ps[:, 0, :], ft[:, 0:P], wall[:, 0:HD], start=True, stop=True).then_inc(factor_products, 1)
            for c in range(4):
                last = mm(ps[32 * c:32 * c + 2 * V, 4, :], ft[:, P:P + 2 * V], wall[:, c * HD:(c + 1) * HD],
                          start=True, stop=True)
            last.then_inc(factor_products, 1)
            for c in range(1, 4):
                mm(ps[:, c, :], ft[:, 0:P], wall[:, c * HD:(c + 1) * HD], start=True, stop=True)\
                    .then_inc(factor_products, 1)

            def expand(o, i, lo_, hi_, stop=True):
                return mm(o, sel, rb[:, i, lo_:hi_], start=True, stop=stop)

            pe.wait_ge(loaded_tables, 48)
            pe.wait_ge(rb_ready[0], 3 * 16)
            pe.wait_ge(part3_ready, 7)
            for k, (i0, n) in enumerate(TILES4):
                for i in range(n):
                    last = expand(ps[:, k, i * P:(i + 1) * P], i0 + i, HC, HC + D)
                last.then_inc(h0_ready, 1)
            pe.wait_ge(inv_s_ready, 2)
            tp(bank16(5)[0:KR, 0:P], absent, identb).then_inc(scales_turned, 1)
            pe.wait_ge(scales_t_ready, 1)
            for k, (i0, n) in enumerate(TILES4):
                for i in range(n):
                    last = mm(ps[0:KR + 1, k, i * P:(i + 1) * P], pick[:, i0 + i, :], sT, start=True, stop=True)
                last.then_inc(scales_spread, 1)
            pe.wait_ge(rb_ready[1], 3 * 16)
            for i in range(NB):
                if i % 4 == 0:
                    pe.wait_ge(scaled_sel_ready, i // 4 + 1)
                if i >= 3:
                    pe.wait_ge(kt_used, i - 2)
                for j in range(4):
                    last = mm(ps[:, 5 + i % 3, j * P:(j + 1) * P], rb1[:, i, KC + j * P:KC + (j + 1) * P],
                              sels[:, i, :], start=True, stop=True)
                last.then_inc(kt_ready, 1)
            pe.wait_ge(neg_max_ready, 2)
            for j in range(4):
                last = tp(bank16(0)[0:KR, j * P:(j + 1) * P], negm[:, j], identb)
            last.then_inc(shift_turned, 1)
            for i in range(NB):
                last = tp(bank16(1 + i // 8)[0:KR, (i % 8) * P:(i % 8 + 1) * P], wsh[:, i], identb)
            last.then_inc(shift_turned, 1)

            ORDER = [B, B + 1] + list(range(B))

            def context(b):
                pe.wait_ge(k_exp_ready, b + 3)
                pe.wait_ge(u_scaled, b + 3)
                pe.wait_ge(counts_placed, b + 3)
                pe.wait_ge(k_last_ready, b + 1)
                if b >= 1:
                    pe.wait_ge(context_scaled, b)
                for h in range(H):
                    o, j = h % 2, h // 2
                    d = ps[o * DH:(o + 1) * DH, 5 + j // 2, (j % 2) * (D + 1):(j % 2 + 1) * (D + 1)]
                    c = slice(h * DH, (h + 1) * DH)
                    mm(d, ek[:, b % 2, c], uu[:, b % 2, h, :], start=True, stop=False)
                    last = mm(d, ekm[:, b % 2, c], uu[:, 2 + b // 8, h, :], start=False, stop=True)
                last.then_inc(context_ready, 1)

            def rows_out(b):
                m = (b % 8) // 2
                q32 = slice(32 * m, 32 * m + 32)
                pe.wait_ge(qt_ready, b + 3)
                pe.wait_ge(context_scaled, b + 1)
                if b >= 1:
                    pe.wait_ge(rows_taken, b)
                for j in range(4):
                    mm(ps[:, 7, 0:P], qt[:, b % 4, j, :], mb[:, b % 2, j, :], start=j == 0, stop=j == 3)
                for j in range(4):
                    last = mm(ps[q32, 7, P:2 * P], qtl[:, b // 8, j, q32], mb[:, b % 2, j, :],
                              start=j == 0, stop=j == 3)
                last.then_inc(rows_ready, 1)

            pe.wait_ge(shift_ready, 2)
            pe.wait_ge(kt_used, NB)
            pe.wait_ge(rb_ready[2], 3 * 16)
            pe.wait_ge(rb_ready[3], 3 * 16)
            for n in range(NB + 1):
                if n < NB:
                    i = ORDER[n]
                    if n >= 1:
                        pe.wait_ge(q_shifted, n)
                    expand(ps[:, 0, :], i, QC, QC + HD).then_inc(q_ready, 1)
                    if n >= 1:
                        pe.wait_ge(k_exp_ready, n)
                    expand(ps[:, 2, :], i, KC, KC + HD, stop=False)
                    mm(ps[:, 2, :], lsh[:, i, :], nm[:, :], start=False, stop=True).then_inc(k_ready, 1)
                    if n >= 1:
                        pe.wait_ge(u_scaled, n)
                    for c in range(2):
                        last = expand(ps[:, 3 + c, :], i, UC + c * HD, UC + (c + 1) * HD)
                    last.then_inc(u_ready, 1)
                if 0 <= n - 3 < B:
                    context(n - 3)
                if 0 <= n - 4 < B:
                    rows_out(n - 4)
                if 0 <= n - 1 < NB:
                    pe.wait_ge(q_probs_ready, n)
                    if n >= 2:
                        pe.wait_ge(qt_ready, n - 1)
                    for j in range(4):
                        last = tp(ps[:, 1, j * P:(j + 1) * P], qn[:, (n - 1) % 2, j * P:(j + 1) * P], ident)
                    last.then_inc(qt_turned, 1)
            pe.wait_ge(qt_ready, NB)
            pe.wait_ge(q_exp_ready, NB)
            pe.wait_ge(k_exp_ready, NB)
            pe.wait_ge(u_scaled, NB)
            for k, (i0, n) in enumerate(TILES4):
                for i in range(n):
                    last = expand(ps[:, k, i * P:(i + 1) * P], i0 + i, HC, HC + D)
                last.then_inc(h0_again, 1)
                if k == 1:
                    rows_out(B - 1)

            def turn(a, banks):
                for k in range(4):
                    tp(ps[:, banks[0], k * P:(k + 1) * P], a[:, 4 * k:4 * k + 4, :].rearrange("p i e -> p (i e)"),
                       ident)
                for o, r in enumerate((slice(0, DH), slice(DH, P))):
                    last = tp(ps[0:DH, banks[1 + o], 0:DH], a[r, B:NB, :].rearrange("p i e -> p (i e)"), ident[r, r])
                last.then_inc(pairs_turned, 1)

            pe.wait_ge(weights_spread, 1)
            pe.wait_ge(context_scaled, B)
            pe.wait_ge(rows_taken, B)
            turn(px, (7, 5, 6))
            pe.wait_ge(loaded_router, 6 * 16)
            for k in range(6):
                if k < 5:
                    i0, n = TILES4[k]
                    pe.wait_ge(xn_ready, i0 + n)
                    if k >= 2:
                        pe.wait_ge(xnt_ready, k - 1)
                    if k == 0:
                        pe.wait_ge(pairs_ready, 1)
                    for i in range(n):
                        last = tp(ps[:, 5 + k % 2, i * P:(i + 1) * P], xn[:, i0 + i, :], ident)
                    last.then_inc(xn_turned, 1)
                if k >= 1:
                    i0, n = TILES4[k - 1]
                    pe.wait_ge(xnt_ready, k)
                    for i in range(n):
                        mm(ps[:, k - 1, i * P:(i + 1) * P], xnT[:, (i0 + i) * P:(i0 + i + 1) * P], wrt[:, :],
                           start=True, stop=True).then_inc(logits_ready, 1)
            pe.wait_ge(probs_ready, 1)
            turn(pr, (0, 1, 4))

            def token_rows(b):
                if b == 0:
                    pe.wait_ge(h1_rest_ready, 2)
                    pe.wait_ge(h1_part2_ready, 1)
                if b >= 2:
                    pe.wait_ge(token_rows_copied, b - 1)
                for w in range(4):
                    o = ps[:, 6 + b % 2, w * P:(w + 1) * P]
                    for q in range(3):
                        last = mm(o, oh[:, b, w * P:(w + 1) * P], h1p[:, q, b, :], start=q == 0,
                                  stop=q == 2 and w < 3)
                    if w == 3:
                        for q in range(3):
                            last = mm(o, ohl[:, b, :], h1p[:, q, B + b // 8, :], start=False, stop=q == 2)
                last.then_inc(token_rows_ready, 1)

            rows_done = 0
            for k in range(ROUNDS + 1):
                w = 3 if k < ROUNDS else 1
                pe.wait_ge(partial_counts, k + 1)
                mm(ps[:, 5, 0:P // w * w], cfv("sameexp"), part[:, 0:w].unsqueeze(1).broadcast_to([P, P // w, w]),
                   start=True, stop=True).then_inc(total_counts, 1)
                if k >= 2:
                    for b in range(rows_done, min(B, rows_done + (2 if k in (3, 6, 9) else 1))):
                        token_rows(b)
                        rows_done = b + 1
            pe.wait_ge(thresholds_diag, 1)
            mm(ps[:, 5, 64:64 + 2 * E], onesf, dtn, start=True, stop=True).then_inc(thresholds_spread, 1)
            pe.wait_ge(row_marks, 2)
            pe.wait_ge(token_rows_copied, B)
            for t in range(NTT):
                b, w = t // 4, t % 4
                o = ps[:, t // 8, (t % 8) * 2 * E:(t % 8 + 1) * 2 * E]
                last = mm(o, oh[:, b, w * P:(w + 1) * P], ge[:, b, :], start=True, stop=w < 3)
                if w == 3:
                    last = mm(o, ohl[:, b, :], ge[:, B + b // 8, :], start=False, stop=True)
                if t % 8 == 7:
                    last.then_inc(token_marks, 1)
            pe.wait_ge(eq_summed, 1)
            pe.wait_ge(gt_ready, 4)
            for k in range(4):
                mm(ps[:, k, :], cbv("notbefore"), eqT[:, k * 512:(k + 1) * 512], start=True, stop=False)
                mm(ps[:, k, :], cbv("onesb"), eqS[:, k * 512:(k + 1) * 512], start=False, stop=True)\
                    .then_inc(rank_ready, 1)
            pe.wait_ge(token_diffs, 1)
            mm(ps[:, 4, 2 * E:2 * E + NTT + 2], cbv("diff"), g0, start=True, stop=True)

            def blocks(k):
                pe.wait_ge(places_ready, k + 1)
                if k >= 1:
                    pe.wait_ge(blocks_copied, 2 * k + 1)
                e8 = slice(8 * k, 8 * k + 8)
                mm(ps[:, 4, e8], cbv("before"), cq[:, e8], start=True, stop=True)
                mm(ps[:, 4, E + 8 * k:E + 8 * k + 8], cbv("shift"), cq[:, e8], start=True, stop=True)\
                    .then_inc(blocks_ready, 1)
                mm(ps[:, k, :], cbv("diff"), pin[:, k * 512:(k + 1) * 512], start=True, stop=True)\
                    .then_inc(place_diffs, 1)

            def slots(gr):
                if gr >= 1:
                    pe.wait_ge(slots_listed, gr)
                pe.wait_ge(steps_ready, 2 * gr + 2)
                pe.wait_ge(pd_ready, gr // 4 + 1)
                for e in (2 * gr, 2 * gr + 1):
                    for h in range(2):
                        lhs = step[:, e, h * P:(h + 1) * P]
                        c = h * (2 * NTT + 3)
                        mm(ps[:, 6 + e % 2, c:c + NTT + 1], lhs, pd[:, e, 0:NTT + 1], start=True, stop=True)
                        last = mm(ps[:, 6 + e % 2, c + NTT + 1:c + 2 * NTT + 3], lhs, gd, start=True, stop=True)
                last.then_inc(slots_ready, 1)

            def gathered(e):
                pe.wait_ge(rows_gathered[e % 4], 32 * (e // 4 + 1))
                if e >= 2:
                    pe.wait_ge(xgt_ready, e - 1)
                for h in range(2):
                    last = tp(ps[:, 5 * (e % 2), h * P:(h + 1) * P], xg[:, e % 4, h, 0:D], ident)
                last.then_inc(rows_turned, 1)

            def up(e):
                pe.wait_ge(xgt_ready, e + 1)
                for k in range(FT):
                    n = min(P, FF - k * P)
                    if e >= 1:
                        pe.wait_ge(hidden_ready, FT * (e - 1) + k + 1)
                    mm(ps[0:n, 1 + k, 0:CAP], wup[:, e // GS, k * P:k * P + n],
                       xgT[:, e % 2, :], start=True, stop=True).then_inc(up_ready, 1)

            def down(e):
                pe.wait_ge(hidden_ready, FT * (e + 1))
                if e >= 1:
                    pe.wait_ge(eo_ready, e)
                for h in range(2):
                    for k in range(FT):
                        n = P if k < FT - 1 else FL + 1
                        last = mm(ps[:, 4, h * P:(h + 1) * P],
                                  actT[0:n, e % 2, k, h * P:(h + 1) * P], wdn[0:n, e, k, :],
                                  start=k == 0, stop=k == FT - 1)
                last.then_inc(down_ready, 1)

            blocks(0)
            slots(0)
            for k in range(1, 4):
                blocks(k)
            slots(1)
            pe.wait_ge(blocks_copied, 9)
            pe.wait_ge(pd_ready, 4)
            pe.wait_ge(experts_loaded, 5 * 16)
            pe.wait_ge(ones_ready, 1)
            gathered(0)
            up(0)
            gathered(1)
            down(0)
            for e in range(E):
                if e + 1 < E:
                    up(e + 1)
                if e >= 1:
                    down(e)
                gr = 2 if e == 0 else e // 2 + 3
                if (e == 0 or e % 2 == 1) and gr < E // 2:
                    slots(gr)
                if e + 2 < E:
                    gathered(e + 2)


        @block.scalar
        def _(act):
            A_ = nc.scalar.activation
            n3 = B * NT
            act.wait_ge(wrt_zero, 1)
            A_(dum, wrt[:, E:E + 1], ACT.Sqrt)
            for c, (v0, nv) in enumerate(VP):
                for r in range(2):
                    act.wait_ge(spectra_ready, 2 * c + r + 1)
                    A_(sq[:, r, v0 * n3:(v0 + nv) * n3], ps[:, 2 * c + r, 0:nv * n3], ACT.Square)\
                        .then_inc(squares_ready, 1)

            act.wait_ge(power_ready, 3)
            A_(mag.rearrange("p v k -> p (v k)"), sq[:, 0, :], ACT.Sqrt).then_inc(mag_ready, 1)
            act.wait_ge(factors_turned, 1)
            act.wait_ge(loaded_proj, 5 * 16)
            A_(ft, ps[:, 6, 0:P + 2 * V], ACT.Copy, scale=gcol[:, 0:1]).then_inc(factors_t_ready, 1)
            for n in range(9):
                if n < 7:
                    if ITEMS[n][2]:
                        act.wait_ge(factor_products, ITEMS[n][2])
                    A_(ITEMS[n][1][:, 0], ITEMS[n][0], ACT.Copy).then_inc(part1_ready, 1)
                if n >= 2:
                    act.wait_ge(rest_ready, n - 1)
                    A_(ITEMS[n - 2][1][:, 1], rest(n - 2), ACT.Copy).then_inc(part2_ready, 1)
            act.wait_ge(h0_var, 1)
            A_(invs, lnv, ACT.Sqrt).then_inc(s_ready, 1)
            act.wait_ge(scales_turned, 1)
            A_(sT, ps[:, 5, :].bitcast(BF16)[0:KR, 0:P], ACT.Copy).then_inc(scales_t_ready, 1)
            A_(dum2, wrt[:, E:E + 1], ACT.Exp)
            act.wait_ge(shift_turned, 1)
            A_(nm, ps[:, 0, :].bitcast(BF16)[0:KR, 0:HD], ACT.Copy).then_inc(shift_ready, 1)
            act.wait_ge(shift_turned, 2)
            for k, n in enumerate((8, 8, 2)):
                ins = A_(lsh[:, 8 * k:8 * k + n, :].rearrange("p i r -> p (i r)"),
                         ps[:, 1 + k, :].bitcast(BF16)[0:KR, 0:n * P], ACT.Copy)
            ins.then_inc(shift_ready, 1)
            for n in range(NB + 1):
                if n < NB:
                    i = B + n if n < 2 else n - 2
                    act.wait_ge(k_ready, n + 1)
                    if n >= 4:
                        act.wait_ge(context_ready, n - 3)
                    A_(ekl[:, n, :] if n < 2 else ek[:, n % 2, :], ps[:, 2, :], ACT.Exp,
                       scale=s1[:, i:i + 1]).then_inc(k_exp_ready, 1)
                    act.wait_ge(u_ready, n + 1)
                    A_(uu[:, 2 + n if n < 2 else n % 2, :, 0:D],
                       ps[:, 3:5, :].rearrange("p b (h c) -> p (b h) c", c=D), ACT.Copy,
                       scale=sc[:, i:i + 1]).then_inc(u_scaled, 1)
                    act.wait_ge(q_shifted, n + 1)
                    A_(eq_[:, n % 2, :], eq_[:, n % 2, :], ACT.Exp, scale=s1[:, i:i + 1]).then_inc(q_exp_ready, 1)
                if n >= 1:
                    act.wait_ge(qt_turned, n)
                    if n >= 7:
                        act.wait_ge(rows_ready, n - 6)
                    A_((qtl[:, n - 1] if n < 3 else qt[:, (n - 3) % 4]).rearrange("p j r -> p (j r)"),
                       ps[:, 1, :], ACT.Copy).then_inc(qt_ready, 1)
            def turned(a, banks, n):
                act.wait_ge(pairs_turned, n)
                A_(a[:, 0:HD], ps[:, banks[0], :], ACT.Copy)
                for o, r in enumerate((slice(0, DH), slice(DH, P))):
                    ins = A_(a[r, HD:BC], ps[0:DH, banks[1 + o], 0:DH], ACT.Copy)
                ins.then_inc(pairs_ready, 1)

            act.wait_ge(att_var, 1)
            A_(rstd, lnv, ACT.Sqrt).then_inc(att_std, 1)
            turned(wbis, (7, 5, 6), 1)
            for k in range(6):
                if k < 5:
                    i0, n = TILES4[k]
                    act.wait_ge(h1_var, k + 1)
                    A_(rstd2[:, i0:i0 + n], lnv2[:, i0:i0 + n], ACT.Sqrt).then_inc(h1_std, 1)
                    act.wait_ge(ln2_factors, k + 1)
                    for i in range(i0, i0 + n):
                        A_(xn[:, i, :], h1[:, i, :], ACT.Identity, bias=nbias[:, i:i + 1], scale=rstd2[:, i:i + 1])\
                            .then_inc(xn_ready, 1)
                if k >= 1:
                    i0, n = TILES4[k - 1]
                    act.wait_ge(xn_turned, k)
                    A_(xnT[:, i0 * P:(i0 + n) * P], ps[:, 5 + (k - 1) % 2, 0:n * P], ACT.Copy).then_inc(xnt_ready, 1)
            act.wait_ge(logits_shifted, 1)
            A_(pr[:, 0:NB, :], px[:, 0:NB, :], ACT.Exp).then_inc(logits_exp, 1)
            turned(pbis, (0, 1, 4), 2)
            A_(h1p[:, 0], h1, ACT.Copy).then_inc(h1_part1_ready, 1)
            act.wait_ge(h1_rest_ready, 1)
            A_(h1p[:, 1], h1r, ACT.Copy).then_inc(h1_part2_ready, 1)
            for b in range(B):
                act.wait_ge(token_rows_ready, b + 1)
                if b >= 5:
                    act.wait_ge(token_rows_written[b % 5], 16 * (b // 5))
                A_(hout[:, b % 5].rearrange("p w c -> p (w c)"), ps[:, 6 + b % 2, :], ACT.Copy)\
                    .then_inc(token_rows_copied, 1)
            act.wait_ge(thresholds_spread, 1)
            act.wait_ge(table_written, 6 * 16)
            for k in range(1, 8, 2):
                act.wait_ge(token_marks, k + 1)
                for c, o in ((0, eqT), (E, gtT)):
                    ins = A_(o.rearrange("p (e t) -> p t e", e=E)[:, 8 * k:8 * k + 8, :],
                             ps[:, k, :].rearrange("p (t c) -> p t c", t=8)[:, :, c:c + E], ACT.Copy)
                ins.then_inc(gt_ready, 1)
            A_(dum3, lnv2[:, 0:1], ACT.Silu)
            for k in range(4):
                act.wait_ge(place_diffs, k + 1)

                A_(pd[:, 8 * k:8 * k + 8, 0:NTT], ps[:, k, :].rearrange("p (e t) -> p e t", e=8), ACT.Copy)\
                    .then_inc(pd_ready, 1)


            for e in range(-1, E):
                if e + 1 < E:
                    n = e + 1
                    act.wait_ge(rows_turned, n + 1)
                    if n >= 2:
                        act.wait_ge(up_ready, FT * (n - 1))
                    A_(xgT[:, n % 2, :], ps[:, 5 * (n % 2), 0:CAP], ACT.Copy).then_inc(xgt_ready, 1)
                    if n >= 2:
                        act.wait_ge(down_ready, n - 1)
                    if n == 0:
                        act.wait_ge(ones_ready, 1)
                    for k in range(FT):
                        r = min(P, FF - k * P)
                        act.wait_ge(up_ready, FT * n + k + 1)
                        A_(actT[0:r, n % 2, k, :], ps[0:r, 1 + k, 0:CAP], ACT.Silu,
                           bias=bup[0:r, k, n // GS:n // GS + 1]).then_inc(hidden_ready, 1)

        @block.vector
        def _(dve):
            vec = nc.vector
            ndve = [0]

            def done(ins):
                ndve[0] += 1
                ins.then_inc(dve_step, 1)
                dve.wait_ge(dve_step, ndve[0])

            dve.wait_ge(loaded_frames, 32)
            for v0, nv in VP:
                ids = slice(2 * v0, 2 * (v0 + nv))
                vec.tensor_tensor(ohn[:, ids], xfrm[:, :].unsqueeze(1).broadcast_to([P, 2 * nv, B * NT]),
                                  cfv("ids")[:, ids].unsqueeze(2).broadcast_to([P, 2 * nv, B * NT]),
                                  ALU.is_equal).then_inc(ids_onehot, 1)
            dve.wait_ge(loaded_ids, 16)
            vec.tensor_tensor(xkey, xseq, cfv("frame16"), ALU.add).then_inc(keys_ready, 1)
            for c, (v0, nv) in enumerate(VP):
                dve.wait_ge(squares_ready, 2 * c + 2)
                at_, n = v0 * B * NT, nv * B * NT
                vec.scalar_tensor_tensor(out=sq[:, 0, at_:at_ + n], in0=sq[:, 0, at_:at_ + n], scalar=1e-34,
                                         in1=sq[:, 1, at_:at_ + n], op0=ALU.max, op1=ALU.add).then_inc(power_ready, 1)

            def onehots(b):
                vec.tensor_scalar(oh[:, b, :], keyb[:, b, :], cfv("pidx"), 0.0, ALU.is_equal, ALU.add,
                                  accum_out=cnt[:, b:b + 1]).then_inc(onehots_ready, 1)

            dve.wait_ge(w_vo_ready, 1)
            vo = ps[:, 6:8, :].rearrange("p o (j c) -> p o j c", j=4)
            oj = lambda a: a.rearrange("p (o j) -> p o j", o=2)
            done(vec.tensor_reduce(oj(wm[:, 0:H]), vo, AX.X, ALU.add))
            done(vec.tensor_scalar(wm[:, H:2 * H], wm[:, 0:H], -1.0 / D, None, ALU.mult))
            for o in range(2):
                ins = vec.tensor_tensor(wall[:, 2 * HD:].rearrange("p (j o c) -> p o j c", j=4, o=2)[:, o], vo[:, o],
                                        wm[:, H + 4 * o:H + 4 * o + 4].unsqueeze(2).broadcast_to([P, 4, D]), ALU.add)
            ins.then_inc(w_vo_centred, 1)
            dve.wait_ge(keys_spread[0], 16)
            dve.wait_ge(padding_zero, 5)
            for b in range(5):
                onehots(b)
            dve.wait_ge(enc_ready, 2)
            dve.wait_ge(loaded_proj, 5 * 16)
            vec.tensor_tensor(fp, ps[:, 4, 0:D], projb, ALU.add)
            done(vec.tensor_tensor(fq[0:V], ps[0:V, 5, 0:D], projb[0:V], ALU.add))
            vec.tensor_reduce(fm[:, 0:1], fp, AX.X, ALU.add)
            done(vec.tensor_reduce(fm[0:2 * V, 1:2], fq, AX.X, ALU.add))
            done(vec.tensor_scalar(fm[:, 2:3], fm[:, 0:1], -1.0 / D, None, ALU.mult))
            done(vec.tensor_scalar(fm[0:2 * V, 3:4], fm[0:2 * V, 1:2], -1.0 / D, None, ALU.mult))
            vec.tensor_scalar(fpc, fp, fm[:, 2:3], None, ALU.add).then_inc(factors_centred, 1)
            vec.tensor_scalar(fqc, fq, fm[0:2 * V, 3:4], None, ALU.add).then_inc(factors_centred, 1)
            for n in range(9):
                if n < 7:
                    dve.wait_ge(part1_ready, n + 1)
                    if n >= 4:
                        dve.wait_ge(part3_ready, n - 3)
                    vec.tensor_tensor(rest(n), ITEMS[n][0], ITEMS[n][1][:, 0], ALU.subtract).then_inc(rest_ready, 1)

                if n >= 2:
                    dve.wait_ge(part2_ready, n - 1)
                    vec.tensor_tensor(ITEMS[n - 2][1][:, 2], rest(n - 2), ITEMS[n - 2][1][:, 1],
                                      ALU.subtract).then_inc(part3_ready, 1)
                if n == 2:
                    for b in range(5, 8):
                        onehots(b)
                if n == 3:
                    dve.wait_ge(keys_spread[1], 16)
                    for b in range(8, 11):
                        onehots(b)
            for b in range(11, B):
                onehots(b)

            dve.wait_ge(onehots_ready, B)
            dve.wait_ge(last_onehots, B)
            for g in range(2):
                ins = vec.tensor_reduce(cnt[:, B + g:B + g + 1], ohl[:, 8 * g:8 * g + 8, LAST0 - 3 * P:P], AX.XY,
                                        ALU.add)
            done(ins)
            vec.tensor_scalar(absent[:, NB:2 * NB], cnt[:, 0:NB], 0.5, -1e30, ALU.is_lt, ALU.mult)\
                .then_inc(inv_s_ready, 1)

            def variances(rows, eps_of):
                for i in range(NB):
                    ins = vec.bn_stats(stats[:, i, :], rows(i))
                done(ins)
                for i in range(NB):
                    ins = vec.bn_aggr(mv[:, i, :], stats[:, i, :])
                done(ins)
                return vec.tensor_scalar(lnv, mv[:, :, 1], eps_of[0], eps_of[1], ALU.mult, ALU.add)

            dve.wait_ge(h0_ready, 5)
            h0ps = lambda i: ps[:, i // 4, (i % 4) * P:(i % 4 + 1) * P]
            variances(h0ps, (1.0 + EPS, EPS * EPS)).then_inc(h0_var, 1)
            dve.wait_ge(s_ready, 1)
            done(vec.reciprocal(s1[:, 0:NB], invs))
            vec.tensor_copy(absent[:, 0:NB], s1[:, 0:NB])
            vec.tensor_copy(ivp[:, 0, :], invs).then_inc(inv_s_ready, 1)
            done(vec.tensor_tensor(sc, s1[:, 0:NB], cnt[:, 0:NB], ALU.mult))
            done(vec.tensor_tensor(ivr[:, 0, :], invs, ivp[:, 0, :], ALU.subtract))
            done(vec.tensor_copy(ivp[:, 1, :], ivr[:, 0, :]))
            done(vec.tensor_tensor(ivp[:, 2, :], ivr[:, 0, :], ivp[:, 1, :], ALU.subtract))
            for q in range(3):
                ins = vec.tensor_tensor(wsh[:, :, q * B:(q + 1) * B], cbv("rowb").rearrange("p (i b) -> p i b", i=NB),
                                        ivp[:, q, :].unsqueeze(2).broadcast_to([P, NB, B]), ALU.mult)
            ins.then_inc(neg_max_ready, 1)

            for k, (i0, n) in enumerate(TILES4):
                dve.wait_ge(scales_spread, k + 1)
                vec.tensor_tensor(sels[:, i0:i0 + n, :], ps[0:KR + 1, k, 0:n * P].rearrange("p (i r) -> p i r", i=n),
                                  sel1.unsqueeze(1).broadcast_to([KR + 1, n, P]), ALU.mult)\
                                      .then_inc(scaled_sel_ready, 1)
            for i in range(NB):
                dve.wait_ge(kt_ready, i + 1)
                kt = ps[:, 5 + i % 3, :].rearrange("p (j r) -> p j r", j=4)
                if i < B:
                    ins = vec.tensor_reduce(mx[:, :, i:i + 1], kt, AX.X, ALU.max)
                else:
                    ins = vec.tensor_reduce(mxl[:, :, 8 * (i - B):8 * (i - B) + 8],
                                            kt.rearrange("p j (b v) -> p j b v", b=8), AX.X, ALU.max)
                ins.then_inc(kt_used, 1)
            dve.wait_ge(kt_used, NB)
            done(vec.tensor_tensor(mx, mx, mxl, ALU.max))
            for q in range(3):
                ins = vec.tensor_scalar(negm[:, :, q * B:(q + 1) * B], mx, -1.0, None, ALU.mult)
            ins.then_inc(neg_max_ready, 1)
            for n in range(NB + 4):
                if n < NB:
                    dve.wait_ge(q_ready, n + 1)
                    by_head = lambda a: a.rearrange("p (h d) -> p h d", h=H)
                    done(vec.tensor_reduce(qm[:, n % 2, :], by_head(ps[:, 0, :]), AX.X, ALU.max))
                    if n >= 2:
                        dve.wait_ge(q_probs_ready, n - 1)
                    vec.tensor_tensor(by_head(eq_[:, n % 2, :]), by_head(ps[:, 0, :]),
                                      qm[:, n % 2, :].unsqueeze(2).broadcast_to([P, H, DH]),
                                      ALU.subtract).then_inc(q_shifted, 1)
                i = n - 1
                if 0 <= i < NB:
                    dve.wait_ge(q_exp_ready, i + 1)
                    if i >= 2:
                        dve.wait_ge(q_probs_ready, i - 1)
                    done(vec.tensor_reduce(zq[:, i % 2, :], eq_[:, i % 2, :].rearrange("p (h d) -> p h d", h=H),
                                           AX.X, ALU.add))
                    vec.reciprocal(rq[:, i % 2, :], zq[:, i % 2, :]).then_inc(q_sum_ready, 1)
                b = n - 3
                if 0 <= b < B:
                    dve.wait_ge(context_ready, b + 1)
                    if b >= 2:
                        dve.wait_ge(rows_ready, b - 1)
                    z = ps[:, 5:7, 0:2 * (D + 1)].rearrange("p k (j c) -> p k j c", j=2)
                    jj = lambda a: a.rearrange("p (k j) -> p k j", k=2)
                    done(vec.reciprocal(jj(rz[:, b, :]), z[:, :, :, D]))
                    done(vec.tensor_scalar(rz[:, b, :], rz[:, b, :], DH ** -0.5, None, ALU.mult))
                    vec.tensor_tensor(mb[:, b % 2].rearrange("p (k j) c -> p k j c", k=2), z[:, :, :, 0:D],
                                      jj(rz[:, b, :]).unsqueeze(3).broadcast_to([P, 2, 2, D]), ALU.mult)\
                        .then_inc(context_scaled, 1)
                b = n - 4
                if 0 <= b < B:
                    g, o, m = b // 8, b % 2, (b % 8) // 2
                    q32 = slice(32 * m, 32 * m + 32)
                    if b >= 1:
                        dve.wait_ge(rows_taken, b)
                        vec.bn_aggr(mv[:, b - 1, :], stats[:, b - 1, :])
                    dve.wait_ge(rows_ready, b + 1)
                    if b == 0:
                        dve.wait_ge(loaded_router, 6 * 16)
                    vec.tensor_tensor(ao[:, b, :], ps[:, 7, 0:D], ogam[:, :], ALU.mult)
                    vec.bn_stats(stats[:, b, :], ps[:, 7, 0:D])
                    mine = cfv("parity")[q32, o:o + 1]
                    if o == 0:
                        vec.tensor_scalar(ao[q32, B + g, :], ps[q32, 7, P:2 * P], mine, None, ALU.mult)\
                            .then_inc(rows_taken, 1)
                    else:
                        vec.scalar_tensor_tensor(out=ao[q32, B + g, :], in0=ps[q32, 7, P:2 * P], scalar=mine,
                                                 in1=ao[q32, B + g, :], op0=ALU.mult, op1=ALU.add)\
                                                     .then_inc(rows_taken, 1)
            dve.wait_ge(rows_taken, B)
            for g in range(2):
                ins = vec.bn_stats(stats[:, B + g, :], ao[:, B + g, :])
            done(ins)
            vec.tensor_tensor(ao[:, B:NB, :], ao[:, B:NB, :], ogam[:, :].unsqueeze(1).broadcast_to([P, 2, D]),
                              ALU.mult)
            for i in range(B - 1, NB):
                ins = vec.bn_aggr(mv[:, i, :], stats[:, i, :])
            done(ins)
            vec.tensor_scalar(lnv, mv[:, :, 1], EPS, None, ALU.add).then_inc(att_var, 1)
            dve.wait_ge(att_std, 1)
            done(vec.reciprocal(rstd, rstd))
            for k in range(6):
                if k < 5:
                    i0, n = TILES4[k]
                    dve.wait_ge(h0_again, 5)
                    for i in range(i0, i0 + n):

                        ins = vec.scalar_tensor_tensor(out=h1[:, i, :], in0=ao[:, i, :], scalar=rstd[:, i:i + 1],
                                                       in1=h0ps(i), op0=ALU.mult, op1=ALU.add)
                    ins.then_inc(h1_ready, 1)
                if k >= 1:
                    j0, m = TILES4[k - 1]
                    dve.wait_ge(h1_std, k)
                    done(vec.reciprocal(rstd2[:, j0:j0 + m], rstd2[:, j0:j0 + m]))
                    vec.scalar_tensor_tensor(out=nbias[:, j0:j0 + m], in0=mv2[:, j0:j0 + m, 0], scalar=-1.0,
                                             in1=rstd2[:, j0:j0 + m], op0=ALU.mult, op1=ALU.mult)\
                                                 .then_inc(ln2_factors, 1)
                if k < 5:
                    dve.wait_ge(h1_ready, k + 1)
                    for i in range(i0, i0 + n):
                        ins = vec.bn_stats(stats2[:, i, :], h1[:, i, :])
                    done(ins)
                    for i in range(i0, i0 + n):
                        ins = vec.bn_aggr(mv2[:, i, :], stats2[:, i, :])
                    done(ins)
                    vec.tensor_scalar(lnv2[:, i0:i0 + n], mv2[:, i0:i0 + n, 1], EPS, None, ALU.add)\
                        .then_inc(h1_var, 1)
            dve.wait_ge(loaded_tokens, 16)
            done(vec.tensor_tensor(vtok, xtok[:, :], cfv("tau16"), ALU.add))
            vec.tensor_tensor(g0[:, 0:NTT - 1], vtok[:, 1:NTT], vtok[:, 0:NTT - 1], ALU.subtract)
            vec.memset(g0[:, NTT - 1:NTT], 0.0)
            vec.tensor_copy(g0[:, NTT:NTT + 1], vtok[:, 0:1])
            vec.tensor_copy(g0[:, NTT + 1:NTT + 2], cfv("pidx")).then_inc(token_diffs, 1)
            dve.wait_ge(logits_ready, NB)
            vec.tensor_tensor(px[:, 0:B, :].rearrange("p (k i) e -> p k i e", k=4),
                              ps[:, 0:4, :].rearrange("p k (i c) -> p k i c", i=4)[:, :, :, 0:E],
                              brt[:, :].unsqueeze(1).unsqueeze(1).broadcast_to([P, 4, 4, E]), ALU.add)
            done(vec.tensor_tensor(px[:, B:NB, :], ps[:, 4, 0:2 * P].rearrange("p (i c) -> p i c", i=2)[:, :, 0:E],
                                   brt[:, :].unsqueeze(1).broadcast_to([P, 2, E]), ALU.add))
            done(vec.tensor_reduce(pmx, px[:, 0:NB, :], AX.X, ALU.max))
            vec.tensor_tensor(px[:, 0:NB, :], px[:, 0:NB, :], pmx.unsqueeze(2).broadcast_to([P, NB, E]),
                              ALU.subtract).then_inc(logits_shifted, 1)
            dve.wait_ge(logits_exp, 1)
            done(vec.tensor_reduce(psm, pr[:, 0:NB, :], AX.X, ALU.add))
            done(vec.reciprocal(psm, psm))
            dve.wait_ge(search_consts, 3 * ROUNDS + 2)
            vec.tensor_tensor(pr[:, 0:NB, :], pr[:, 0:NB, :], psm.unsqueeze(2).broadcast_to([P, NB, E]),
                              ALU.mult).then_inc(probs_ready, 1)
            dve.wait_ge(pairs_ready, 2)
            def count(op, threshold, j):
                return vec.scalar_tensor_tensor(out=junk[j], in0
=pbis, scalar=threshold, in1=wbis, op0=op, op1=ALU.mult,
                                                accum_out=part[:, j:j + 1])

            for k in range(ROUNDS):
                r = ROUNDS - 1 - k
                at3 = steps3[:, r] if k == 0 else cand
                for j in range(3):
                    ins = count(ALU.is_ge, at3[:, j:j + 1].bitcast(F32), j)
                ins.then_inc(partial_counts, 1)
                dve.wait_ge(total_counts, k + 1)
                done(vec.scalar_tensor_tensor(out=passed, in0=ps[:, 5, 0:3], scalar=CAP - 0.5,
                                              in1=steps3[:, r, 0:1].broadcast_to([P, 3]), op0=ALU.is_ge,
                                              op1=ALU.mult, accum_out=digit))
                done(vec.tensor_copy(delta, digit))
                if r > 0:
                    done(vec.scalar_tensor_tensor(out=cand, in0=base, scalar=delta, in1=steps3[:, r - 1],
                                                  op0=ALU.bitwise_xor, op1=ALU.bitwise_xor))
                done(vec.tensor_tensor(base, base, delta.broadcast_to([P, 3]), ALU.bitwise_xor))
            cf_ = base[:, 0:1].bitcast(F32)
            count(ALU.is_gt, cf_, 0).then_inc(partial_counts, 1)
            dve.wait_ge(total_counts, ROUNDS + 1)
            done(vec.tensor_scalar(need, ps[:, 5, 0:1], -1.0, float(CAP), ALU.mult, ALU.add))
            vec.tensor_scalar(dtn[:, 0:E], cfv("eyeexp")[0:E], cf_[0:E], None, ALU.mult)
            vec.tensor_scalar(dtn[:, E:2 * E], cfv("eyeexp")[0:E], need[0:E], None, ALU.mult)\
                .then_inc(thresholds_diag, 1)
            dve.wait_ge(thresholds_spread, 1)
            done(vec.tensor_copy(tn, ps[:, 5, 64:64 + 2 * E]))
            for q, op in ((0, ALU.is_equal), (1, ALU.is_gt)):
                vec.tensor_tensor(ge[:, :, q * E:(q + 1) * E], pr[:, 0:NB, :],
                                  tn[:, 0:E].unsqueeze(1).broadcast_to([P, NB, E]), op).then_inc(row_marks, 1)
            dve.wait_ge(table_written, 6 * 16)
            for k in range(0, 8, 2):
                dve.wait_ge(token_marks, k + 1)
                for c, o in ((0, eqT), (E, gtT)):
                    ins = vec.tensor_copy(o.rearrange("p (e t) -> p t e", e=E)[:, 8 * k:8 * k + 8, :],
                                          ps[:, k, :].rearrange("p (t c) -> p t c", t=8)[:, :, c:c + E])
                ins.then_inc(eq_ready, 1)
            dve.wait_ge(eq_ready, 4)
            dve.wait_ge(gt_ready, 4)
            vec.tensor_tensor_scan(eqS, cbv("carry"), eqT, 0.0, ALU.mult, ALU.add).then_inc(eq_summed, 1)
            dve.wait_ge(eq_summed, 1)

            def chosen(k):
                c = slice(k * 512, (k + 1) * 512)
                dve.wait_ge(rank_ready, k + 1)
                done(vec.tensor_tensor(pin[:, c].rearrange("p (e t) -> p e t", e=8),
                                       ps[:, k, :].rearrange("p (e t) -> p e t", e=8),
                                       tn[:, E + 8 * k:E + 8 * k + 8].unsqueeze(2).broadcast_to([P, 8, NTT]),
                                       ALU.is_lt))
                done(vec.tensor_tensor(eqT[:, c], pin[:, c], eqT[:, c], ALU.mult))
                done(vec.tensor_tensor(gtT[:, c], eqT[:, c], gtT[:, c], ALU.add))
                done(vec.tensor_tensor_scan(pin[:, c], cbv("carry")[:, c], gtT[:, c], 0.0, ALU.mult, ALU.add))
                vec.tensor_copy(cq[:, 8 * k:8 * k + 8], pin[:, c].rearrange("p (e t) -> p e t", e=8)[:, :, NTT - 1])\
                    .then_inc(places_ready, 1)

            def firsts(k):
                dve.wait_ge(blocks_ready, k + 1)
                e8 = slice(8 * k, 8 * k + 8)
                vec.tensor_copy(bx[:, e8], ps[:, 4, e8]).then_inc(blocks_copied, 1)
                if k == 0:
                    vec.tensor_copy(gd, ps[:, 4, 2 * E:2 * E + NTT + 2]).then_inc(blocks_copied, 1)
                vec.tensor_copy(pd[:, e8, NTT], ps[:, 4, E + 8 * k:E + 8 * k + 8]).then_inc(blocks_copied, 1)
                dve.wait_ge(blocks_copied, 2 * k + 3)

            def steps(e0, e1):
                for e in range(e0, e1):
                    vec.tensor_scalar(step[:, e, :], cbv("slots"), bx[:, e:e + 1], None, ALU.is_ge)\
                       .then_inc(steps_ready, 1)

            chosen(0)
            firsts(0)
            steps(0, 4)

            def listed(gr):
                v = ps[:, 6:8, 0:2 * (2 * NTT + 3)].rearrange("p b (h c) -> p b h c", h=2)
                as3 = lambda a: a.rearrange("p (b h) -> p b h", b=2)
                dve.wait_ge(slots_ready, gr + 1)
                done(vec.tensor_tensor(as3(sr), cfv("slot").unsqueeze(1).broadcast_to([P, 2, 2]), v[:, :, :, NTT],
                                       ALU.subtract))
                done(vec.tensor_tensor(lm, v[:, :, :, 0:NTT],
                                       as3(sr).unsqueeze(3).broadcast_to([P, 2, 2, NTT]), ALU.is_le))
                done(vec.tensor_tensor(lp, lm, v[:, :, :, NTT + 1:2 * NTT + 1], ALU.mult))
                done(vec.tensor_reduce(sv, lp.rearrange("p b h c -> p (b h) c"), AX.X, ALU.add))
                done(vec.tensor_tensor(as3(vi), as3(sv), v[:, :, :, 2 * NTT + 1], ALU.add))
                vec.tensor_scalar(offi, vi, 4, None, ALU.arith_shift_right)
                done(vec.tensor_scalar(idi, vi, V - 1, None, ALU.bitwise_and))
                done(vec.tensor_scalar(sv, offi, float(P), None, ALU.mult))
                done(vec.tensor_tensor(as3(sr), as3(sv), v[:, :, :, 2 * NTT + 2], ALU.add))
                vec.tensor_copy(toki[:, 4 * gr:4 * gr + 4], sr)
                done(vec.tensor_scalar(seg, sr, NT / L, 0.5 / L - 0.5 + 0.5 / L, ALU.mult, ALU.add))
                vec.scalar_tensor_tensor(out=rowi[:, 4 * gr:4 * gr + 4], in0=seg, scalar=float(V), in1=idi,
                                         op0=ALU.mult, op1=ALU.add).then_inc(slots_listed, 1)

            listed(0)
            chosen(1)
            for k in range(1, 4):
                if k < 3:
                    chosen(k + 1)
                firsts(k)
            listed(1)
            steps(4, 10)

            for e in range(E):
                dve.wait_ge(down_ready, e + 1)
                if e >= 4:
                    dve.wait_ge(rows_scattered[e % 2], 32 * (e // 2 - 1))
                for h in range(2):
                    c = h * P
                    ins = vec.tensor_scalar(eo[:, e % 4, h, :], ps[:, 4, c:c + P],
                                            xg[:, e % 4, h, D + e:D + e + 1], None, ALU.mult)
                ins.then_inc(eo_ready, 1)
                gr = 2 if e == 0 else e // 2 + 3
                if (e == 0 or e % 2 == 1) and gr < E // 2:
                    listed(gr)
                steps(min(E, e + 10), min(E, e + 11))



_OUT = "out_dram"


def kernel(**inputs):
    import concourse.bacc as bacc
    from concourse.bass_utils import run_bass_kernel_spmd

    c = np.ascontiguousarray
    x = np.asarray(inputs["x"])
    at = np.arange(NT * NFFT) - NFFT // 2
    at = np.where(at < 0, -at, at)
    at = np.where(at >= L, 2 * (L - 1) - at, at)
    frames = x[:, at].reshape(B, NT, NFFT)
    cols = np.concatenate([frames[:, :TM].reshape(B * TM, NFFT), frames[:, TM]], 0).T
    cf, cb = constants()
    w_qkv, w_out, b_up = (np.asarray(inputs[n]) for n in ("L0_attn_w_qkv", "L0_attn_w_out", "L0_ffn_b_up"))
    zeros = np.zeros((P, P), np.float32)
    k, i, m = np.arange(KR)[:, None, None], np.arange(NB)[None, :, None], np.arange(KR + 1)[None, None, :]
    pick = np.where(m < KR, k == i, k == NB + i).reshape(KR, NB * (KR + 1))
    proj_w = np.zeros((2, P // 2, V // 2, D), np.float32)
    proj_w[:, :NF, :, DE:] = np.asarray(inputs["L0_tok_proj_w"]).reshape(NF, V // 2, 2, DS).transpose(2, 0, 1, 3)
    arrays = {
        "x_frames": c(np.concatenate([cols, cols], 0)),
        "x_seq": c(x),
        "pick": pick.astype(mybir.dt.np(BF16)),
        "ones": np.ones((1, HD), mybir.dt.np(BF16)),
        "x_tokens": c(x.reshape(NTT, P).T),
        "const_f32": _pack(cf, np.float32),
        "const_bf16": _pack(cb, mybir.dt.np(BF16)),
        "emb": c(np.concatenate([np.asarray(inputs["L0_tok_emb_table"]), zeros[:V, :DS]], 1)),
        "proj_w": proj_w.reshape(P, V // 2, D),
        "proj_b": c(np.concatenate([zeros[0, :DE], np.asarray(inputs["L0_tok_proj_b"])])),
        "norm_gamma": c(np.asarray(inputs["L0_attn_norm_gamma"]).reshape(D, 1)),
        "w_kq_t": c(np.concatenate([w_qkv[HD:2 * HD], w_qkv[:HD]], 0).T),
        "w_v": c(w_qkv[2 * HD:]),
        "w_out_t": c(w_out.T),
        "out_gamma": c(inputs["L0_attn_out_gamma"]),
        "w_router": c(inputs["L0_ffn_W_router"]),
        "b_router": c(inputs["L0_ffn_b_router"]),
        "w_up": c(inputs["L0_ffn_W_up"]),
        "b_up_t": c(b_up.T),
        "w_down": c(inputs["L0_ffn_W_down"]),
        "b_down": c(inputs["L0_ffn_b_down"]),
    }
    nc = bacc.Bacc("TRN2", target_bir_lowering=False, num_devices=1)
    args = {n: nc.dram_tensor(f"in_{n}", a.shape, mybir.dt.from_np(a.dtype), kind="ExternalInput").ap()
            for n, a in arrays.items()}
    out = nc.dram_tensor(_OUT, (B * L, D), F32, kind="ExternalOutput").ap()
    program(nc, args, out)
    r = run_bass_kernel_spmd(nc, [{f"in_{n}": a for n, a in arrays.items()}], core_ids=[0])
    return r.results[0][_OUT].reshape(B, L, D)
```
